# Optimizing a Trainium2 kernel written in Bass

```python
import numpy as np
import jax
import jax.numpy as jnp

def _softmax(x, axis=-1):
    return jax.nn.softmax(x, axis=axis)

def _gelu(x):
    return jax.nn.gelu(x, approximate=True)

def _silu(x):
    return jax.nn.silu(x)

def _sigmoid(x):
    return jax.nn.sigmoid(x)

def _layernorm(x, axis=-1, eps=1e-05):
    m = jnp.mean(x, axis=axis, keepdims=True)
    v = jnp.var(x, axis=axis, keepdims=True)
    return (x - m) / jnp.sqrt(v + eps)

def _scatter_add(tgt, idx, src, axis=0):
    return tgt.at[idx].add(src)

def _segment_sum(src, seg, n):
    return jax.ops.segment_sum(src, seg, n)
kernel_name = 'mk_audio_tower_d2_tok_audfeat768_r4_24239d'

def setup_inputs(seed: int=0):
    np.random.seed(seed)
    _w = jnp.asarray

    def _rec_inputs():
        import jax
        import jax.numpy as jnp
        _rk = jax.random.key(seed)
        x = 7.22013e-05 + 1.00017 * jax.random.normal(jax.random.fold_in(_rk, 1), (4, 64, 750), jnp.float32)
        return x
    x = _rec_inputs()

    def _L0_tok_setup():
        import jax, jax.numpy as jnp
        import numpy as np
        from jax import lax
        B, C, N = (32, 64, 256)
        KS = (3, 5, 7)

        def _att_block(x, w, b):
            pool = jnp.stack([jnp.mean(x, axis=1), jnp.std(x, axis=1, ddof=1), jnp.max(x, axis=1), jnp.min(x, axis=1)], axis=1)
            conv = lax.conv_general_dilated(pool, w, (1,), 'SAME', dimension_numbers=('NCH', 'OIH', 'NCH'))
            conv = conv + b[None, :, None]
            wgt = jax.nn.relu(conv[:, 0, :])
            row = jnp.einsum('bl,bdl->bd', wgt, x)
            Bq, D, L = x.shape
            return jnp.broadcast_to(row[:, None, :], (Bq, L, D))

        def _triplet(x, wt, bt, wc, bc):
            t_out = _att_block(x, wt, bt)
            c_out = _att_block(jnp.swapaxes(x, 1, 2), wc, bc)
            return 0.5 * (t_out + jnp.swapaxes(c_out, 1, 2))
        key = jax.random.key(seed)
        keys = jax.random.split(key, 8)
        inp = {'x': jax.random.normal(keys[0], (B, C, N), dtype=jnp.float32)}
        i = 1
        for k in KS:
            for pre in ('t', 'c'):
                inp[f'w_{pre}{k}'] = jax.random.normal(keys[i], (1, 4, k), dtype=jnp.float32) * 0.1
                inp[f'b_{pre}{k}'] = jnp.zeros((1,), dtype=jnp.float32)
            i += 1
        return inp
    _L0_tok_all = _L0_tok_setup()
    _L0_tok_in = {k: v for k, v in _L0_tok_all.items() if k in ('w_t3', 'b_t3', 'w_c3', 'b_c3', 'w_t5', 'b_t5', 'w_c5', 'b_c5', 'w_t7', 'b_t7', 'w_c7', 'b_c7')}
    del _L0_tok_all

    def _L0_attn_setup():
        import math
        import jax, jax.numpy as jnp
        import numpy as np
        B, L, D_MODEL = (2, 512, 192)
        H = 12
        FEAT = 16
        HEAD_DIM = D_MODEL // H

        def taylor_exp(x):
            d = x.shape[-1]
            rd = math.sqrt(d)
            rrd = math.sqrt(rd)
            r2 = math.sqrt(2.0)
            x2 = (x[..., :, None] * x[..., None, :]).reshape(*x.shape[:-1], d * d) / r2
            ones = jnp.ones(x.shape[:-1] + (1,), dtype=x.dtype)
            return jnp.concatenate([ones, x / rrd, x2 / rd], axis=-1)
        key = jax.random.key(seed)
        k1, k2, k3, k4, k5 = jax.random.split(key, 5)
        s = 0.02
        return {'hidden_states': jax.random.normal(k1, (B, L, D_MODEL), jnp.float32), 'Wq': jax.random.normal(k2, (H * FEAT, D_MODEL), jnp.float32) * s, 'Wk': jax.random.normal(k3, (H * FEAT, D_MODEL), jnp.float32) * s, 'Wv': jax.random.normal(k4, (D_MODEL, D_MODEL), jnp.float32) * s, 'Wo': jax.random.normal(k5, (D_MODEL, D_MODEL), jnp.float32) * s}
    _L0_attn_all = _L0_attn_setup()
    _L0_attn_in = {k: v for k, v in _L0_attn_all.items() if k in ('Wq', 'Wk', 'Wv', 'Wo')}
    del _L0_attn_all

    def _L0_ffn_setup():
        import jax, jax.numpy as jnp
        import numpy as np
        D_MODEL = 192
        D_EXPERT = 384
        N_EXPERTS = 8
        TOP_K = 2
        EPS = 1e-06

        def _rms_norm(x, w):
            var = jnp.mean(jnp.square(x), axis=-1, keepdims=True)
            return x * jax.lax.rsqrt(var + EPS) * w
        key = jax.random.key(seed)
        ks = jax.random.split(key, 6)
        s_in = 1.0 / np.sqrt(D_MODEL)
        s_mid = 1.0 / np.sqrt(D_EXPERT)
        return {'x': jax.random.normal(ks[0], (2, 512, D_MODEL), dtype=jnp.float32), 'norm_w': jnp.ones((D_MODEL,), dtype=jnp.float32), 'router_w': jax.random.normal(ks[1], (N_EXPERTS, D_MODEL), dtype=jnp.float32) * s_in, 'gate_w': jax.random.normal(ks[2], (N_EXPERTS, D_EXPERT, D_MODEL), dtype=jnp.float32) * s_in, 'up_w': jax.random.normal(ks[3], (N_EXPERTS, D_EXPERT, D_MODEL), dtype=jnp.float32) * s_in, 'down_w': jax.random.normal(ks[4], (N_EXPERTS, D_MODEL, D_EXPERT), dtype=jnp.float32) * s_mid}
    _L0_ffn_all = _L0_ffn_setup()
    _L0_ffn_in = {k: v for k, v in _L0_ffn_all.items() if k in ('norm_w', 'router_w', 'gate_w', 'up_w', 'down_w')}
    del _L0_ffn_all

    def _L1_attn_setup():
        import jax, jax.numpy as jnp
        import numpy as np
        L = 14
        H = 12
        HD = 64

        def rel_pos_embed(N, table_v, table_h):
            n = N - 1
            s = int(n ** 0.5)
            r = jnp.arange(n)
            dv = r[None, :] // s - r[:, None] // s
            dh = r[None, :] % s - r[:, None] % s
            iv = jnp.clip(dv, -L, L) + L + 1
            ih = jnp.clip(dh, -L, L) + L + 1
            iv = jnp.pad(iv, ((1, 0), (1, 0)))
            ih = jnp.pad(ih, ((1, 0), (1, 0)))
            return table_v[iv] + table_h[ih]
        key = jax.random.key(seed)
        ks = jax.random.split(key, 11)
        B, N, E = (64, 197, 192)
        T = 2 * L + 2
        std = 0.02
        return {'x': jax.random.normal(ks[0], (B, N, E), jnp.float32), 'wq': jax.random.normal(ks[1], (E, H * HD), jnp.float32) * std, 'wk': jax.random.normal(ks[2], (E, H * HD), jnp.float32) * std, 'wv': jax.random.normal(ks[3], (E, H * HD), jnp.float32) * std, 'wproj': jax.random.normal(ks[4], (H * HD, E), jnp.float32) * std, 'bproj': jnp.zeros((E,), jnp.float32), 'rk_v': jax.random.normal(ks[5], (T, HD), jnp.float32) * std, 'rk_h': jax.random.normal(ks[6], (T, HD), jnp.float32) * std, 'rv_v': jax.random.normal(ks[7], (T, HD), jnp.float32) * std, 'rv_h': jax.random.normal(ks[8], (T, HD), jnp.float32) * std}
    _L1_attn_all = _L1_attn_setup()
    _L1_attn_in = {k: v for k, v in _L1_attn_all.items() if k in ('wq', 'wk', 'wv', 'wproj', 'bproj', 'rk_v', 'rk_h', 'rv_v', 'rv_h')}
    del _L1_attn_all

    def _L1_ffn_setup():
        import jax, jax.numpy as jnp
        import numpy as np
        B, S, D, F, E = (4, 512, 192, 768, 8)
        key = jax.random.key(seed)
        ks = jax.random.split(key, 5)
        return {'x': jax.random.normal(ks[0], (B, S, D), dtype=jnp.float32), 'Ws': jax.random.normal(ks[1], (D, E), dtype=jnp.float32) * 0.02, 'bs': jnp.zeros((E,), dtype=jnp.float32), 'W1': jax.random.normal(ks[2], (E, D, F), dtype=jnp.float32) * 0.02, 'b1': jnp.zeros((E, F), dtype=jnp.float32), 'W2': jax.random.normal(ks[3], (E, F, D), dtype=jnp.float32) * 0.02, 'b2': jnp.zeros((E, D), dtype=jnp.float32)}
    _L1_ffn_all = _L1_ffn_setup()
    _L1_ffn_in = {k: v for k, v in _L1_ffn_all.items() if k in ('Ws', 'bs', 'W1', 'b1', 'W2', 'b2')}
    del _L1_ffn_all
    return {'x': x, 'L0_tok_w_t3': _L0_tok_in['w_t3'], 'L0_tok_b_t3': _L0_tok_in['b_t3'], 'L0_tok_w_c3': _L0_tok_in['w_c3'], 'L0_tok_b_c3': _L0_tok_in['b_c3'], 'L0_tok_w_t5': _L0_tok_in['w_t5'], 'L0_tok_b_t5': _L0_tok_in['b_t5'], 'L0_tok_w_c5': _L0_tok_in['w_c5'], 'L0_tok_b_c5': _L0_tok_in['b_c5'], 'L0_tok_w_t7': _L0_tok_in['w_t7'], 'L0_tok_b_t7': _L0_tok_in['b_t7'], 'L0_tok_w_c7': _L0_tok_in['w_c7'], 'L0_tok_b_c7': _L0_tok_in['b_c7'], 'L0_attn_Wq': _L0_attn_in['Wq'], 'L0_attn_Wk': _L0_attn_in['Wk'], 'L0_attn_Wv': _L0_attn_in['Wv'], 'L0_attn_Wo': _L0_attn_in['Wo'], 'L0_ffn_norm_w': _L0_ffn_in['norm_w'], 'L0_ffn_router_w': _L0_ffn_in['router_w'], 'L0_ffn_gate_w': _L0_ffn_in['gate_w'], 'L0_ffn_up_w': _L0_ffn_in['up_w'], 'L0_ffn_down_w': _L0_ffn_in['down_w'], 'L1_attn_wq': _L1_attn_in['wq'], 'L1_attn_wk': _L1_attn_in['wk'], 'L1_attn_wv': _L1_attn_in['wv'], 'L1_attn_wproj': _L1_attn_in['wproj'], 'L1_attn_bproj': _L1_attn_in['bproj'], 'L1_attn_rk_v': _L1_attn_in['rk_v'], 'L1_attn_rk_h': _L1_attn_in['rk_h'], 'L1_attn_rv_v': _L1_attn_in['rv_v'], 'L1_attn_rv_h': _L1_attn_in['rv_h'], 'L1_ffn_Ws': _L1_ffn_in['Ws'], 'L1_ffn_bs': _L1_ffn_in['bs'], 'L1_ffn_W1': _L1_ffn_in['W1'], 'L1_ffn_b1': _L1_ffn_in['b1'], 'L1_ffn_W2': _L1_ffn_in['W2'], 'L1_ffn_b2': _L1_ffn_in['b2']}

def reference(x, L0_tok_w_t3, L0_tok_b_t3, L0_tok_w_c3, L0_tok_b_c3, L0_tok_w_t5, L0_tok_b_t5, L0_tok_w_c5, L0_tok_b_c5, L0_tok_w_t7, L0_tok_b_t7, L0_tok_w_c7, L0_tok_b_c7, L0_attn_Wq, L0_attn_Wk, L0_attn_Wv, L0_attn_Wo, L0_ffn_norm_w, L0_ffn_router_w, L0_ffn_gate_w, L0_ffn_up_w, L0_ffn_down_w, L1_attn_wq, L1_attn_wk, L1_attn_wv, L1_attn_wproj, L1_attn_bproj, L1_attn_rk_v, L1_attn_rk_h, L1_attn_rv_v, L1_attn_rv_h, L1_ffn_Ws, L1_ffn_bs, L1_ffn_W1, L1_ffn_b1, L1_ffn_W2, L1_ffn_b2):
    import jax
    import jax.numpy as jnp

    def _L0_tok_ref(x, w_t3, b_t3, w_c3, b_c3, w_t5, b_t5, w_c5, b_c5, w_t7, b_t7, w_c7, b_c7):
        import jax, jax.numpy as jnp
        import numpy as np
        from jax import lax
        B, C, N = (32, 64, 256)
        KS = (3, 5, 7)

        def _att_block(x, w, b):
            pool = jnp.stack([jnp.mean(x, axis=1), jnp.std(x, axis=1, ddof=1), jnp.max(x, axis=1), jnp.min(x, axis=1)], axis=1)
            conv = lax.conv_general_dilated(pool, w, (1,), 'SAME', dimension_numbers=('NCH', 'OIH', 'NCH'))
            conv = conv + b[None, :, None]
            wgt = jax.nn.relu(conv[:, 0, :])
            row = jnp.einsum('bl,bdl->bd', wgt, x)
            Bq, D, L = x.shape
            return jnp.broadcast_to(row[:, None, :], (Bq, L, D))

        def _triplet(x, wt, bt, wc, bc):
            t_out = _att_block(x, wt, bt)
            c_out = _att_block(jnp.swapaxes(x, 1, 2), wc, bc)
            return 0.5 * (t_out + jnp.swapaxes(c_out, 1, 2))
        x3 = _triplet(x, w_t3, b_t3, w_c3, b_c3)
        x5 = _triplet(x, w_t5, b_t5, w_c5, b_c5)
        x7 = _triplet(x, w_t7, b_t7, w_c7, b_c7)
        return jnp.concatenate([x3, x5, x7], axis=2)

    def _L0_attn_ref(hidden_states, Wq, Wk, Wv, Wo):
        import math
        import jax, jax.numpy as jnp
        import numpy as np
        B, L, D_MODEL = (2, 512, 192)
        H = 12
        FEAT = 16
        HEAD_DIM = D_MODEL // H

        def taylor_exp(x):
            d = x.shape[-1]
            rd = math.sqrt(d)
            rrd = math.sqrt(rd)
            r2 = math.sqrt(2.0)
            x2 = (x[..., :, None] * x[..., None, :]).reshape(*x.shape[:-1], d * d) / r2
            ones = jnp.ones(x.shape[:-1] + (1,), dtype=x.dtype)
            return jnp.concatenate([ones, x / rrd, x2 / rd], axis=-1)
        b, l, d = hidden_states.shape
        q = jnp.einsum('bld,fd->blf', hidden_states, Wq).reshape(b, l, H, FEAT).transpose(0, 2, 1, 3)
        k = jnp.einsum('bld,fd->blf', hidden_states, Wk).reshape(b, l, H, FEAT).transpose(0, 2, 1, 3)
        v = jnp.einsum('bld,fd->blf', hidden_states, Wv).reshape(b, l, H, HEAD_DIM).transpose(0, 2, 1, 3)
        q = taylor_exp(q)
        k = taylor_exp(k)
        k_state = jnp.sum(k, axis=2, keepdims=True) + jnp.cumsum(k, axis=2)
        z = 1.0 / jnp.sum(q * k_state, axis=-1)
        A = jnp.einsum('bhnd,bhmd->bhnm', q, k)
        causal = jnp.tril(jnp.ones((l, l), dtype=A.dtype))
        A_total = A * causal + A
        y = jnp.einsum('bhnm,bhme->bhne', A_total, v) * z[..., None]
        out = y.transpose(0, 2, 1, 3).reshape(b, l, H * HEAD_DIM)
        return jnp.einsum('blf,df->bld', out, Wo)

    def _L0_ffn_ref(x, norm_w, router_w, gate_w, up_w, down_w):
        import jax, jax.numpy as jnp
        import numpy as np
        D_MODEL = 192
        D_EXPERT = 384
        N_EXPERTS = 8
        TOP_K = 2
        EPS = 1e-06

        def _rms_norm(x, w):
            var = jnp.mean(jnp.square(x), axis=-1, keepdims=True)
            return x * jax.lax.rsqrt(var + EPS) * w
        residual = x
        B, S, D = x.shape
        xn = _rms_norm(x, norm_w)
        xf = xn.reshape(-1, D)
        logits = xf @ router_w.T
        probs = jax.nn.softmax(logits, axis=-1)
        _, top_idx = jax.lax.top_k(probs, TOP_K)
        sel = jax.nn.one_hot(top_idx, N_EXPERTS, dtype=probs.dtype).sum(axis=1)
        comb_w = probs * sel
        g = jnp.einsum('td,efd->tef', xf, gate_w)
        u = jnp.einsum('td,efd->tef', xf, up_w)
        h = jax.nn.silu(g) * u
        h = h * comb_w[:, :, None]
        y = jnp.einsum('tef,edf->td', h, down_w)
        return y.reshape(B, S, D) + residual

    def _L1_attn_ref(x, wq, wk, wv, wproj, bproj, rk_v, rk_h, rv_v, rv_h):
        import jax, jax.numpy as jnp
        import numpy as np
        L = 14
        H = 12
        HD = 64

        def rel_pos_embed(N, table_v, table_h):
            n = N - 1
            s = int(n ** 0.5)
            r = jnp.arange(n)
            dv = r[None, :] // s - r[:, None] // s
            dh = r[None, :] % s - r[:, None] % s
            iv = jnp.clip(dv, -L, L) + L + 1
            ih = jnp.clip(dh, -L, L) + L + 1
            iv = jnp.pad(iv, ((1, 0), (1, 0)))
            ih = jnp.pad(ih, ((1, 0), (1, 0)))
            return table_v[iv] + table_h[ih]
        B, N, E = x.shape
        scale = HD ** (-0.5)
        q = (x @ wq).reshape(B, N, H, HD).transpose(0, 2, 1, 3)
        k = (x @ wk).reshape(B, N, H, HD).transpose(0, 2, 1, 3)
        v = (x @ wv).reshape(B, N, H, HD).transpose(0, 2, 1, 3)
        attn = jnp.einsum('bhid,bhjd->bhij', q, k) * scale
        rpk = rel_pos_embed(N, rk_v, rk_h)
        attn = attn + jnp.einsum('bhid,ijd->bhij', q, rpk) * scale
        attn = jax.nn.softmax(attn, axis=-1)
        out = jnp.einsum('bhij,bhjd->bhid', attn, v)
        rpv = rel_pos_embed(N, rv_v, rv_h)
        out = out + jnp.einsum('bhij,ijd->bhid', attn, rpv)
        out = out.transpose(0, 2, 1, 3).reshape(B, N, H * HD)
        return out @ wproj + bproj

    def _L1_ffn_ref(x, Ws, bs, W1, b1, W2, b2):
        import jax, jax.numpy as jnp
        import numpy as np
        B, S, D, F, E = (4, 512, 192, 768, 8)
        b, s, d = x.shape
        xt = x.reshape(-1, d)
        logits = xt @ Ws + bs
        probs = jax.nn.softmax(logits, axis=-1)
        routes = jnp.argmax(probs, axis=-1)
        prob_max = jnp.max(probs, axis=-1)
        h = jax.nn.gelu(jnp.einsum('td,edf->etf', xt, W1) + b1[:, None, :], approximate=False)
        y = jnp.einsum('etf,efd->etd', h, W2) + b2[:, None, :]
        out = jnp.take_along_axis(y, routes[None, :, None], axis=0)[0]
        out = out * prob_max[:, None]
        return out.reshape(b, s, d)
    h = _L0_tok_ref(x, L0_tok_w_t3, L0_tok_b_t3, L0_tok_w_c3, L0_tok_b_c3, L0_tok_w_t5, L0_tok_b_t5, L0_tok_w_c5, L0_tok_b_c5, L0_tok_w_t7, L0_tok_b_t7, L0_tok_w_c7, L0_tok_b_c7)
    h = h + _L0_attn_ref(_layernorm(h, axis=-1), L0_attn_Wq, L0_attn_Wk, L0_attn_Wv, L0_attn_Wo)
    h = h + _L0_ffn_ref(_layernorm(h, axis=-1), L0_ffn_norm_w, L0_ffn_router_w, L0_ffn_gate_w, L0_ffn_up_w, L0_ffn_down_w)
    h = h + _L1_attn_ref(_layernorm(h, axis=-1), L1_attn_wq, L1_attn_wk, L1_attn_wv, L1_attn_wproj, L1_attn_bproj, L1_attn_rk_v, L1_attn_rk_h, L1_attn_rv_v, L1_attn_rv_h)
    h = h + _L1_ffn_ref(_layernorm(h, axis=-1), L1_ffn_Ws, L1_ffn_bs, L1_ffn_W1, L1_ffn_b1, L1_ffn_W2, L1_ffn_b2)
    return h

_drawn_inputs = setup_inputs


def setup_inputs(seed=0):
    import zlib

    import numpy as np

    out = dict(_drawn_inputs(seed))
    spreads = {'L0_ffn_norm_w': (1.0, 0.6),
     'L1_attn_bproj': (0.0, 2.0),
     'L1_ffn_bs': (0.0, 0.8),
     'L1_ffn_b1': (0.0, 0.8),
     'L1_ffn_b2': (0.0, 2.0)}
    factors = {'L0_tok_w_c3': 3.664,
     'L0_attn_Wq': 8.0,
     'L0_attn_Wk': 8.0,
     'L0_attn_Wv': 8.0,
     'L0_attn_Wo': 8.0,
     'L0_ffn_router_w': 4.109,
     'L0_ffn_gate_w': 3.579,
     'L0_ffn_up_w': 3.656,
     'L0_ffn_down_w': 3.666,
     'L1_attn_wq': 8.0,
     'L1_attn_wk': 8.0,
     'L1_attn_wv': 6.851,
     'L1_attn_wproj': 6.904,
     'L1_attn_rk_v': 64.0,
     'L1_attn_rk_h': 64.0,
     'L1_attn_rv_v': 64.0,
     'L1_attn_rv_h': 64.0,
     'L1_ffn_Ws': 8.0,
     'L1_ffn_W1': 8.0,
     'L1_ffn_W2': 8.0}
    for name, (base, spread) in spreads.items():
        noise = np.random.default_rng([zlib.crc32(name.encode()), seed]).standard_normal(out[name].shape)
        drawn = base * np.exp(spread * noise) if base else spread * noise
        out[name] = jnp.asarray(drawn.astype(out[name].dtype))
    for name, factor in factors.items():
        out[name] = (out[name] * factor).astype(out[name].dtype)
    return out
```

```python
import itertools

import numpy as np

import concourse.bass as bass
from concourse import mybir
from contextlib import ExitStack

F32 = mybir.dt.float32
F32R = mybir.dt.float32r
I32 = mybir.dt.int32
U32 = mybir.dt.uint32
ALU = mybir.AluOpType
ACT = mybir.ActivationFunctionType
AX = mybir.AxisListType

B, D, L = 4, 64, 750
KS = (3, 5, 7)
E = len(KS) * D
CH, P = 6, 125
NT = B * CH
H0, FEAT = 12, 16
EPS = 1e-5
HALF = L // 2

MONO = [()] + [(a,) for a in range(3)] + list(itertools.combinations_with_replacement(range(3), 2)) \
    + list(itertools.combinations_with_replacement(range(3), 3))
MI = {m: i for i, m in enumerate(MONO)}
NM = len(MONO)
PAIRS = [m for m in MONO if len(m) == 2]
FEATS = [(a, m) for a in MONO if len(a) == 2 for m in MONO if len(m) == 3] \
    + [(a, m) for a in MONO if len(a) == 1 for m in MONO if len(m) == 2] \
    + [((), m) for m in MONO if len(m) == 1] \
    + [(a, m) for a in MONO if len(a) == 2 for m in MONO if len(m) == 2] \
    + [(a, m) for a in MONO if len(a) == 1 for m in MONO if len(m) == 1] + [((), ())]
FI = {f: i for i, f in enumerate(FEATS)}
NF = len(FEATS)
ROWS = [(a, b, c, d) for a in range(3) for b in range(3) for c in range(3) for d in range(3)] \
    + [(a, b) for a in range(3) for b in range(3)] + [()]
NR = len(ROWS)


def moment_constants():
    sel = np.zeros((128, B, 2, NF), np.float32)
    for b in range(B):
        for f, (a, m) in enumerate(FEATS):
            sel[32 * b + MI[a], b, 0, f] = 1.0
            sel[32 * b + MI[m], b, 1, f] = 1.0
    xy = np.zeros((128, B, 2, NR), np.float32)
    merge = np.zeros((NR, 4, NF), np.float32)
    for r, row in enumerate(ROWS):
        ab = [row[0:2], row[2:4]]
        for side in range(2):
            j = 3 * ab[side][0] + ab[side][1] if ab[side] else 9
            for b in range(B):
                xy[32 * b + j, b, side, r] = 1.0
        left = tuple(sorted(row[0::2]))
        right = row[1::2]
        w = 0.5 if len(row) == 4 else 1.0
        for i in range(3):
            merge[r, i, FI[(left, tuple(sorted(right + (i,))))]] += w
        merge[r, 3, FI[(left, tuple(sorted(right)))]] += w
    one9 = np.zeros((128, 1), np.float32)
    one9[9::32] = 1.0
    return sel, xy, merge, one9


def conv_weights(w, b):
    out = np.zeros((17, 7, 4, 3), w[0].dtype)
    for k, width in enumerate(KS):
        at = 3 - width // 2
        for i in range(B):
            out[4 * i:4 * i + 4, at:at + width, i, k] = w[k][0]
        out[16, 3, :, k] = b[k][0]
    return out.reshape(17, 7, 12)


class Chain:

    def __init__(self, eng, sem):
        self.eng, self.sem, self.n = eng, sem, 0

    def __call__(self, ins):
        self.n += 1
        ins.then_inc(self.sem, 1)
        self.eng.wait_ge(self.sem, self.n)


class Stage:

    def __init__(self, nc):
        self.nc, self.stack, self.all = nc, ExitStack(), []

    def enter_context(self, semaphore):
        self.all.append(self.stack.enter_context(semaphore))
        return self.all[-1]

    def close(self):
        with self.nc.Block() as block:
            @block.gpsimd
            def _(pool):
                for s in self.all:
                    pool.sem_clear(s)
        self.stack.close()


def token_mixer_and_attention(nc, keep, A, h, ident):
    ctx = ExitStack()
    with ctx:
        def sb(name, shape, dt=F32):
            return ctx.enter_context(nc.sbuf_tensor(name, shape, dt))

        def sem(name):
            return keep.enter_context(nc.semaphore(name))

        xd = sb("xd", [D, B, L])
        xT = sb("xT", [P, CH, B, D])
        xc = sb("xc", [P, CH, B, D])
        wt = sb("wt", [17, 7, 12])
        wc = sb("wc", [17, 7, 12])
        wqk = sb("wqk", [D, 2, 3, E])
        wv = sb("wv", [D, 3, E])
        wo = sb("wo", [96, 2, E])
        sel = sb("sel", [128, B, 2, NF])
        selxy = sb("selxy", [128, B, 2, NR])
        merge = sb("merge", [NR, 4, NF])
        one9 = sb("one9", [128, 1])
        statT = sb("statT", [P, CH, 17])
        statC = sb("statC", [D, 17])
        smean = sb("smean", [D, B])
        nmean = sb("nmean", [D, B])
        ssq = sb("ssq", [D, B])
        mtok = sb("mtok", [P, NT])
        sqd = sb("sqd", [D, L])
        poolT = sb("poolT", [17, L + 6])
        poolC = sb("poolC", [17, D + 6])
        wgtT = sb("wgtT", [P, CH, 12])
        wgtC = sb("wgtC", [D, 12])
        ones64 = sb("ones64", [D, 128])
        rt = sb("rt", [D, 12])
        rtc = sb("rtc", [D, 2, 12])
        bm = sb("bm", [128, 2, 12])
        v0 = sb("v0", [128, B])
        rc = sb("rc", [P, B, CH, 3])
        hm = sb("hm", [P, B, CH, 3])
        ak = sb("ak", [P, B, CH, 3])
        aq = sb("aq", [P, B, CH, 3])
        m1 = sb("m1", [P, B, CH])
        rs = sb("rs", [P, B, CH])
        phi = sb("phi", [P, CH, B, 32])
        phiT = sb("phiT", [128, L])
        ones = sb("ones", [128, L])
        S = sb("S", [128, L])
        basis = sb("basis", [D, 3, B, 3])
        qku = sb("qku", [D, 2, 3, B, 32])
        vu = sb("vu", [D, 3, B, 3, NR])
        qs = sb("qs", [128, E])
        qk = sb("qk", [128, E])
        Mx = sb("Mx", [128, H0])
        xs = sb("xs", [NR, H0])
        T2 = sb("T2", [NR, B, H0])
        T3 = sb("T3", [NR, 3, E])
        C = sb("C", [NF, B, E + H0])
        G1 = sb("G1", [NF, L])
        Ft = sb("Ft", [NF, B, L])
        diag = sb("diag", [D, 12, D])
        u0row = sb("u0row", [P, B, E])
        rden = sb("rden", [P, 2, H0])
        yn = sb("yn", [P, 2, E])
        yT = sb("yT", [96, 2, 2, P])
        ps = [ctx.enter_context(nc.psum_tensor(f"psA{i}", [128, 512], F32)) for i in range(8)]

        s_x, s_w, s_cst = sem("s_x"), sem("s_w"), sem("s_cst")
        s_id = sem("s_id")
        s_a, s_v, s_g = sem("s_a"), sem("s_v"), sem("s_g")
        s_xt, s_xtc = sem("s_xt"), sem("s_xtc")
        s_mean, s_var = sem("s_mean"), sem("s_var")
        s_std, s_sd = sem("s_std"), sem("s_sd")
        s_stat, s_statT, s_pool = sem("s_stat"), sem("s_statT"), sem("s_pool")
        s_conv, s_wgt, s_rows, s_rowc = sem("s_conv"), sem("s_wgt"), sem("s_rows"), sem("s_rowc")
        s_bm, s_usq, s_v0, s_phi, s_phiT, s_phic, s_S = (sem(n) for n in (
            "s_bm", "s_usq", "s_v0", "s_phi", "s_phiT", "s_phic", "s_S"))
        s_basis, s_qk, s_qc, s_Mx, s_xy, s_xyc, s_T2 = (sem(n) for n in (
            "s_basis", "s_qk", "s_qc", "s_Mx", "s_xy", "s_xyc", "s_T2"))
        s_vps, s_T3, s_C, s_Cc = sem("s_vps"), sem("s_T3"), sem("s_C"), sem("s_Cc")
        s_G, s_Gc, s_F = sem("s_G"), sem("s_Gc"), sem("s_F")
        s_dg, s_u0, s_u0c = sem("s_dg"), sem("s_u0"), sem("s_u0c")
        s_y, s_yn, s_yt, s_ytc, s_o, s_h = (sem(n) for n in ("s_y", "s_yn", "s_yt", "s_ytc", "s_o", "s_h"))
        block = ctx.enter_context(nc.Block())

        @block.sync
        def _(sp):
            for b in range(B):
                sp.dma_start(xd[:, b, :], A["x"][b]).then_inc(s_x, 16)
            sp.dma_start(wt[:], A["wt"]).then_inc(s_w, 16)
            sp.dma_start(wc[:], A["wc"]).then_inc(s_w, 16)
            sp.dma_start(sel[:], A["sel"]).then_inc(s_w, 16)
            sp.dma_start(selxy[:], A["selxy"]).then_inc(s_w, 16)
            sp.dma_start(merge[:], A["merge"]).then_inc(s_w, 16)
            sp.dma_start(one9[:], A["one9"]).then_inc(s_w, 16)
            sp.dma_start(wqk[:, 0], A["Wq0T"].rearrange("(k d) f -> d k f", d=D)).then_inc(s_w, 16)
            sp.dma_start(wqk[:, 1], A["Wk0T"].rearrange("(k d) f -> d k f", d=D)).then_inc(s_w, 16)
            sp.dma_start(wv[:], A["Wv0T"].rearrange("(k d) f -> d k f", d=D)).then_inc(s_w, 16)
            sp.dma_start(wo[:], A["Wo0T"].rearrange("(k f) e -> f k e", f=96)).then_inc(s_w, 16)
            sp.wait_ge(s_x, 64)
            sp.wait_ge(s_w, 160)

        @block.gpsimd
        def _(pool):
            pool.memset(ident[:], 0.0).then_inc(s_g, 1)
            pool.wait_ge(s_g, 1)
            pool.affine_select(out=ident[:], in_=ident[:], compare_op=ALU.not_equal, fill=1.0, base=0,
                               pattern=[[-1, 128]], channel_multiplier=1).then_inc(s_id, 1)
            pool.memset(statT[:], 1.0)
            pool.memset(statC[:], 1.0)
            pool.memset(poolT[:], 0.0)
            pool.memset(poolC[:], 0.0)
            pool.memset(ones64[:], 1.0 / D)
            pool.memset(ones[:], 1.0)
            pool.memset(phi[:], 0.0)
            pool.memset(qku[:], 0.0)
            pool.memset(basis[:], 0.0).then_inc(s_g, 1)
            pool.wait_ge(s_g, 2)
            pool.memset(phi[:, :, :, 0:1], 1.0)
            pool.memset(basis[:, 0, :, 1:2], 1.0)
            pool.memset(basis[:, 1, :, 2:3], 1.0)
            pool.memset(basis[:, 2, :, 1:3], -1.0).then_inc(s_cst, 1)

        @block.tensor
        def _(pe):
            pe.wait_ge(s_x, 16 * B)
            pe.wait_ge(s_id, 1)
            for c in range(CH):
                for b in range(B):
                    g = c * B + b
                    last = nc.tensor.transpose(ps[g // 8][0:P, (g % 8) * D:(g % 8 + 1) * D],
                                               xd[:, b, c * P:(c + 1) * P], ident[0:D, 0:D])
                    if g % 8 == 7:
                        last.then_inc(s_xt, 1)
            pe.wait_ge(s_stat, 2)
            for c in range(CH):
                nc.tensor.transpose(ps[3 + c // 4][0:17, (c % 4) * P:(c % 4 + 1) * P], statT[:, c, :],
                                    ident[0:P, 0:P])
            nc.tensor.transpose(ps[5][0:17, 0:D], statC[:], ident[0:D, 0:D]).then_inc(s_statT, 1)
            pe.wait_ge(s_w, 160)
            pe.wait_ge(s_pool, 1)
            for c in range(CH):
                for t in range(7):
                    nc.tensor.matmul(ps[6][0:P, 12 * c:12 * c + 12], poolT[:, c * P + t:c * P + t + P], wt[:, t, :],
                                     start=(t == 0), stop=(t == 6))
            for t in range(7):
                last = nc.tensor.matmul(ps[7][0:D, 0:12], poolC[:, t:t + D], wc[:, t, :],
                                        start=(t == 0), stop=(t == 6))
            last.then_inc(s_conv, 1)
            pe.wait_ge(s_wgt, 1)
            for b in range(B):
                for c in range(CH):
                    nc.tensor.matmul(ps[0][0:D, 3 * b:3 * b + 3], xT[:, c, b, :], wgtT[:, c, 3 * b:3 * b + 3],
                                     start=(c == 0), stop=(c == CH - 1))
            for b in range(B):
                for c in range(CH):
                    at = 3 * (b * CH + c)
                    last = nc.tensor.matmul(ps[1][0:P, at:at + 3], xd[:, b, c * P:(c + 1) * P],
                                            wgtC[:, 3 * b:3 * b + 3], start=True, stop=True)
            last.then_inc(s_rows, 1)
            pe.wait_ge(s_rowc, 1)
            pe.wait_ge(s_cst, 1)
            nc.tensor.matmul(ps[2][:, 0:12], ones64[:], rt[:], start=True, stop=True).then_inc(s_bm, 1)
            pe.wait_ge(s_usq, 1)
            nc.tensor.matmul(ps[3][:, 0:12], ones64[:], rtc[:, 1, :], start=True, stop=True).then_inc(s_v0, 1)
            pe.wait_ge(s_basis, 1)
            for j in range(2):
                for k in range(3):
                    last = nc.tensor.matmul(ps[4 + j][:, 0:E], qku[:, j, k, :, :].rearrange("d b r -> d (b r)"),
                                            wqk[:, j, k, :], start=(k == 0), stop=(k == 2))
            last.then_inc(s_qk, 1)
            for b in range(B):
                for k in range(3):
                    bank = 6 + b // 2
                    last = nc.tensor.matmul(ps[bank][0:P, (b % 2) * E + k * D:(b % 2) * E + (k + 1) * D],
                                            ones[0:D, 0:P], diag[:, 3 * b + k, :], start=True, stop=True)
            last.then_inc(s_u0, 1)
            pe.wait_ge(s_phi, 1)
            for c in range(CH):
                last = nc.tensor.transpose(ps[c // 4][:, (c % 4) * P:(c % 4 + 1) * P],
                                           phi[:, c, :, :].rearrange("p b s -> p (b s)"), ident[0:P, 0:P])
            last.then_inc(s_phiT, 1)
            pe.wait_ge(s_Mx, 1)
            for b in range(B):
                for side in range(2):
                    last = nc.tensor.matmul(ps[4 + side][0:NR, b * H0:(b + 1) * H0], selxy[:, b, side, :],
                                            Mx[:], start=True, stop=True)
            last.then_inc(s_xy, 1)
            for b in range(B):
                if b >= 1:
                    pe.wait_ge(s_T3, b)
                else:
                    pe.wait_ge(s_phic, 1)
                    pe.wait_ge(s_u0c, 1)
                for i in range(3):
                    bank = (2, 3, 6)[i]
                    for k in range(3):
                        last = nc.tensor.matmul(ps[bank][0:NR, 0:E], vu[:, k, b, i, :], wv[:, k, :],
                                                start=(k == 0), stop=(k == 2))
                last.then_inc(s_vps, 1)
                pe.wait_ge(s_T3, b + 1)
                if b >= 1:
                    pe.wait_ge(s_Cc, b)
                for i in range(3):
                    nc.tensor.matmul(ps[7][0:NF, 0:E], merge[:, i, :], T3[:, i, :], start=(i == 0), stop=(i == 2))
                nc.tensor.matmul(ps[7][0:NF, E:E + H0], merge[:, 3, :], T2[:, b, :], start=True,
                                 stop=True).then_inc(s_C, 1)
            pe.wait_ge(s_S, 1)
            for b in range(B):
                if b >= 1:
                    pe.wait_ge(s_Gc, b)
                    pe.wait_ge(s_F, b)
                for f in range(2):
                    for n in range(2):
                        last = nc.tensor.matmul(ps[2 * f + n][0:NF, 0:HALF], sel[:, b, f, :],
                                                (phiT if f == 0 else S)[:, n * HALF:(n + 1) * HALF],
                                                start=True, stop=True)
                    if f == 1:
                        last.then_inc(s_G, 1)
            pe.wait_ge(s_Cc, B)
            pe.wait_ge(s_F, B)

            def project(t):
                pe.wait_ge(s_yn, t + 1)
                if t >= 2:
                    pe.wait_ge(s_ytc, t - 1)
                for k in range(2):
                    last = nc.tensor.transpose(ps[6 + t % 2][0:96, k * P:(k + 1) * P],
                                               yn[:, t % 2, 96 * k:96 * k + 96], ident[0:P, 0:P])
                last.then_inc(s_yt, 1)
                pe.wait_ge(s_ytc, t + 1)
                if t >= 2:
                    pe.wait_ge(s_h, t - 1)
                for k in range(2):
                    last = nc.tensor.matmul(ps[4 + t % 2][0:P, 0:E], yT[:, t % 2, k, :], wo[:, k, :],
                                            start=(k == 0), stop=(k == 1))
                last.then_inc(s_o, 1)

            for t in range(NT):
                b, c = divmod(t, CH)
                if t >= 2:
                    pe.wait_ge(s_yn, t - 1)
                nc.tensor.matmul(ps[t % 2][0:P, 0:E + H0], Ft[:, b, c * P:(c + 1) * P], C[:, b, :],
                                 start=True, stop=True).then_inc(s_y, 1)
                if t >= 1:
                    project(t - 1)
            project(NT - 1)

        @block.scalar
        def _(act):
            link = Chain(act, s_a)
            for g in range(3):
                act.wait_ge(s_xt, g + 1)
                nc.scalar.activation(xT[:].rearrange("p c b d -> p (c b d)")[:, g * 512:(g + 1) * 512],
                                     ps[g][0:P, :], ACT.Copy).then_inc(s_xtc, 1)
            act.wait_ge(s_mean, 1)
            for b in range(B):
                link(nc.scalar.activation(sqd[:], xd[:, b, :], ACT.Square, bias=nmean[:, b:b + 1],
                                          accum_out=ssq[:, b:b + 1]))
            act.wait_ge(s_cst, 1)
            nc.scalar.activation(statC[:, 1:16:4], ssq[:], ACT.Sqrt, scale=1.0 / (L - 1)).then_inc(s_stat, 1)
            act.wait_ge(s_var, 1)
            nc.scalar.activation(statT[:, :, 1:16:4], m1[:].rearrange("p b c -> p (b c)").rearrange(
                "p (c b) -> p c b", b=B), ACT.Sqrt, scale=1.0 / (D - 1)).then_inc(s_std, 1)
            act.wait_ge(s_statT, 1)
            nc.scalar.activation(poolT[:, 3:3 + 4 * P], ps[3][0:17, 0:4 * P], ACT.Copy)
            nc.scalar.activation(poolT[:, 3 + 4 * P:3 + L], ps[4][0:17, 0:2 * P], ACT.Copy)
            nc.scalar.activation(poolC[:, 3:3 + D], ps[5][0:17, 0:D], ACT.Copy).then_inc(s_pool, 1)
            act.wait_ge(s_conv, 1)
            nc.scalar.activation(wgtT[:].rearrange("p c k -> p (c k)"), ps[6][0:P, 0:72], ACT.Relu)
            nc.scalar.activation(wgtC[:], ps[7][0:D, 0:12], ACT.Relu).then_inc(s_wgt, 1)
            act.wait_ge(s_var, 2)
            nc.scalar.activation(rs[:], rs[:], ACT.Sqrt).then_inc(s_std, 1)
            act.wait_ge(s_phiT, 1)
            nc.scalar.activation(phiT[:, 0:4 * P], ps[0][:, 0:4 * P], ACT.Copy)
            nc.scalar.activation(phiT[:, 4 * P:L], ps[1][:, 0:2 * P], ACT.Copy).then_inc(s_phic, 1)
            act.wait_ge(s_u0, 1)
            nc.scalar.activation(u0row[:, 0:2, :].rearrange("p b e -> p (b e)"), ps[6][0:P, 0:2 * E], ACT.Copy,
                                 scale=float(D) / D)
            nc.scalar.activation(u0row[:, 2:4, :].rearrange("p b e -> p (b e)"), ps[7][0:P, 0:2 * E],
                                 ACT.Copy).then_inc(s_u0c, 1)
            for b in range(B):
                act.wait_ge(s_C, b + 1)
                nc.scalar.activation(C[:, b, :], ps[7][0:NF, 0:E + H0], ACT.Copy).then_inc(s_Cc, 1)
            for b in range(B):
                act.wait_ge(s_G, b + 1)
                if b >= 1:
                    act.wait_ge(s_F, b)
                for n in range(2):
                    last = nc.scalar.activation(G1[:, n * HALF:(n + 1) * HALF], ps[n][0:NF, 0:HALF], ACT.Copy)
                last.then_inc(s_Gc, 1)
            for t in range(NT):
                act.wait_ge(s_yt, t + 1)
                if t >= 2:
                    act.wait_ge(s_o, t - 1)
                nc.scalar.activation(yT[:, t % 2, :, :].rearrange("f k p -> f (k p)"), ps[6 + t % 2][0:96, 0:2 * P],
                                     ACT.Copy).then_inc(s_ytc, 1)

        @block.vector
        def _(dve):
            v = nc.vector
            link = Chain(dve, s_v)
            dve.wait_ge(s_x, 16 * B)
            dve.wait_ge(s_cst, 1)
            link(v.tensor_reduce(smean[:], xd[:], AX.X, ALU.add))
            v.tensor_scalar(nmean[:], smean[:], -1.0 / L, None, ALU.mult).then_inc(s_mean, 1)
            v.tensor_scalar(statC[:, 0:16:4], smean[:], 1.0 / L, None, ALU.mult)
            v.tensor_reduce(statC[:, 2:16:4], xd[:], AX.X, ALU.max)
            link(v.tensor_reduce(statC[:, 3:16:4], xd[:], AX.X, ALU.min))
            dve.wait_ge(s_xtc, 3)
            xg = xT[:].rearrange("p c b d -> p (c b) d")
            cg = xc[:].rearrange("p c b d -> p (c b) d")
            link(v.tensor_reduce(mtok[:], xg, AX.X, ALU.add))
            link(v.tensor_scalar(mtok[:], mtok[:], 1.0 / D, None, ALU.mult))
            link(v.tensor_tensor(cg, xg, mtok[:].unsqueeze(2).broadcast_to([P, NT, D]), ALU.subtract))
            link(v.tensor_tensor(cg, cg, cg, ALU.mult))
            v.tensor_reduce(m1[:].rearrange("p b c -> p (b c)"), cg, AX.X, ALU.add).then_inc(s_var, 1)
            v.tensor_copy(statT[:, :, 0:16:4], mtok[:].rearrange("p (c b) -> p c b", b=B))
            v.tensor_reduce(statT[:, :, 2:16:4], xT[:], AX.X, ALU.max)
            link(v.tensor_reduce(statT[:, :, 3:16:4], xT[:], AX.X, ALU.min))
            dve.wait_ge(s_std, 1)
            v.sem_inc(s_stat, 1)
            dve.wait_ge(s_rows, 1)
            v.tensor_copy(rt[:], ps[0][0:D, 0:12]).then_inc(s_rowc, 1)
            link(v.tensor_copy(rc[:].rearrange("p b c k -> p (b c k)"), ps[1][0:P, 0:72]))
            dve.wait_ge(s_bm, 1)
            link(v.tensor_scalar(bm[:, 0, :], ps[2][:, 0:12], 0.5, None, ALU.mult))
            link(v.tensor_scalar(rtc[:, 0, :], rt[:], 0.5, None, ALU.mult))
            link(v.tensor_tensor(rtc[:, 0, :], rtc[:, 0, :], bm[0:D, 0, :], ALU.subtract))
            v.tensor_tensor(rtc[:, 1, :], rtc[:, 0, :], rtc[:, 0, :], ALU.mult).then_inc(s_usq, 1)
            link(v.tensor_copy(basis[:, :, :, 0], rtc[:, 0, :].rearrange("d (b k) -> d k b", k=3)))
            for a in range(3):
                v.tensor_copy(qku[:, 0, :, :, 3 * a:3 * a + 3].rearrange("d k b r -> d (k b) r"),
                              basis[:, :, :, a:a + 1].rearrange("d k b r -> d (k b) r").broadcast_to([D, 12, 3]))
                v.tensor_copy(qku[:, 1, :, :, 3 * a:3 * a + 3], basis[:])
            for k in range(3):
                v.tensor_copy(vu[:, k, :, :, :].rearrange("d b i r -> d (b i) r"),
                              basis[:, k, :, :].rearrange("d b i -> d (b i)").unsqueeze(2).broadcast_to([D, 12, NR]))
            for j in range(12):
                last = v.tensor_scalar(diag[:, j, :], ident[0:D, 0:D], rtc[:, 0, j:j + 1], None, ALU.mult)
            last.then_inc(s_basis, 1)
            link(
                 v.tensor_scalar(hm[:], rc[:], 0.5, None, ALU.mult))
            for c in range(CH):
                link(v.tensor_tensor(hm[:, :, c, :], hm[:, :, c, :],
                                     bm[0:P, 0, :].rearrange("p (b k) -> p b k", k=3), ALU.add))
            link(v.tensor_reduce(m1[:], hm[:], AX.X, ALU.add))
            link(v.tensor_scalar(m1[:], m1[:], 1.0 / 3, None, ALU.mult))
            hg = hm[:].rearrange("p b c k -> p (b c) k")
            ag = ak[:].rearrange("p b c k -> p (b c) k")
            mg = m1[:].rearrange("p b c -> p (b c)")
            link(v.tensor_tensor(ag, hg, mg.unsqueeze(2).broadcast_to([P, NT, 3]), ALU.subtract))
            link(v.tensor_tensor(aq[:], ak[:], ak[:], ALU.mult))
            link(v.tensor_reduce(rs[:], aq[:], AX.X, ALU.add))
            dve.wait_ge(s_v0, 1)
            link(v.tensor_reduce(v0[:], ps[3][:, 0:12].rearrange("p (b k) -> p b k", k=3), AX.X, ALU.add))
            link(v.tensor_tensor(rs[:], rs[:], v0[0:P, :].unsqueeze(2).broadcast_to([P, B, CH]), ALU.add))
            v.tensor_scalar(rs[:], rs[:], 1.0 / 3, EPS, ALU.mult, ALU.add).then_inc(s_var, 1)
            dve.wait_ge(s_std, 2)
            link(v.reciprocal(rs[:], rs[:]))
            rcb = rs[:].rearrange("p b c -> p c b")
            link(v.tensor_copy(phi[:, :, :, 1], rcb))
            for a in range(2):
                link(v.tensor_tensor(phi[:, :, :, 2 + a], rcb, ak[:, :, :, a].rearrange("p b c -> p c b"), ALU.mult))
            pg = phi[:].rearrange("p c b s -> p (c b) s")

            def product(out, n, a, src):
                link(v.tensor_tensor(pg[:, :, out:out + n], pg[:, :, 1 + a:2 + a].broadcast_to([P, NT, n]),
                                     pg[:, :, src:src + n], ALU.mult))

            product(4, 3, 0, 1)
            product(7, 2, 1, 2)
            product(9, 1, 2, 3)
            product(10, 6, 0, 4)
            product(16, 3, 1, 7)
            product(19, 1, 2, 9)
            v.sem_inc(s_phi, 1)
            dve.wait_ge(s_qk, 1)
            link(v.tensor_copy(qs[:], ps[4][:, 0:E]))
            link(v.tensor_tensor(qk[:], qs[:], ps[5][:, 0:E], ALU.mult))
            link(v.tensor_reduce(Mx[:], qk[:].rearrange("p (h f) -> p h f", f=FEAT), AX.X, ALU.add))
            link(v.tensor_scalar(Mx[:], Mx[:], 0.25, one9[:], ALU.mult, ALU.add))
            v.sem_inc(s_Mx, 1)
            dve.wait_ge(s_phic, 1)
            link(v.tensor_tensor_scan(S[:], ones[:], phiT[:], 0.0, ALU.mult, ALU.add))
            link(v.tensor_copy(v0[:, 0:1], S[:, L - 1:L]))
            v.tensor_scalar(S[:], S[:], v0[:, 0:1], None, ALU.add).then_inc(s_S, 1)
            dve.wait_ge(s_xy, 1)
            for b in range(B):
                link(v.tensor_copy(xs[:], ps[4][0:NR, b * H0:(b + 1) * H0]))
                link(v.tensor_tensor(T2[:, b, :], xs[:], ps[5][0:NR, b * H0:(b + 1) * H0], ALU.mult))
            for b in range(B):
                dve.wait_ge(s_vps, b + 1)
                if b >= 1:
                    dve.wait_ge(s_C, b)
                for i in range(3):
                    last = v.tensor_tensor(T3[:, i, :].rearrange("r (h e) -> r h e", e=FEAT),
                                           T2[:, b, :].unsqueeze(2).broadcast_to([NR, H0, FEAT]),
                                           ps[(2, 3, 6)[i]][0:NR, 0:E].rearrange("r (h e) -> r h e", e=FEAT), ALU.mult)
                last.then_inc(s_T3, 1)
            for b in range(B):
                dve.wait_ge(s_Gc, b + 1)
                for n in range(2):
                    at = slice(n * HALF, (n + 1) * HALF)
                    last = v.tensor_tensor(Ft[:, b, at], G1[:, at], ps[2 + n][0:NF, 0:HALF], ALU.mult)
                last.then_inc(s_F, 1)

            def residual(t):
                b, c = divmod(t, CH)
                dve.wait_ge(s_o, t + 1)
                link(v.tensor_tensor(h[:, t, :], ps[4 + t % 2][0:P, 0:E], u0row[:, b, :], ALU.add))
                hk = h[:, t, :].rearrange("p (k d) -> p k d", k=3)
                v.tensor_tensor(hk, hk, hm[:, b, c, :].unsqueeze(2).broadcast_to([P, 3, D]), ALU.add).then_inc(s_h, 1)

            for t in range(NT):
                dve.wait_ge(s_y, t + 1)
                if t >= 2:
                    dve.wait_ge(s_yt, t - 1)
                link(v.reciprocal(rden[:, t % 2, :], ps[t % 2][0:P, E:E + H0]))
                v.tensor_tensor(yn[:, t % 2, :].rearrange("p (h e) -> p h e", e=FEAT),
                                ps[t % 2][0:P, 0:E].rearrange("p (h e) -> p h e", e=FEAT),
                                rden[:, t % 2, :].unsqueeze(2).broadcast_to([P, H0, FEAT]), ALU.mult).then_inc(s_yn, 1)
                if t >= 1:
                    residual(t - 1)
            residual(NT - 1)
            dve.wait_ge(s_h, NT)


NE, SLOT = 8, 128


class Moe:

    def __init__(self, name, top, width, gated):
        self.name, self.top, self.width, self.gated = name, top, width, gated
        worst = (NT * P * top) // SLOT + NE
        self.tiles = worst + worst % 2
        self.cols = 2 * width if gated else width
        self.kc = width // 128


MOE0 = Moe("m0", 2, 384, True)
MOE1 = Moe("m1", 1, 768, False)


def moe(nc, keep, A, h, ident, cfg, out):
    name, top, S = cfg.name, cfg.top, cfg.tiles
    ctx = ExitStack()
    with ctx:
        def sb(n, shape, dt=F32):
            return ctx.enter_context(nc.sbuf_tensor(f"{name}_{n}", shape, dt))

        def sem(n):
            return keep.enter_context(nc.semaphore(f"{name}_{n}"))

        kx = 96 if cfg.gated else 97
        w1 = sb("w1", [kx, NE, 2, cfg.cols])
        w2 = sb("w2", [128, NE, cfg.kc, E])
        wr = sb("wr", [96, 2, NE])
        row = sb("row", [P, E if cfg.gated else NE])
        b2 = None if cfg.gated else sb("b2", [1, NE, E])
        n = sb("n", [P, NT, E])
        xn = sb("xn", [P, NT, E]) if cfg.gated else n
        got = [xn if cfg.gated else sb("got0", [P, NT, E]), sb("got1", [P, NT, E]) if top == 2 else None]
        zero = sb("zero", [128, (S + 2) * E // 4])
        st = sb("st", [P, NT, 6])
        mv = sb("mv", [P, NT, 2])
        rstd = sb("rstd", [P, NT])
        msq = sb("msq", [P, NT])
        sq = sb("sq", [P, E])
        xnT = sb("xnT", [96, 2, 2, P])
        lg = sb("lg", [P, NT, NE])
        lm = sb("lm", [P, NT])
        pr = sb("pr", [P, NT, NE])
        tmp = sb("tmp", [P, NT, NE])
        oh = sb("oh", [P, 2, NT, NE])
        msk = sb("msk", [P, NT, NE])
        pe_ = sb("pe", [P, top, NT])
        idx = sb("idx", [P, NT])
        iotx = sb("iotx", [P, NT, NE])
        iot128 = sb("iot128", [128, NT])
        iots = sb("iots", [1, S + 2])
        tri = sb("tri", [P, P])
        ones = sb("ones", [128, NE * NT])
        tot = sb("tot", [128, NE, NT])
        inc = sb("inc", [128, NE, NT])
        exc = sb("exc", [128, NE, NT])
        cnt = sb("cnt", [128, NE])
        big = sb("big", [128, NE, NT])
        nt_ = sb("nt", [128, NE])
        cum = sb("cum", [128, NE])
        pos = sb("pos", [P, NT, NE])
        posf = sb("posf", [P, top, NT])
        posi = sb("posi", [P, top, NT], U32)
        ecmp = sb("ecmp", [1, S + 2, NE])
        eidf = sb("eidf", [1, S + 2])
        eid = sb("eid", [1, S + 2], I32)
        xg = sb("xg", [SLOT, 2, E])
        xgT = sb("xgT", [kx, 2, 2, SLOT])
        act_g = sb("act_g", [SLOT, cfg.width])
        hid = sb("hid", [SLOT, cfg.width])
        hidT = sb("hidT", [128, cfg.width])
        y = sb("y", [SLOT, 2, E])
        X = nc.dram_tensor(f"{name}_X", ((S + 2) * SLOT, E), F32, kind="Internal").ap()
        Y = nc.dram_tensor(f"{name}_Y", ((S + 2) * SLOT, E), F32, kind="Internal").ap()
        psX = ctx.enter_context(nc.psum_tensor(f"{name}_psX", [128, 512], F32))
        psG = [ctx.enter_context(nc.psum_tensor(f"{name}_psG{i}", [128, 2, 512], F32)) for i in range(2)]
        nH = cfg.width // 384
        psH = ctx.enter_context(nc.psum_tensor(f"{name}_psH", [128, nH, 512], F32))
        psY = ctx.enter_context(nc.psum_tensor(f"{name}_psY", [128, 512], F32))

        s_w, s_r, s_z, s_zero, s_cst = sem("w"), sem("r"), sem("z"), sem("zero"), sem("cst")
        s_v, s_ln, s_sd, s_n, s_sq, s_xn = sem("v"), sem("ln"), sem("sd"), sem("n"), sem("sq"), sem("xn")
        s_rt, s_rc, s_lg, s_ls, s_ex, s_m, s_rank, s_pos = (sem(k) for k in (
            "rt", "rc", "lg", "ls", "ex", "m", "rank", "pos"))
        s_eid, s_sc = sem("eid"), sem("sc")
        s_in = [sem("in0"), sem("in1")]
        s_st = [sem("st0"), sem("st1")]
        s_xt, s_xc, s_gu, s_sg, s_h, s_ht, s_hc, s_c, s_y = (sem(k) for k in (
            "xt", "xc", "gu", "sg", "h", "ht", "hc", "c", "y"))
        s_got, s_out, s_res = sem("got"), sem("out"), sem("res")
        block = ctx.enter_context(nc.Block())

        @block.sync
        def _(sp):
            sp.dma_start(wr[:], A[f"{name}_wr"]).then_inc(s_r, 16)
            sp.dma_start(row[:], A[f"{name}_row"].partition_broadcast(P)).then_inc(s_r, 16)
            sp.wait_ge(s_z, 1)
            for q in range(4):
                size = (S + 2) * E // 4
                sp.dma_start(X.rearrange("(p s) e -> p (s e)", p=128)[:, q * size:(q + 1) * size],
                             zero[:]).then_inc(s_zero, 16)
            for e in range(NE):
                sp.dma_start(w1[:, e], A[f"{name}_w1"][:, e]).then_inc(s_w, 16)
                sp.dma_start(w2[:, e], A[f"{name}_w2"][:, e]).then_inc(s_w, 16)
            if not cfg.gated:
                sp.dma_start(b2[:], A[f"{name}_b2"]).then_inc(s_w, 16)
            sp.wait_ge(s_sc, 16 * top * NT)
            for j in range(2):
                sp.dma_start(xg[:, j, :], X[j * SLOT:(j + 1) * SLOT, :]).then_inc(s_in[j], 16)
            with sp.Fori(0, S // 2) as i:
                for j in range(2):
                    sp.wait_ge(s_xt, 2 * i + (j + 1))
                    sp.dma_start(xg[:, j, :], X[bass.ds(i * (2 * SLOT) + (j + 2) * SLOT, SLOT), :]).then_inc(s_in[j], 16)
            sp.wait_ge(s_in[0], 16 * (S // 2 + 1))
            sp.wait_ge(s_in[1], 16 * (S // 2 + 1))
            if out is not None:
                for b in range(B):
                    sp.wait_ge(s_res, CH * (b + 1))
                    sp.dma_start(out[b].rearrange("(c p) e -> p c e", p=P),
                                 h[:, b * CH:(b + 1) * CH, :]).then_inc(s_out, 16)
                sp.wait_ge(s_out, 16 * B)

        @block.gpsimd
        def _(pool):
            if not cfg.gated:
                pool.memset(xgT[96:97, :, :, :], 1.0).then_inc(s_cst, 1)
                pool.wait_ge(s_cst, 1)
            pool.memset(zero[:], 0.0).then_inc(s_z, 1)
            pool.memset(ones[:], 1.0)
            pool.memset(tri[:], 1.0)
            pool.iota(iotx[:], pattern=[[0, NT], [1, NE]], base=NE, channel_multiplier=0, allow_small_or_imprecise_dtypes=True)
            pool.iota(iot128[:], pattern=[[SLOT, NT]], base=0, channel_multiplier=0,
                      allow_small_or_imprecise_dtypes=True)
            pool.iota(iots[:], pattern=[[1, S + 2]], base=0, channel_multiplier=0,
                      allow_small_or_imprecise_dtypes=True).then_inc(s_z, 1)
            pool.wait_ge(s_z, 2)
            pool.affine_select(out=tri[:], in_=tri[:], compare_op=ALU.is_gt, fill=0.0, base=0,
                               pattern=[[1, P]], channel_multiplier=-1).then_inc(s_cst, 1)
            pool.wait_ge(s_z, 2)
            for j in range(2):
                pool.dma_start(Y[(S + j) * SLOT:(S + j + 1) * SLOT, :], zero[:, 0:E]).then_inc(s_st[j], 16)
            pool.wait_ge(s_zero, 64)
            pool.wait_ge(s_pos, 1)
            for t in range(NT):
                if cfg.gated:
                    pool.wait_ge(s_xn, t + 1)
                for k in range(top):
                    pool.indirect_dma_start(out=X, out_offset=bass.IndirectOffsetOnAxis(ap=posi[:, k, t:t + 1], axis=0),
                                            in_=xn[:, t, :], in_offset=None).then_inc(s_sc, 16)
            with pool.Fori(0, S // 2) as i:
                for j in range(2):
                    pool.wait_ge(s_y, 2 * i + (j + 2))
                    pool.dma_start(Y[bass.ds(i * (2 * SLOT) + j * SLOT, SLOT), :], y[:, j, :]).then_inc(s_st[j], 16)
            pool.wait_ge(s_sc, 16 * top * NT)
            pool.wait_ge(s_st[0], 16 * (S // 2 + 1))
            pool.wait_ge(s_st[1], 16 * (S // 2 + 1))
            for t in range(NT):
                for k in range(top):
                    pool.indirect_dma_start(out=got[k][:, t, :], out_offset=None, in_=Y,
                                            in_offset=bass.IndirectOffsetOnAxis(ap=posi[:, k, t:t + 1], axis=0)
                                            ).then_inc(s_got, 16)
            pool.wait_ge(s_got, 16 * top * NT)

        @block.tensor
        def _(pe):
            pe.wait_ge(s_r, 32)

            def logits(t):
                pe.wait_ge(s_rc, t + 1)
                for k in range(2):
                    last = nc.tensor.matmul(psX[0:P, 256 + NE * t:256 + NE * t + NE], xnT[:, t % 2, k, :],
                                            wr[:, k, :], start=(k == 0), stop=(k == 1))
                last.then_inc(s_lg, 1)

            for t in range(NT):
                pe.wait_ge(s_xn if cfg.gated else s_n, t + 1)
                if t >= 2:
                    pe.wait_ge(s_rc, t - 1)
                for k in range(2):
                    last = nc.tensor.transpose(psG[t % 2][0:96, 0, k * P:(k + 1) * P], xn[:, t, 96 * k:96 * k + 96],
                                               ident[0:P, 0:P])
                last.then_inc(s_rt, 1)
                if t >= 1:
                    logits(t - 1)
            logits(NT - 1)
            pe.wait_ge(s_m, 1)
            pe.wait_ge(s_cst, 1 if cfg.gated else 2)
            mm = msk[:].rearrange("p t e -> p (t e)")
            nc.tensor.matmul(psG[0][0:P, 0, 0:NT * NE], tri[:], mm, start=True, stop=True)
            nc.tensor.matmul(psG[0][:, 1, 0:NT * NE], ones[0:P, 0:128], mm, start=True, stop=True).then_inc(s_rank, 1)

            def to_columns(buf):
                for k in range(2):
                    last = nc.tensor.transpose(psX[0:96, k * SLOT:(k + 1) * SLOT], xg[:, buf, 96 * k:96 * k + 96],
                                               ident[:])
                last.then_inc(s_xt, 1)

            def first_products(buf, e):
                half = cfg.cols // 2
                for g in range(2):
                    for k in range(2):
                        last = nc.tensor.matmul(psG[buf][:, g, 0:half], xgT[:, buf, k, :],
                                                w1[:, bass.ds(e, 1), k, g * half:(g + 1) * half].rearrange(
                                                    "d o f -> d (o f)"),
                                                start=(k == 0), stop=(k == 1))
                last.then_inc(s_gu, 1)

            pe.wait_ge(s_eid, 1)
            pe.wait_ge(s_w, 16 * (2 * NE + (0 if cfg.gated else 1)))
            for j in range(2):
                pe.wait_ge(s_in[j], 16)
                if j:
                    pe.wait_ge(s_xc, 1)
                to_columns(j)
            pe.wait_ge(s_xc, 2)
            pe.sem_inc(s_ht, 1)
            pe.sem_inc(s_c, 1)
            owner = [nc.tensor.alloc_register(f"{name}_owner{j}") for j in range(2)]
            nc.tensor.reg_load(owner[0], eid[0:1, 0:1])
            first_products(0, nc.tensor.snap(owner[0], min_val=0, max_val=NE - 1))
            with pe.Fori(0, S // 2) as i:
                for j in range(2):
                    pe.wait_ge(s_in[j], 16 * i + 32)
                    pe.wait_ge(s_xc, 2 * i + (j + 2))
                    to_columns(j)
                    pe.wait_ge(s_h, 2 * i + (j + 2))
                    pe.wait_ge(s_hc, 2 * i + (j + 1))
                    for k in range(cfg.kc):
                        last = nc.tensor.transpose(psH[:, k // 3, (k % 3) * 128:(k % 3 + 1) * 128],
                                                   hid[:, k * 128:(k + 1) * 128], ident[:])
                    last.then_inc(s_ht, 1)
                    nc.tensor.reg_load(owner[1 - j], eid[0:1, bass.ds(2 * i + (j + 1), 1)])
                    here = nc.tensor.snap(owner[j], min_val=0, max_val=NE - 1)
                    after = nc.tensor.snap(owner[1 - j], min_val=0, max_val=NE - 1)
                    first_products(1 - j, after)
                    pe.wait_ge(s_hc, 2 * i + (j + 2))
                    pe.wait_ge(s_y, 2 * i + (j + 1))
                    for k in range(cfg.kc):
                        last = nc.tensor.matmul(psY[:, 0:E], hidT[:, k * 128:(k + 1) * 128],
                                                w2[:, bass.ds(here, 1), k, :].rearrange("f o e -> f (o e)"),
                                                start=(k == 0), stop=(cfg.gated and k == cfg.kc - 1))
                    if not cfg.gated:
                        last = nc.tensor.matmul(psY[:, 0:E], ones[0:1, 0:128],
                                                b2[:, bass.ds(here, 1), :].rearrange("f o e -> f (o e)"),
                                                start=False, stop=True)
                    last.then_inc(s_c, 1)

        @block.scalar
        def _(act):
            act.wait_ge(s_ln, 1)
            nc.scalar.activation(rstd[:], rstd[:], ACT.Sqrt).then_inc(s_sd, 1)
            if cfg.gated:
                link = Chain(act, s_sq)
                for t in range(NT):
                    act.wait_ge(s_n, t + 1)
                    link(nc.scalar.activation(sq[:], n[:, t, :], ACT.Square, accum_out=msq[:, t:t + 1]))
                act.wait_ge(s_ln, 2)
                nc.scalar.activation(msq[:], msq[:], ACT.Sqrt).then_inc(s_sd, 1)
            for t in range(NT):
                act.wait_ge(s_rt, t + 1)
                if t >= 2:
                    act.wait_ge(s_lg, t - 1)
                nc.scalar.activation(xnT[:, t % 2, :, :].rearrange("d k p -> d (k p)"),
                                     psG[t % 2][0:96, 0, 0:2 * P], ACT.Copy).then_inc(s_rc, 1)
            act.wait_ge(s_ls, 1)
            nc.scalar.activation(lg[:], lg[:], ACT.Exp).then_inc(s_ex, 1)

            def columns(buf):
                nc.scalar.activation(xgT[0:96, buf, :, :].rearrange("d k p -> d (k p)"), psX[0:96, 0:2 * SLOT],
                                     ACT.Copy).then_inc(s_xc, 1)

            if not cfg.gated:
                act.wait_ge(s_z, 2)
            for j in range(2):
                act.wait_ge(s_xt, j + 1)
                columns(j)
            with act.Fori(0, S // 2) as i:
                for j in range(2):
                    act.wait_ge(s_gu, 2 * i + (j + 1))
                    if cfg.gated:
                        act.wait_ge(s_h, 2 * i + (j + 1))
                        nc.scalar.activation(act_g[:], psG[j][:, 0, 0:384], ACT.Silu).then_inc(s_sg, 1)
                    else:
                        act.wait_ge(s_ht, 2 * i + (j + 1))
                        nc.scalar.activation(hid[:].rearrange("p (a f) -> p a f", a=2), psG[j][:, :, 0:384],
                                             ACT.Gelu).then_inc(s_h, 1)
                    act.wait_ge(s_xt, 2 * i + (j + 3))
                    columns(j)

        @block.vector
        def _(dve):
            v = nc.vector
            link = Chain(dve, s_v)
            for t in range(NT):
                v.bn_stats(st[:, t, :], h[:, t, :]).then_inc(s_v, 1)
            link.n += NT
            dve.wait_ge(s_v, link.n)
            for t in range(NT):
                v.bn_aggr(mv[:, t, :], st[:, t, :]).then_inc(s_v, 1)
            link.n += NT
            dve.wait_ge(s_v, link.n)
            v.tensor_scalar(rstd[:], mv[:, :, 1], EPS, None, ALU.add).then_inc(s_ln, 1)
            dve.wait_ge(s_sd, 1)
            link(v.reciprocal(rstd[:], rstd[:]))
            for t in range(NT):
                v.tensor_scalar(n[:, t, :], h[:, t, :], mv[:, t, 0:1], rstd[:, t:t + 1], ALU.subtract,
                                ALU.mult).then_inc(s_n, 1)
            if cfg.gated:
                dve.wait_ge(s_sq, NT)
                v.tensor_scalar(msq[:], msq[:], 1.0 / E, 1e-6, ALU.mult, ALU.add).then_inc(s_ln, 1)
                dve.wait_ge(s_sd, 2)
                link(v.reciprocal(msq[:], msq[:]))
                dve.wait_ge(s_r, 32)
                for t in range(NT):
                    v.scalar_tensor_tensor(xn[:, t, :], n[:, t, :], msq[:, t:t + 1], row[:], ALU.mult,
                                           ALU.mult).then_inc(s_xn, 1)
            dve.wait_ge(s_lg, NT)
            dve.wait_ge(s_r, 32)
            lps = psX[0:P, 256:256 + NT * NE].rearrange("p (t e) -> p t e", e=NE)
            if cfg.gated:
                link(v.tensor_copy(lg[:], lps))
            else:
                link(v.tensor_tensor(lg[:], lps, row[:].unsqueeze(1).broadcast_to([P, NT, NE]), ALU.add))
            link(v.tensor_reduce(lm[:], lg[:], AX.X, ALU.max))
            v.tensor_tensor(lg[:], lg[:], lm[:].unsqueeze(2).broadcast_to([P, NT, NE]), ALU.subtract).then_inc(s_ls, 1)
            dve.wait_ge(s_ex, 1)
            link(v.tensor_reduce(lm[:], lg[:], AX.X, ALU.add))
            link(v.reciprocal(lm[:], lm[:]))
            link(v.tensor_tensor(pr[:], lg[:], lm[:].unsqueeze(2).broadcast_to([P, NT, NE]), ALU.mult))
            dve.wait_ge(s_z, 2)
            for k in range(top):
                link(v.tensor_reduce(pe_[:, k, :], pr[:], AX.X, ALU.max))
                link(v.tensor_tensor(tmp[:], pr[:], pe_[:, k, :].unsqueeze(2).broadcast_to([P, NT, NE]), ALU.is_equal))
                link(v.scalar_tensor_tensor(tmp[:].rearrange("p t e -> p (t e)"), tmp[:].rearrange("p t e -> p (t e)"),
                                            -float(NE), iotx[:].rearrange("p t e -> p (t e)"), ALU.mult, ALU.add))
                link(v.tensor_reduce(idx[:], tmp[:], AX.X, ALU.min))
                link(v.tensor_scalar(idx[:], idx[:], float(NE), None, ALU.add))
                link(v.tensor_tensor(oh[:, k, :, :], iotx[:], idx[:].unsqueeze(2).broadcast_to([P, NT, NE]), ALU.is_equal))
                if k + 1 < top:
                    link(v.scalar_tensor_tensor(pr[:].rearrange("p t e -> p (t e)"),
                                                oh[:, k, :, :].rearrange("p t e -> p (t e)"), -2.0,
                                                pr[:].rearrange("p t e -> p (t e)"), ALU.mult, ALU.add))
            if top == 2:
                v.tensor_tensor(msk[:], oh[:, 0], oh[:, 1], ALU.add).then_inc(s_m, 1)
            else:
                v.tensor_copy(msk[:], oh[:, 0]).then_inc(s_m, 1)
            dve.wait_ge(s_rank, 1)
            flat = "p e t -> p (e t)"
            link(v.tensor_copy(tot[:], psG[0][:, 1, 0:NT * NE].rearrange("p (t e) -> p e t", e=NE)))
            link(v.tensor_tensor_scan(inc[:].rearrange(flat), ones[:], tot[:].rearrange(flat), 0.0, ALU.mult, ALU.add))
            link(v.tensor_tensor(exc[:], inc[:], tot[:], ALU.subtract))
            link(v.tensor_tensor(cnt[:], inc[:, :, NT - 1], exc[:, :, 0], ALU.subtract))
            link(v.tensor_tensor(big[:], cnt[:].unsqueeze(2).broadcast_to([128, NE, NT]),
                                 iot128[:].unsqueeze(1).broadcast_to([128, NE, NT]), ALU.is_gt))
            link(v.tensor_reduce(nt_[:], big[:], AX.X, ALU.add))
            link(v.tensor_tensor_scan(cum[:], ones[:, 0:NE], nt_[:], 0.0, ALU.mult, ALU.add))
            link(v.tensor_tensor(ecmp[:], iots[:].unsqueeze(2).broadcast_to([1, S + 2, NE]),
                                 cum[0:1, :].unsqueeze(1).broadcast_to([1, S + 2, NE]), ALU.is_ge))
            link(v.tensor_reduce(eidf[:], ecmp[:], AX.X, ALU.add))
            link(v.tensor_scalar(eidf[:], eidf[:], float(NE - 1), None, ALU.min))
            v.tensor_copy(eid[:], eidf[:]).then_inc(s_eid, 1)
            link(v.tensor_tensor(cnt[:], cum[:], nt_[:], ALU.subtract))
            link(v.tensor_scalar(cnt[:], cnt[:], float(SLOT), None, ALU.mult))
            link(v.tensor_tensor(cnt[:], cnt[:], exc[:, :, 0], ALU.subtract))
            link(v.tensor_tensor(exc[:], exc[:], cnt[:].unsqueeze(2).broadcast_to([128, NE, NT]), ALU.add))
            link(v.tensor_tensor(pos[:], exc[0:P].rearrange("p e t -> p t e"),
                                 psG[0][0:P, 0, 0:NT * NE].rearrange("p (t e) -> p t e", e=NE), ALU.add))
            for k in range(top):
                link(v.tensor_tensor(tmp[:], pos[:], oh[:, k], ALU.mult))
                link(v.tensor_reduce(posf[:, k, :], tmp[:], AX.X, ALU.add))
            v.tensor_copy(posi[:], posf[:]).then_inc(s_pos, 1)
            v.sem_inc(s_h, 1)
            v.sem_inc(s_hc, 1)
            v.sem_inc(s_y, 1)
            with dve.Fori(0, S // 2) as i:
                for j in range(2):
                    if cfg.gated:
                        dve.wait_ge(s_sg, 2 * i + (j + 1))
                        dve.wait_ge(s_ht, 2 * i + (j + 1))
                        v.tensor_tensor(hid[:], act_g[:], psG[j][:, 1, 0:384], ALU.mult).then_inc(s_h, 1)
                    dve.wait_ge(s_ht, 2 * i + (j + 2))
                    dve.wait_ge(s_c, 2 * i + (j + 1))
                    v.tensor_copy(hidT[:].rearrange("p (a f) -> p a f", a=nH), psH[:, :, 0:384]).then_inc(s_hc, 1)
                    dve.wait_ge(s_c, 2 * i + (j + 2))
                    dve.wait_ge(s_st[j], 16 * i + 16)
                    v.tensor_copy(y[:, j, :], psY[:, 0:E]).then_inc(s_y, 1)
            dve.wait_ge(s_got, 16 * top * NT)
            for t in range(NT):
                if cfg.gated:
                    link(v.tensor_tensor(h[:, t, :], h[:, t, :], n[:, t, :], ALU.add))
                for k in range(top):
                    ins = v.scalar_tensor_tensor(h[:, t, :], got[k][:, t, :], pe_[:, k, t:t + 1], h[:, t, :], ALU.mult,
                                                 ALU.add)
                    if k + 1 < top:
                        link(ins)
                ins.then_inc(s_res, 1)
            dve.wait_ge(s_res, NT)


def moe_inputs(f):
    t = np.ascontiguousarray
    gu = np.concatenate([f["L0_ffn_gate_w"], f["L0_ffn_up_w"]], axis=1)
    w1 = f["L1_ffn_W1"].reshape(NE, 2, 96, 768).transpose(2, 0, 1, 3)
    w1b = np.zeros((97,) + w1.shape[1:], w1.dtype)
    w1b[:96] = w1
    w1b[96, :, 1] = f["L1_ffn_b1"]
    return {
        "m0_wr": t(f["L0_ffn_router_w"].T.reshape(2, 96, NE).transpose(1, 0, 2)),
        "m0_row": f["L0_ffn_norm_w"],
        "m0_w1": t(gu.transpose(2, 0, 1).reshape(2, 96, NE, 768).transpose(1, 2, 0, 3)),
        "m0_w2": t(f["L0_ffn_down_w"].transpose(2, 0, 1).reshape(3, 128, NE, E).transpose(1, 2, 0, 3)),
        "m1_wr": t(f["L1_ffn_Ws"].reshape(2, 96, NE).transpose(1, 0, 2)),
        "m1_row": f["L1_ffn_bs"],
        "m1_w1": w1b,
        "m1_w2": t(f["L1_ffn_W2"].reshape(NE, 6, 128, E).transpose(2, 0, 1, 3)),
        "m1_b2": t(f["L1_ffn_b2"].reshape(1, NE, E)),
    }


NH, HD, GRID, REACH = 12, 64, 27, 14
HG = 6
LP, HP = 752, 376
LW = 1 + 28 * GRID + 1
NPR = HG // 2
NVG = -(-(L - 1) // GRID)
SCALE = HD ** -0.5
RV, RH, ONE = 64, 96, 127
V_SETS = [(range(a, min(a + 6, NVG - 1)), GRID) for a in range(0, NVG - 1, 6)] + [(range(NVG - 1, NVG), L - 1 - GRID * (NVG - 1))]
FULL = L - 1 - GRID * (NVG - 1)
H_SETS = [(range(a, min(a + 6, FULL)), NVG) for a in range(0, FULL, 6)] \
    + [(range(a, min(a + 6, GRID)), NVG - 1) for a in range(FULL, GRID, 6)]
NV, NHS = len(V_SETS), len(H_SETS)
NSET = NV + NHS + 1


def relative_inputs(f):
    def rows(table, n, g):
        at = np.zeros(n, int) if g is None else np.clip(np.arange(n) - g, -REACH, REACH) + REACH + 1
        return table[at]

    out = {}
    for key, v, hh in (("rq", f["L1_attn_rk_v"], f["L1_attn_rk_h"]), ("rv", f["L1_attn_rv_v"], f["L1_attn_rv_h"])):
        for side, table, n, count in (("v", v, NVG, NVG), ("h", hh, GRID, GRID)):
            t = np.zeros((128, count + 1, 64), table.dtype)
            for g in range(count + 1):
                r = np.concatenate([rows(table, n, None if g == 0 else g - 1), table[0:1]])
                if key == "rq":
                    t[0:64, g, 0:n + 1] = r.T
                    t[64:128, g, 32:33 + n] = r.T
                else:
                    at = RV if side == "v" else RH
                    t[at:at + n + 1, g] = r
                    if side == "v":
                        t[0:64, g] = np.eye(64, dtype=table.dtype)
            out[key + side] = t
    oh = np.zeros((64, L), np.float32)
    j = np.arange(1, L)
    oh[(j - 1) // GRID, j] = 1
    oh[RH - 64 + (j - 1) % GRID, j] = 1
    oh[NVG, 0] = oh[RH - 64 + GRID, 0] = 1
    oh[ONE - 64] = 1
    out["oh"] = oh
    out["ohT"] = np.ascontiguousarray(oh.T.reshape(CH, P, 64).transpose(1, 0, 2))
    t = np.ascontiguousarray
    for k in "qkv":
        out["w" + k] = t(f["L1_attn_w" + k].reshape(2, 96, NH * HD).transpose(1, 0, 2))
    out["wp"] = t(f["L1_attn_wproj"].reshape(NH // 2, 128, E).transpose(1, 0, 2))
    out["bp"] = f["L1_attn_bproj"]
    return {"a1_" + k: v for k, v in out.items()}


def window_attention(nc, keep, A, h, ident):
    ctx = ExitStack()
    with ctx:
        def sb(n, shape, dt=F32):
            return ctx.enter_context(nc.sbuf_tensor(f"a1_{n}", shape, dt))

        def sem(n):
            return keep.enter_context(nc.semaphore(f"a1_{n}"))

        w = {k: sb("w" + k, [96, 2, NH * HD]) for k in "qkv"}
        wp = sb("wp", [128, NH // 2, E])
        rqv, rvv = sb("rqv", [128, NVG + 1, 64]), sb("rvv", [128, NVG + 1, 64])
        rqh, rvh = sb("rqh", [128, GRID + 1, 64]), sb("rvh", [128, GRID + 1, 64])
        bp = sb("bp", [P, E])
        qhi, qlo = sb("qhi", [128, HG, LP], F32R), sb("qlo", [128, HG, LP], F32R)
        khi, klo = sb("khi", [128, HG, L], F32R), sb("klo", [128, HG, L], F32R)
        work = sb("work", [128, HG, LW])
        pairs = sb("pairs", [128, NPR, LW])
        vaug = sb("vaug", [P, CH, HG, 128])
        hnT = sb("hnT", [96, 2, L])
        PT = sb("PT", [P, 2, LP])
        nb = PT[:].rearrange("p a l -> p (a l)")[:, 0:CH * E].rearrange("p (c e) -> p c e", e=E)
        rdb = sb("rdb", [128, NPR, LP])
        dcol = sb("dcol", [LP // 8, HG, 8])
        st = PT[:, 0, 0:6 * NT].rearrange("p (t s) -> p t s", s=6)
        mean = sb("mean", [P, NT])
        rstd = sb("rstd", [P, NT])
        mv_ = sb("mv", [P, NT, 2])
        nmx = sb("nmx", [P, 2, CH])
        mrow = sb("mrow", [CH, 2, P], F32R)
        psS = [ctx.enter_context(nc.psum_tensor(f"a1_S{i}", [128, 2, 512], F32)) for i in range(2)]
        psM = ctx.enter_context(nc.psum_tensor("a1_M", [128, 2, 512], F32))
        psO = ctx.enter_context(nc.psum_tensor("a1_O", [128, 2, 512], F32))

        s_w, s_oh, s_oz, s_og = sem("w"), sem("oh"), sem("oz"), sem("og")
        s_v, s_ln, s_sd = sem("v"), sem("ln"), sem("sd")
        names = ("nb", "xt", "xc", "pj", "pja", "pjd", "vp", "vc", "bg", "bga", "bgd", "sp", "m1", "mx", "mt", "mr",
                 "s", "e", "av", "o", "rg", "rga", "rgd", "pr", "g", "cp2", "rd", "nm")
        sg = {n: sem(n) for n in names}
        dens = nc.dram_tensor("a1_dens", (HG, LP), F32, kind="Internal").ap()
        rdens = nc.dram_tensor("a1_rdens", (HG, LP), F32, kind="Internal").ap()
        s_dr, s_dc, s_dw = sem("dr"), sem("dc"), sem("dw")
        s_md, s_db = [sem("md0"), sem("md1")], sem("db")
        PER = dict(nb=CH, xt=3, xc=3, pj=12, pja=12, pjd=12, vp=12, vc=12, bg=2 * NSET, bga=2 * NSET, bgd=2 * NSET,
                   sp=12, m1=72, mx=72, mt=12, mr=12, s=72, e=72, av=72, o=12, rg=2 * NSET, rga=2 * NV,
                   rgd=2 * (NHS + 1), pr=12, g=12, cp2=12, rd=2, nm=2)

        def waiter(eng, i):
            def wait(name, k):
                eng.wait_ge(sg[name], i * PER[name] + k)
            return wait

        block = ctx.enter_context(nc.Block())

        @block.sync
        def _(sp):
            for k in "qkv":
                sp.dma_start(w[k][:], A["a1_w" + k]).then_inc(s_w, 16)
            sp.dma_start(wp[:], A["a1_wp"]).then_inc(s_w, 16)
            for t, k in ((rqv, "rqv"), (rqh, "rqh"), (rvv, "rvv"), (rvh, "rvh")):
                sp.dma_start(t[:], A["a1_" + k]).then_inc(s_w, 16)
            sp.dma_start(bp[:], A["a1_bp"].partition_broadcast(P)).then_inc(s_w, 16)
            sp.dma_start(rdb[64:128, 0, 0:L], A["a1_oh"]).then_inc(s_oh, 16)
            for hh in range(HG):
                sp.dma_start(vaug[:, :, hh, 64:128], A["a1_ohT"]).then_inc(s_oh, 16)
            with sp.Fori(0, B) as i:
                wait = waiter(sp, i)
                for half in range(2):
                    def max_row(u):
                        wait("mr", u + 1)
                        for c in range(CH):
                            sp.dma_start(qhi[ONE:ONE + 1, u % HG, c * P:(c + 1) * P].bitcast(F32),
                                         mrow[c:c + 1, u % 2, :].bitcast(F32)).then_inc(s_md[u % 2], 16)

                    u0 = half * HG
                    max_row(u0)
                    max_row(u0 + 1)
                    for u in range(u0, u0 + HG):
                        if u + 2 < u0 + HG:
                            max_row(u + 2)
                        wait("o", u + 1)
                        sp.dma_start(dens[u % HG:u % HG + 1, :], work[ONE:ONE + 1, u % HG, 0:LP]).then_inc(s_dr, 16)
                    sp.wait_ge(s_dr, (2 * i + half + 1) * (16 * HG))
                    sp.dma_start(dcol[:], dens.rearrange("h (p s) -> p h s", s=8)).then_inc(s_dc, 16)
                    wait("rd", half + 1)
                    sp.dma_start(rdens.rearrange("h (p s) -> p h s", s=8), dcol[:]).then_inc(s_dw, 16)
                    sp.wait_ge(s_dw, (2 * i + half + 1) * 16)
                    for par in range(2):
                        sp.dma_start(rdb[64 * par:64 * par + 64, :, :],
                                     rdens[par::2, :].partition_broadcast(64)).then_inc(s_db, 16)

        @block.gpsimd
        def _(pool):
            pool.memset(klo[:].bitcast(F32), 0.0)
            pool.memset(qlo[:].bitcast(F32), 0.0)
            pool.memset(qhi[:].bitcast(F32), 0.0)
            pool.memset(work[:], 0.0).then_inc(s_oz, 1)
            pool.wait_ge(s_oz, 1)

        def group_sets():
            for m, (gs, n) in enumerate(V_SETS):
                yield m, "v", gs, n
            for m, (gs, n) in enumerate(H_SETS):
                yield NV + m, "h", gs, n

        def tokens(view, side, g, n):
            if side == "v":
                return view[:, :, 1 + GRID * g:1 + GRID * g + n]
            return view[:, :, 1 + g:1 + g + GRID * (n - 1) + 1:GRID]

        def grid_rows(view, gs, n):
            lo = 1 + GRID * gs[0]
            return view[:, :, lo:lo + n * len(gs)].rearrange("p h (g n) -> p h g n", n=n)

        def relative_rows(eng, wait, half, par, copy, done):
            for m, side, gs, n in group_sets():
                wait("bg", half * NSET + m + 1)
                rows, at = (NVG + 1, RV) if side == "v" else (GRID + 1, RH)
                k = len(gs)
                dst = work[at:at + rows, par::2, :]
                src = psO[32 * par:32 * par + rows, m % 2, 0:k * NPR * n]
                if side == "v":
                    last = copy(grid_rows(dst, gs, n), src.rearrange("p (g h n) -> p h g n", h=NPR, n=n))
                else:
                    last = copy(grid_columns(dst, gs, n), src.rearrange("p (g h n) -> p h n g", h=NPR, n=n))
                last.then_inc(sg[done], 1)
            m = NSET - 1
            wait("bg", half * NSET + m + 1)
            copy(work[RV:RV + NVG + 1, par::2, 0], psO[32 * par:32 * par + NVG + 1, m % 2, 0:NPR])
            copy(work[RH:RH + GRID + 1, par::2, 0], psO[32 * par:32 * par + GRID + 1, m % 2, NPR:2 * NPR]
                 ).then_inc(sg[done], 1)

        def grid_columns(view, gs, n):
            return view[:, :, 1:1 + GRID * n].rearrange("p h (n g) -> p h n g", g=GRID)[:, :, :, gs[0]:gs[0] + len(gs)]

        @block.tensor
        def _(pe):
            pe.wait_ge(s_w, 16 * 9)
            pe.wait_ge(s_oz, 1)
            pe.wait_ge(s_og, 1)
            pe.wait_ge(s_oh, 16 * (HG + 1))
            with pe.Fori(0, B) as i:
                wait = waiter(pe, i)
                for c in range(CH):
                    wait("nb", c + 1)
                    for k in range(2):
                        last = nc.tensor.transpose(
                            (psS[0][0:96, 0], psS[0][0:96, 1], psS[1][0:96, 0])[c // 2][
                                :, (2 * (c % 2) + k) * P:(2 * (c % 2) + k + 1) * P],
                            nb[:, c, 96 * k:96 * k + 96], ident[0:P, 0:P])
                    if c % 2:
                        last.then_inc(sg["xt"], 1)
                wait("xc", 3)
                for half in range(2):
                    u0 = half * HG
                    for m in range(2 * NPR):
                        pr, kind = divmod(m, 2)
                        if m >= 2:
                            wait("pja", half * 6 + m - 1)
                            wait("pjd", half * 6 + m - 1)
                        col = (half * NPR + pr) * 128
                        for a in range(2):
                            for k in range(2):
                                last = nc.tensor.matmul(psS[m % 2][:, a, 0:HALF], w["qk"[kind]][:, k, col:col + 128],
                                                        hnT[:, k, a * HALF:(a + 1) * HALF], start=(k == 0),
                                                        stop=(k == 1))
                        last.then_inc(sg["pj"], 1)
                    for c in range(CH):
                        if c >= 2:
                            wait("vc", half * CH + c - 1)
                        for k in range(2):
                            last = nc.tensor.matmul(psM[0:P, c % 2, 0:HG * HD], hnT[:, k, c * P:(c + 1) * P],
                                                    w["v"][:, k, half * HG * HD:(half + 1) * HG * HD],
                                                    start=(k == 0), stop=(k == 1))
                        last.then_inc(sg["vp"], 1)
                    wait("pja", half * 6 + 6)

                    def bank_free(m):
                        if m >= 2:
                            wait("bga", half * NSET + m - 1)
                            wait("bgd", half * NSET + m - 1)

                    for m, side, gs, n in group_sets():
                        bank_free(m)
                        for a, g in enumerate(gs):
                            last = nc.tensor.matmul(psO[0:64, m % 2, a * NPR * n:(a + 1) * NPR * n],
                                                    (rqv if side == "v" else rqh)[:, g + 1, :],
                                                    tokens(pairs, side, g, n), start=True, stop=True)
                        last.then_inc(sg["bg"], 1)
                    m = NSET - 1
                    bank_free(m)
                    nc.tensor.matmul(psO[0:64, m % 2, 0:NPR], rqv[:, 0, :], pairs[:, :, 0], start=True, stop=True)
                    nc.tensor.matmul(psO[0:64, m % 2, NPR:2 * NPR], rqh[:, 0, :], pairs[:, :, 0], start=True,
                                     stop=True).then_inc(sg["bg"], 1)

                    def row_scores(u, c):
                        if c == 0:
                            wait("sp", u + 1)
                            if u == u0:
                                wait("vc", (half + 1) * CH)
                                wait("pja", half * 6 + 6)
                        if u * CH + c > u0 * CH:
                            wait("mx", u * CH + c)
                        if c == 0 and u > u0:
                            wait("mr", u)
                        for a in range(2):
                            last = nc.tensor.matmul(psM[0:P, a, 0:376],
                                                    qhi[0:ONE, u % HG, c * P:(c + 1) * P],
                                                    khi[0:ONE, u % HG, a * 374:a * 374 + 376],
                                                    start=True, stop=True)
                        last.then_inc(sg["m1"], 1)

                    def max_to_row(u):
                        wait("mx", (u + 1) * CH)
                        nc.tensor.transpose(psM[0:CH, 0, 384:384 + P], nmx[:, u % 2, :], ident[0:P, 0:P]
                                            ).then_inc(sg["mt"], 1)

                    def scores(u, c):
                        wd = u * CH + c
                        if c == 0:
                            pe.wait_ge(s_md[u % 2], i * (96 * 6) + 96 * (u // 2 + 1))
                        if wd >= u0 * CH + 2:
                            wait("e", wd - 1)
                        at = slice(c * P, (c + 1) * P)
                        for x, (kk, qq) in enumerate(((khi, qhi), (khi, qlo), (klo, qhi))):
                            for a in range(2):
                                last = nc.tensor.matmul(psS[wd % 2][0:P, a, 0:HP], kk[:, u % HG, at],
                                                        qq[:, u % HG, a * HP:(a + 1) * HP], start=(x == 0),
                                                        stop=(x == 2))
                        last.then_inc(sg["s"], 1)

                    def values(u, c):
                        wd = u * CH + c
                        wait("e", wd + 1)
                        if c == 0 and u > u0:
                            wait("o", u)
                        for a in range(2):
                            last = nc.tensor.matmul(psO[:, a, 0:HP], vaug[:, c, u % HG, :],
                                                    PT[:, wd % 2, a * HP:(a + 1) * HP], start=(c == 0),
                                                    stop=(c == CH - 1))
                        last.then_inc(sg["av"], 1)

                    for u in (u0, u0 + 1):
                        for c in range(CH):
                            row_scores(u, c)
                        max_to_row(u)
                    wait("bga", (half + 1) * NSET)
                    wait("bgd", (half + 1) * NSET)
                    scores(u0, 0)
                    for u in range(u0, u0 + HG):
                        for c in range(CH):
                            if c + 1 < CH:
                                scores(u, c + 1)
                            elif u + 1 < u0 + HG:
                                scores(u + 1, 0)
                            if u + 2 < u0 + HG:
                                row_scores(u + 2, c)
                            values(u, c)
                        if u + 2 < u0 + HG:
                            max_to_row(u + 2)
                    wait("o", u0 + HG)
                    wait("e", (half + 1) * 36)

                    def out_bank(m):
                        return psS[(m // 2) % 2][:, m % 2, :]

                    def bank_done(m):
                        if m >= 4:
                            k = m - 4
                            if k < NV:
                                wait("rga", half * NV + k + 1)
                            else:
                                wait("rgd", half * (NHS + 1) + k - NV + 1)

                    for m, side, gs, n in group_sets():
                        bank_done(m)
                        for a, g in enumerate(gs):
                            for par in range(2):
                                last = nc.tensor.matmul(
                                    out_bank(m)[64 * par:64 * par + 64, a * NPR * n:(a + 1) * NPR * n],
                                    (rvv if side == "v" else rvh)[:, g + 1, :],
                                    tokens(work[:, par::2, :], side, g, n), start=True, stop=True)
                        last.then_inc(sg["rg"], 1)
                    m = NSET - 1
                    bank_done(m)
                    for par in range(2):
                        for x, table in enumerate((rvv, rvh)):
                            last = nc.tensor.matmul(out_bank(m)[64 * par:64 * par + 64, 0:NPR], table[:, 0, :],
                                                    work[:, par::2, 0], start=(x == 0), stop=(x == 1))
                    last.then_inc(sg["rg"], 1)
                    wait("nm", half + 1)
                    for c in range(CH):
                        if c >= 2:
                            wait("g", half * CH + c - 1)
                        for pr in range(NPR):
                            last = nc.tensor.matmul(psM[0:P, c % 2, 0:E], pairs[:, pr, c * P:(c + 1) * P],
                                                    wp[:, half * NPR + pr, :], start=(pr == 0), stop=(pr == NPR - 1))
                        last.then_inc(sg["pr"], 1)
                    if half == 0:
                        wait("g", CH)

        @block.scalar
        def _(act):
            act.wait_ge(s_ln, 1)
            nc.scalar.activation(rstd[:], rstd[:], ACT.Sqrt).then_inc(s_sd, 1)
            act.wait_ge(s_oh, 16 * (HG + 1))
            for hh in range(HG):
                last = nc.scalar.activation(khi[64:128, hh, :], rdb[64:128, 0, 0:L], ACT.Copy)
            last.then_inc(s_og, 1)
            with act.Fori(0, B) as i:
                wait = waiter(act, i)
                for g in range(3):
                    wait("xt", g + 1)
                    nc.scalar.activation(
                        hnT[:, :, 2 * g * P:2 * (g + 1) * P].rearrange("d k (c p) -> d c k p", p=P),
                        (psS[0][0:96, 0], psS[0][0:96, 1], psS[1][0:96, 0])[g][:, 0:4 * P].rearrange(
                            "d (c k p) -> d c k p", c=2, k=2), ACT.Copy).then_inc(sg["xc"], 1)
                for half in range(2):
                    u0 = half * HG
                    for m in range(2 * NPR):
                        pr, kind = divmod(m, 2)
                        wait("pj", half * 6 + m + 1)
                        if kind == 0:
                            last = nc.scalar.activation(pairs[:, pr, 0:L].rearrange("p (a l) -> p a l", a=2),
                                                        psS[m % 2][:, :, 0:HALF], ACT.Copy)
                        else:
                            for par in range(2):
                                last = nc.scalar.activation(
                                    khi[0:64, 2 * pr + par, :].rearrange("p (a l) -> p a l", a=2),
                                    psS[m % 2][64 * par:64 * par + 64, :, 0:HALF], ACT.Copy)
                        last.then_inc(sg["pja"], 1)
                    for c in range(CH):
                        wait("vp", half * CH + c + 1)
                        nc.scalar.activation(vaug[:, c, :, 0:64],
                                             psM[0:P, c % 2, 0:HG * HD].rearrange("p (h d) -> p h d", d=HD),
                                             ACT.Copy).then_inc(sg["vc"], 1)
                    wait("pjd", half * 6 + 6)
                    relative_rows(act, wait, half, 0, lambda o, x: nc.scalar.activation(o, x, ACT.Copy), "bga")
                    for u in range(u0, u0 + HG):
                        for c in range(CH):
                            wd = u * CH + c
                            wait("s", wd + 1)
                            if wd >= u0 * CH + 2:
                                wait("av", wd - 1)
                            nc.scalar.activation(PT[:, wd % 2, :].rearrange("p (a l) -> p a l", a=2),
                                                 psS[wd % 2][0:P, :, 0:HP], ACT.Exp, scale=SCALE
                                                 ).then_inc(sg["e"], 1)
                    for m, (gs, n) in enumerate(V_SETS):
                        wait("rg", half * NSET + m + 1)
                        k = len(gs)
                        nc.scalar.activation(
                            grid_rows(pairs, gs, n),
                            psS[(m // 2) % 2][:, m % 2, 0:k * NPR * n].rearrange("p (g h n) -> p h g n", h=NPR, n=n),
                            ACT.Copy).then_inc(sg["rga"], 1)

        @block.vector
        def _(dve):
            v = nc.vector
            link = Chain(dve, s_v)
            for t in range(NT):
                v.bn_stats(st[:, t, :], h[:, t, :]).then_inc(s_v, 1)
            link.n += NT
            dve.wait_ge(s_v, link.n)
            for t in range(NT):
                v.bn_aggr(mv_[:, t, :], st[:, t, :]).then_inc(s_v, 1)
            link.n += NT
            dve.wait_ge(s_v, link.n)
            link(v.tensor_copy(mean[:], mv_[:, :, 0]))
            v.tensor_scalar(rstd[:], mv_[:, :, 1], EPS, None, ALU.add).then_inc(s_ln, 1)
            dve.wait_ge(s_sd, 1)
            link(v.reciprocal(rstd[:], rstd[:]))
            dve.wait_ge(s_w, 16 * 9)
            dve.wait_ge(s_og, 1)
            dve.wait_ge(s_oz, 1)
            with dve.Fori(0, B) as i:
                wait = waiter(dve, i)
                for c in range(CH):
                    t = i * CH + c
                    v.tensor_scalar(nb[:, c, :], h[:, bass.ds(t, 1), :].rearrange("p o e -> p (o e)"),
                                    mean[:, bass.ds(t, 1)], rstd[:, bass.ds(t, 1)], ALU.subtract,
                                    ALU.mult).then_inc(sg["nb"], 1)
                wait("nb", CH)
                hb = h[:, bass.ds(i * CH, CH), :]
                v.tensor_tensor(hb, hb, bp[:].unsqueeze(1).broadcast_to([P, CH, E]), ALU.add)
                for half in range(2):
                    u0 = half * HG
                    for m in range(2 * NPR):
                        pr, kind = divmod(m, 2)
                        wait("pja", half * 6 + m + 1)
                        for par in range(2):
                            if kind == 0:
                                last = v.tensor_copy(work[0:64, 2 * pr + par, 0:L], pairs[64 * par:64 * par + 64, pr, 0:L])
                            else:
                                last = v.tensor_tensor(
                                    klo[0:64, 2 * pr + par, :].rearrange("p (a l) -> p a l", a=2),
                                    psS[m % 2][64 * par:64 * par + 64, :, 0:HALF],
                                    khi[0:64, 2 * pr + par, :].bitcast(F32).rearrange("p (a l) -> p a l", a=2),
                                    ALU.subtract)
                        last.then_inc(sg["pjd"], 1)
                    relative_rows(dve, wait, half, 1, lambda o, x: v.tensor_copy(o, x), "bgd")
                    wait("bga", (half + 1) * NSET)
                    wait("bgd", (half + 1) * NSET)
                    wait("pjd", half * 6 + 6)
                    for hh in range(HG):
                        v.tensor_copy(qhi[0:ONE, hh, 0:L], work[0:ONE, hh, 0:L]).then_inc(sg["cp2"], 1)
                        wait("cp2", u0 + hh + 1)
                        v.tensor_tensor(qlo[0:ONE, hh, 0:L], work[0:ONE, hh, 0:L], qhi[0:ONE, hh, 0:L].bitcast(F32),
                                        ALU.subtract).then_inc(sg["sp"], 1)

                    def maxima(u, c):
                        wait("m1", u * CH + c + 1)
                        v.tensor_reduce(nmx[:, u % 2, c:c + 1], psM[0:P, :, 0:376], AX.XY, ALU.max,
                                        negate=True).then_inc(sg["mx"], 1)

                    def to_row(u):
                        wait("mt", u + 1)
                        v.tensor_copy(mrow[:, u % 2, :], psM[0:CH, 0, 384:384 + P]).then_inc(sg["mr"], 1)

                    for u in (u0, u0 + 1):
                        for c in range(CH):
                            maxima(u, c)
                        to_row(u)
                    for u in range(u0, u0 + HG):
                        for c in range(CH):
                            if u + 2 < u0 + HG:
                                if c == 0:
                                    dve.wait_ge(s_md[u % 2], i * (96 * 6) + 96 * (u // 2 + 1))
                                maxima(u + 2, c)
                        wait("av", (u + 1) * CH)
                        v.tensor_copy(work[:, u % HG, 0:LP].rearrange("p (a l) -> p a l", a=2), psO[:, :, 0:HP]
                                      ).then_inc(sg["o"], 1)
                        if u + 2 < u0 + HG:
                            to_row(u + 2)
                    dve.wait_ge(s_dc, (2 * i + half + 1) * 16)
                    v.reciprocal(dcol[:], dcol[:]).then_inc(sg["rd"], 1)
                    wait("rga", (half + 1) * NV)
                    for m, (gs, n) in enumerate(H_SETS):
                        mm = NV + m
                        wait("rg", half * NSET + mm + 1)
                        k = len(gs)
                        dst = grid_columns(pairs, gs, n)
                        v.tensor_tensor(dst, dst, psS[(mm // 2) % 2][:, mm % 2, 0:k * NPR * n].rearrange(
                            "p (g h n) -> p h n g", h=NPR, n=n), ALU.add).then_inc(sg["rgd"], 1)
                    mm = NSET - 1
                    wait("rg", half * NSET + mm + 1)
                    v.tensor_copy(pairs[:, :, 0], psS[(mm // 2) % 2][:, mm % 2, 0:NPR]).then_inc(sg["rgd"], 1)
                    wait("rgd", (half + 1) * (NHS + 1))
                    dve.wait_ge(s_db, (2 * i + half + 1) * 32)
                    v.tensor_tensor(pairs[:, :, 0:L], pairs[:, :, 0:L], rdb[:, :, 0:L], ALU.mult).then_inc(sg["nm"], 1)
                    for c in range(CH):
                        wait("pr", half * CH + c + 1)
                        if half == 1:
                            wait("g", c + 1)
                        hc = h[:, bass.ds(i * CH + c, 1), :].rearrange("p o e -> p (o e)")
                        v.tensor_tensor(hc, hc, psM[0:P, c % 2, 0:E], ALU.add).then_inc(sg["g"], 1)
                    wait("g", (half + 1) * CH)


def host_inputs(i):
    sel, xy, merge, one9 = moment_constants()
    t = np.ascontiguousarray
    f = {k: np.asarray(v) for k, v in i.items()}
    return {
        "x": f["x"],
        "wt": conv_weights([f[f"L0_tok_w_t{k}"] for k in KS], [f[f"L0_tok_b_t{k}"] for k in KS]),
        "wc": conv_weights([f[f"L0_tok_w_c{k}"] for k in KS], [f[f"L0_tok_b_c{k}"] for k in KS]),
        "Wq0T": t(f["L0_attn_Wq"].T), "Wk0T": t(f["L0_attn_Wk"].T), "Wv0T": t(f["L0_attn_Wv"].T),
        "Wo0T": t(f["L0_attn_Wo"].T),
        "sel": sel, "selxy": xy, "merge": merge, "one9": one9,
        **moe_inputs(f),
        **relative_inputs(f),
    }


def build(nc, A, out):
    ctx = ExitStack()
    with ctx:
        h = ctx.enter_context(nc.sbuf_tensor("h", [P, NT, E], F32))
        ident = ctx.enter_context(nc.sbuf_tensor("ident", [128, 128], F32))
        for run in (lambda keep: token_mixer_and_attention(nc, keep, A, h, ident),
                    lambda keep: moe(nc, keep, A, h, ident, MOE0, None),
                    lambda keep: window_attention(nc, keep, A, h, ident)):
            stage = Stage(nc)
            run(stage)
            stage.close()
        moe(nc, ctx, A, h, ident, MOE1, out)


def kernel(**inputs):
    import concourse.bacc as bacc
    from concourse.bass_utils import run_bass_kernel_spmd

    nc = bacc.Bacc("TRN2", target_bir_lowering=False, num_devices=1)
    arrays, A = {}, {}
    for name, a in host_inputs(inputs).items():
        a = np.ascontiguousarray(a)
        arrays[f"in_{name}"] = a
        A[name] = nc.dram_tensor(f"in_{name}", a.shape, mybir.dt.from_np(a.dtype), kind="ExternalInput").ap()
    out = nc.dram_tensor("out_0", (B, L, E), F32, kind="ExternalOutput").ap()
    build(nc, A, out)
    r = run_bass_kernel_spmd(nc, [arrays], core_ids=[0])
    return r.results[0]["out_0"]
```

```python
import itertools

import numpy as np

import concourse.bass as bass
from concourse import mybir
from contextlib import ExitStack

F32 = mybir.dt.float32
F32R = mybir.dt.float32r
I32 = mybir.dt.int32
U32 = mybir.dt.uint32
ALU = mybir.AluOpType
ACT = mybir.ActivationFunctionType
AX = mybir.AxisListType

B, D, L = 4, 64, 750
KS = (3, 5, 7)
E = len(KS) * D
CH, P = 6, 125
NT = B * CH
H0, FEAT = 12, 16
EPS = 1e-5
HALF = L // 2

MONO = [()] + [(a,) for a in range(3)] + list(itertools.combinations_with_replacement(range(3), 2)) \
    + list(itertools.combinations_with_replacement(range(3), 3))
MI = {m: i for i, m in enumerate(MONO)}
NM = len(MONO)
PAIRS = [m for m in MONO if len(m) == 2]
FEATS = [(a, m) for a in MONO if len(a) == 2 for m in MONO if len(m) == 3] \
    + [(a, m) for a in MONO if len(a) == 1 for m in MONO if len(m) == 2] \
    + [((), m) for m in MONO if len(m) == 1] \
    + [(a, m) for a in MONO if len(a) == 2 for m in MONO if len(m) == 2] \
    + [(a, m) for a in MONO if len(a) == 1 for m in MONO if len(m) == 1] + [((), ())]
FI = {f: i for i, f in enumerate(FEATS)}
NF = len(FEATS)
ROWS = [(a, b, c, d) for a in range(3) for b in range(3) for c in range(3) for d in range(3)] \
    + [(a, b) for a in range(3) for b in range(3)] + [()]
NR = len(ROWS)


def moment_constants():
    sel = np.zeros((128, B, 2, NF), np.float32)
    for b in range(B):
        for f, (a, m) in enumerate(FEATS):
            sel[32 * b + MI[a], b, 0, f] = 1.0
            sel[32 * b + MI[m], b, 1, f] = 1.0
    xy = np.zeros((128, B, 2, NR), np.float32)
    merge = np.zeros((NR, 4, NF), np.float32)
    for r, row in enumerate(ROWS):
        ab = [row[0:2], row[2:4]]
        for side in range(2):
            j = 3 * ab[side][0] + ab[side][1] if ab[side] else 9
            for b in range(B):
                xy[32 * b + j, b, side, r] = 1.0
        left = tuple(sorted(row[0::2]))
        right = row[1::2]
        w = 0.5 if len(row) == 4 else 1.0
        for i in range(3):
            merge[r, i, FI[(left, tuple(sorted(right + (i,))))]] += w
        merge[r, 3, FI[(left, tuple(sorted(right)))]] += w
    one9 = np.zeros((128, 1), np.float32)
    one9[9::32] = 1.0
    return sel, xy, merge, one9


def conv_weights(w, b):
    out = np.zeros((17, 7, 4, 3), w[0].dtype)
    for k, width in enumerate(KS):
        at = 3 - width // 2
        for i in range(B):
            out[4 * i:4 * i + 4, at:at + width, i, k] = w[k][0]
        out[16, 3, :, k] = b[k][0]
    return out.reshape(17, 7, 12)


class Chain:

    def __init__(self, eng, sem):
        self.eng, self.sem, self.n = eng, sem, 0

    def __call__(self, ins):
        self.n += 1
        ins.then_inc(self.sem, 1)
        self.eng.wait_ge(self.sem, self.n)


class Stage:

    def __init__(self, nc):
        self.nc, self.stack, self.all = nc, ExitStack(), []

    def enter_context(self, semaphore):
        self.all.append(self.stack.enter_context(semaphore))
        return self.all[-1]

    def close(self):
        with self.nc.Block() as block:
            @block.gpsimd
            def _(pool):
                for s in self.all:
                    pool.sem_clear(s)
        self.stack.close()


def token_mixer_and_attention(nc, keep, A, h, ident):
    ctx = ExitStack()
    with ctx:
        def sb(name, shape, dt=F32):
            return ctx.enter_context(nc.sbuf_tensor(name, shape, dt))

        def sem(name):
            return keep.enter_context(nc.semaphore(name))

        xd = sb("xd", [D, B, L])
        xT = sb("xT", [P, CH, B, D])
        xc = sb("xc", [P, CH, B, D])
        wt = sb("wt", [17, 7, 12])
        wc = sb("wc", [17, 7, 12])
        wqk = sb("wqk", [D, 2, 3, E])
        wv = sb("wv", [D, 3, E])
        wo = sb("wo", [96, 2, E])
        sel = sb("sel", [128, B, 2, NF])
        selxy = sb("selxy", [128, B, 2, NR])
        merge = sb("merge", [NR, 4, NF])
        one9 = sb("one9", [128, 1])
        statT = sb("statT", [P, CH, 17])
        statC = sb("statC", [D, 17])
        smean = sb("smean", [D, B])
        nmean = sb("nmean", [D, B])
        ssq = sb("ssq", [D, B])
        mtok = sb("mtok", [P, NT])
        sqd = sb("sqd", [D, L])
        poolT = sb("poolT", [17, L + 6])
        poolC = sb("poolC", [17, D + 6])
        wgtT = sb("wgtT", [P, CH, 12])
        wgtC = sb("wgtC", [D, 12])
        ones64 = sb("ones64", [D, 128])
        rt = sb("rt", [D, 12])
        rtc = sb("rtc", [D, 2, 12])
        bm = sb("bm", [128, 2, 12])
        v0 = sb("v0", [128, B])
        rc = sb("rc", [P, B, CH, 3])
        hm = sb("hm", [P, B, CH, 3])
        ak = sb("ak", [P, B, CH, 3])
        aq = sb("aq", [P, B, CH, 3])
        m1 = sb("m1", [P, B, CH])
        rs = sb("rs", [P, B, CH])
        phi = sb("phi", [P, CH, B, 32])
        phiT = sb("phiT", [128, L])
        ones = sb("ones", [128, L])
        S = sb("S", [128, L])
        basis = sb("basis", [D, 3, B, 3])
        qku = sb("qku", [D, 2, 3, B, 32])
        vu = sb("vu", [D, 3, B, 3, NR])
        qs = sb("qs", [128, E])
        qk = sb("qk", [128, E])
        Mx = sb("Mx", [128, H0])
        xs = sb("xs", [NR, H0])
        T2 = sb("T2", [NR, B, H0])
        T3 = sb("T3", [NR, 3, E])
        C = sb("C", [NF, B, E + H0])
        G1 = sb("G1", [NF, L])
        Ft = sb("Ft", [NF, B, L])
        diag = sb("diag", [D, 12, D])
        u0row = sb("u0row", [P, B, E])
        rden = sb("rden", [P, 2, H0])
        yn = sb("yn", [P, 2, E])
        yT = sb("yT", [96, 2, 2, P])
        ps = [ctx.enter_context(nc.psum_tensor(f"psA{i}", [128, 512], F32)) for i in range(8)]

        s_x, s_w, s_cst = sem("s_x"), sem("s_w"), sem("s_cst")
        s_id = sem("s_id")
        s_a, s_v, s_g = sem("s_a"), sem("s_v"), sem("s_g")
        s_xt, s_xtc = sem("s_xt"), sem("s_xtc")
        s_mean, s_var = sem("s_mean"), sem("s_var")
        s_std, s_sd = sem("s_std"), sem("s_sd")
        s_stat, s_statT, s_pool = sem("s_stat"), sem("s_statT"), sem("s_pool")
        s_conv, s_wgt, s_rows, s_rowc = sem("s_conv"), sem("s_wgt"), sem("s_rows"), sem("s_rowc")
        s_bm, s_usq, s_v0, s_phi, s_phiT, s_phic, s_S = (sem(n) for n in (
            "s_bm", "s_usq", "s_v0", "s_phi", "s_phiT", "s_phic", "s_S"))
        s_basis, s_qk, s_qc, s_Mx, s_xy, s_xyc, s_T2 = (sem(n) for n in (
            "s_basis", "s_qk", "s_qc", "s_Mx", "s_xy", "s_xyc", "s_T2"))
        s_vps, s_T3, s_C, s_Cc = sem("s_vps"), sem("s_T3"), sem("s_C"), sem("s_Cc")
        s_G, s_Gc, s_F = sem("s_G"), sem("s_Gc"), sem("s_F")
        s_dg, s_u0, s_u0c = sem("s_dg"), sem("s_u0"), sem("s_u0c")
        s_y, s_yn, s_yt, s_ytc, s_o, s_h = (sem(n) for n in ("s_y", "s_yn", "s_yt", "s_ytc", "s_o", "s_h"))
        block = ctx.enter_context(nc.Block())

        @block.sync
        def _(sp):
            for b in range(B):
                sp.dma_start(xd[:, b, :], A["x"][b]).then_inc(s_x, 16)
            sp.dma_start(wt[:], A["wt"]).then_inc(s_w, 16)
            sp.dma_start(wc[:], A["wc"]).then_inc(s_w, 16)
            sp.dma_start(sel[:], A["sel"]).then_inc(s_w, 16)
            sp.dma_start(selxy[:], A["selxy"]).then_inc(s_w, 16)
            sp.dma_start(merge[:], A["merge"]).then_inc(s_w, 16)
            sp.dma_start(one9[:], A["one9"]).then_inc(s_w, 16)
            sp.dma_start(wqk[:, 0], A["Wq0T"].rearrange("(k d) f -> d k f", d=D)).then_inc(s_w, 16)
            sp.dma_start(wqk[:, 1], A["Wk0T"].rearrange("(k d) f -> d k f", d=D)).then_inc(s_w, 16)
            sp.dma_start(wv[:], A["Wv0T"].rearrange("(k d) f -> d k f", d=D)).then_inc(s_w, 16)
            sp.dma_start(wo[:], A["Wo0T"].rearrange("(k f) e -> f k e", f=96)).then_inc(s_w, 16)
            sp.wait_ge(s_x, 64)
            sp.wait_ge(s_w, 160)

        @block.gpsimd
        def _(pool):
            pool.memset(ident[:], 0.0).then_inc(s_g, 1)
            pool.wait_ge(s_g, 1)
            pool.affine_select(out=ident[:], in_=ident[:], compare_op=ALU.not_equal, fill=1.0, base=0,
                               pattern=[[-1, 128]], channel_multiplier=1).then_inc(s_id, 1)
            pool.memset(statT[:], 1.0)
            pool.memset(statC[:], 1.0)
            pool.memset(poolT[:], 0.0)
            pool.memset(poolC[:], 0.0)
            pool.memset(ones64[:], 1.0 / D)
            pool.memset(ones[:], 1.0)
            pool.memset(phi[:], 0.0)
            pool.memset(qku[:], 0.0)
            pool.memset(basis[:], 0.0).then_inc(s_g, 1)
            pool.wait_ge(s_g, 2)
            pool.memset(phi[:, :, :, 0:1], 1.0)
            pool.memset(basis[:, 0, :, 1:2], 1.0)
            pool.memset(basis[:, 1, :, 2:3], 1.0)
            pool.memset(basis[:, 2, :, 1:3], -1.0).then_inc(s_cst, 1)

        @block.tensor
        def _(pe):
            pe.wait_ge(s_x, 16 * B)
            pe.wait_ge(s_id, 1)
            for c in range(CH):
                for b in range(B):
                    g = c * B + b
                    last = nc.tensor.transpose(ps[g // 8][0:P, (g % 8) * D:(g % 8 + 1) * D],
                                               xd[:, b, c * P:(c + 1) * P], ident[0:D, 0:D])
                    if g % 8 == 7:
                        last.then_inc(s_xt, 1)
            pe.wait_ge(s_stat, 2)
            for c in range(CH):
                nc.tensor.transpose(ps[3 + c // 4][0:17, (c % 4) * P:(c % 4 + 1) * P], statT[:, c, :],
                                    ident[0:P, 0:P])
            nc.tensor.transpose(ps[5][0:17, 0:D], statC[:], ident[0:D, 0:D]).then_inc(s_statT, 1)
            pe.wait_ge(s_w, 160)
            pe.wait_ge(s_pool, 1)
            for c in range(CH):
                for t in range(7):
                    nc.tensor.matmul(ps[6][0:P, 12 * c:12 * c + 12], poolT[:, c * P + t:c * P + t + P], wt[:, t, :],
                                     start=(t == 0), stop=(t == 6))
            for t in range(7):
                last = nc.tensor.matmul(ps[7][0:D, 0:12], poolC[:, t:t + D], wc[:, t, :],
                                        start=(t == 0), stop=(t == 6))
            last.then_inc(s_conv, 1)
            pe.wait_ge(s_wgt, 1)
            for b in range(B):
                for c in range(CH):
                    nc.tensor.matmul(ps[0][0:D, 3 * b:3 * b + 3], xT[:, c, b, :], wgtT[:, c, 3 * b:3 * b + 3],
                                     start=(c == 0), stop=(c == CH - 1))
            for b in range(B):
                for c in range(CH):
                    at = 3 * (b * CH + c)
                    last = nc.tensor.matmul(ps[1][0:P, at:at + 3], xd[:, b, c * P:(c + 1) * P],
                                            wgtC[:, 3 * b:3 * b + 3], start=True, stop=True)
            last.then_inc(s_rows, 1)
            pe.wait_ge(s_rowc, 1)
            pe.wait_ge(s_cst, 1)
            nc.tensor.matmul(ps[2][:, 0:12], ones64[:], rt[:], start=True, stop=True).then_inc(s_bm, 1)
            pe.wait_ge(s_usq, 1)
            nc.tensor.matmul(ps[3][:, 0:12], ones64[:], rtc[:, 1, :], start=True, stop=True).then_inc(s_v0, 1)
            pe.wait_ge(s_basis, 1)
            for j in range(2):
                for k in range(3):
                    last = nc.tensor.matmul(ps[4 + j][:, 0:E], qku[:, j, k, :, :].rearrange("d b r -> d (b r)"),
                                            wqk[:, j, k, :], start=(k == 0), stop=(k == 2))
            last.then_inc(s_qk, 1)
            for b in range(B):
                for k in range(3):
                    bank = 6 + b // 2
                    last = nc.tensor.matmul(ps[bank][0:P, (b % 2) * E + k * D:(b % 2) * E + (k + 1) * D],
                                            ones[0:D, 0:P], diag[:, 3 * b + k, :], start=True, stop=True)
            last.then_inc(s_u0, 1)
            pe.wait_ge(s_phi, 1)
            for c in range(CH):
                last = nc.tensor.transpose(ps[c // 4][:, (c % 4) * P:(c % 4 + 1) * P],
                                           phi[:, c, :, :].rearrange("p b s -> p (b s)"), ident[0:P, 0:P])
            last.then_inc(s_phiT, 1)
            pe.wait_ge(s_Mx, 1)
            for b in range(B):
                for side in range(2):
                    last = nc.tensor.matmul(ps[4 + side][0:NR, b * H0:(b + 1) * H0], selxy[:, b, side, :],
                                            Mx[:], start=True, stop=True)
            last.then_inc(s_xy, 1)
            for b in range(B):
                if b >= 1:
                    pe.wait_ge(s_T3, b)
                else:
                    pe.wait_ge(s_phic, 1)
                    pe.wait_ge(s_u0c, 1)
                for i in range(3):
                    bank = (2, 3, 6)[i]
                    for k in range(3):
                        last = nc.tensor.matmul(ps[bank][0:NR, 0:E], vu[:, k, b, i, :], wv[:, k, :],
                                                start=(k == 0), stop=(k == 2))
                last.then_inc(s_vps, 1)
                pe.wait_ge(s_T3, b + 1)
                if b >= 1:
                    pe.wait_ge(s_Cc, b)
                for i in range(3):
                    nc.tensor.matmul(ps[7][0:NF, 0:E], merge[:, i, :], T3[:, i, :], start=(i == 0), stop=(i == 2))
                nc.tensor.matmul(ps[7][0:NF, E:E + H0], merge[:, 3, :], T2[:, b, :], start=True,
                                 stop=True).then_inc(s_C, 1)
            pe.wait_ge(s_S, 1)
            for b in range(B):
                if b >= 1:
                    pe.wait_ge(s_Gc, b)
                    pe.wait_ge(s_F, b)
                for f in range(2):
                    for n in range(2):
                        last = nc.tensor.matmul(ps[2 * f + n][0:NF, 0:HALF], sel[:, b, f, :],
                                                (phiT if f == 0 else S)[:, n * HALF:(n + 1) * HALF],
                                                start=True, stop=True)
                    if f == 1:
                        last.then_inc(s_G, 1)
            pe.wait_ge(s_Cc, B)
            pe.wait_ge(s_F, B)

            def project(t):
                pe.wait_ge(s_yn, t + 1)
                if t >= 2:
                    pe.wait_ge(s_ytc, t - 1)
                for k in range(2):
                    last = nc.tensor.transpose(ps[6 + t % 2][0:96, k * P:(k + 1) * P],
                                               yn[:, t % 2, 96 * k:96 * k + 96], ident[0:P, 0:P])
                last.then_inc(s_yt, 1)
                pe.wait_ge(s_ytc, t + 1)
                if t >= 2:
                    pe.wait_ge(s_h, t - 1)
                for k in range(2):
                    last = nc.tensor.matmul(ps[4 + t % 2][0:P, 0:E], yT[:, t % 2, k, :], wo[:, k, :],
                                            start=(k == 0), stop=(k == 1))
                last.then_inc(s_o, 1)

            for t in range(NT):
                b, c = divmod(t, CH)
                if t >= 2:
                    pe.wait_ge(s_yn, t - 1)
                nc.tensor.matmul(ps[t % 2][0:P, 0:E + H0], Ft[:, b, c * P:(c + 1) * P], C[:, b, :],
                                 start=True, stop=True).then_inc(s_y, 1)
                if t >= 1:
                    project(t - 1)
            project(NT - 1)

        @block.scalar
        def _(act):
            link = Chain(act, s_a)
            for g in range(3):
                act.wait_ge(s_xt, g + 1)
                nc.scalar.activation(xT[:].rearrange("p c b d -> p (c b d)")[:, g * 512:(g + 1) * 512],
                                     ps[g][0:P, :], ACT.Copy).then_inc(s_xtc, 1)
            act.wait_ge(s_mean, 1)
            for b in range(B):
                link(nc.scalar.activation(sqd[:], xd[:, b, :], ACT.Square, bias=nmean[:, b:b + 1],
                                          accum_out=ssq[:, b:b + 1]))
            act.wait_ge(s_cst, 1)
            nc.scalar.activation(statC[:, 1:16:4], ssq[:], ACT.Sqrt, scale=1.0 / (L - 1)).then_inc(s_stat, 1)
            act.wait_ge(s_var, 1)
            nc.scalar.activation(statT[:, :, 1:16:4], m1[:].rearrange("p b c -> p (b c)").rearrange(
                "p (c b) -> p c b", b=B), ACT.Sqrt, scale=1.0 / (D - 1)).then_inc(s_std, 1)
            act.wait_ge(s_statT, 1)
            nc.scalar.activation(poolT[:, 3:3 + 4 * P], ps[3][0:17, 0:4 * P], ACT.Copy)
            nc.scalar.activation(poolT[:, 3 + 4 * P:3 + L], ps[4][0:17, 0:2 * P], ACT.Copy)
            nc.scalar.activation(poolC[:, 3:3 + D], ps[5][0:17, 0:D], ACT.Copy).then_inc(s_pool, 1)
            act.wait_ge(s_conv, 1)
            nc.scalar.activation(wgtT[:].rearrange("p c k -> p (c k)"), ps[6][0:P, 0:72], ACT.Relu)
            nc.scalar.activation(wgtC[:], ps[7][0:D, 0:12], ACT.Relu).then_inc(s_wgt, 1)
            act.wait_ge(s_var, 2)
            nc.scalar.activation(rs[:], rs[:], ACT.Sqrt).then_inc(s_std, 1)
            act.wait_ge(s_phiT, 1)
            nc.scalar.activation(phiT[:, 0:4 * P], ps[0][:, 0:4 * P], ACT.Copy)
            nc.scalar.activation(phiT[:, 4 * P:L], ps[1][:, 0:2 * P], ACT.Copy).then_inc(s_phic, 1)
            act.wait_ge(s_u0, 1)
            nc.scalar.activation(u0row[:, 0:2, :].rearrange("p b e -> p (b e)"), ps[6][0:P, 0:2 * E], ACT.Copy,
                                 scale=float(D) / D)
            nc.scalar.activation(u0row[:, 2:4, :].rearrange("p b e -> p (b e)"), ps[7][0:P, 0:2 * E],
                                 ACT.Copy).then_inc(s_u0c, 1)
            for b in range(B):
                act.wait_ge(s_C, b + 1)
                nc.scalar.activation(C[:, b, :], ps[7][0:NF, 0:E + H0], ACT.Copy).then_inc(s_Cc, 1)
            for b in range(B):
                act.wait_ge(s_G, b + 1)
                if b >= 1:
                    act.wait_ge(s_F, b)
                for n in range(2):
                    last = nc.scalar.activation(G1[:, n * HALF:(n + 1) * HALF], ps[n][0:NF, 0:HALF], ACT.Copy)
                last.then_inc(s_Gc, 1)
            for t in range(NT):
                act.wait_ge(s_yt, t + 1)
                if t >= 2:
                    act.wait_ge(s_o, t - 1)
                nc.scalar.activation(yT[:, t % 2, :, :].rearrange("f k p -> f (k p)"), ps[6 + t % 2][0:96, 0:2 * P],
                                     ACT.Copy).then_inc(s_ytc, 1)

        @block.vector
        def _(dve):
            v = nc.vector
            link = Chain(dve, s_v)
            dve.wait_ge(s_x, 16 * B)
            dve.wait_ge(s_cst, 1)
            link(v.tensor_reduce(smean[:], xd[:], AX.X, ALU.add))
            v.tensor_scalar(nmean[:], smean[:], -1.0 / L, None, ALU.mult).then_inc(s_mean, 1)
            v.tensor_scalar(statC[:, 0:16:4], smean[:], 1.0 / L, None, ALU.mult)
            v.tensor_reduce(statC[:, 2:16:4], xd[:], AX.X, ALU.max)
            link(v.tensor_reduce(statC[:, 3:16:4], xd[:], AX.X, ALU.min))
            dve.wait_ge(s_xtc, 3)
            xg = xT[:].rearrange("p c b d -> p (c b) d")
            cg = xc[:].rearrange("p c b d -> p (c b) d")
            link(v.tensor_reduce(mtok[:], xg, AX.X, ALU.add))
            link(v.tensor_scalar(mtok[:], mtok[:], 1.0 / D, None, ALU.mult))
            link(v.tensor_tensor(cg, xg, mtok[:].unsqueeze(2).broadcast_to([P, NT, D]), ALU.subtract))
            link(v.tensor_tensor(cg, cg, cg, ALU.mult))
            v.tensor_reduce(m1[:].rearrange("p b c -> p (b c)"), cg, AX.X, ALU.add).then_inc(s_var, 1)
            v.tensor_copy(statT[:, :, 0:16:4], mtok[:].rearrange("p (c b) -> p c b", b=B))
            v.tensor_reduce(statT[:, :, 2:16:4], xT[:], AX.X, ALU.max)
            link(v.tensor_reduce(statT[:, :, 3:16:4], xT[:], AX.X, ALU.min))
            dve.wait_ge(s_std, 1)
            v.sem_inc(s_stat, 1)
            dve.wait_ge(s_rows, 1)
            v.tensor_copy(rt[:], ps[0][0:D, 0:12]).then_inc(s_rowc, 1)
            link(v.tensor_copy(rc[:].rearrange("p b c k -> p (b c k)"), ps[1][0:P, 0:72]))
            dve.wait_ge(s_bm, 1)
            link(v.tensor_scalar(bm[:, 0, :], ps[2][:, 0:12], 0.5, None, ALU.mult))
            link(v.tensor_scalar(rtc[:, 0, :], rt[:], 0.5, None, ALU.mult))
            link(v.tensor_tensor(rtc[:, 0, :], rtc[:, 0, :], bm[0:D, 0, :], ALU.subtract))
            v.tensor_tensor(rtc[:, 1, :], rtc[:, 0, :], rtc[:, 0, :], ALU.mult).then_inc(s_usq, 1)
            link(v.tensor_copy(basis[:, :, :, 0], rtc[:, 0, :].rearrange("d (b k) -> d k b", k=3)))
            for a in range(3):
                v.tensor_copy(qku[:, 0, :, :, 3 * a:3 * a + 3].rearrange("d k b r -> d (k b) r"),
                              basis[:, :, :, a:a + 1].rearrange("d k b r -> d (k b) r").broadcast_to([D, 12, 3]))
                v.tensor_copy(qku[:, 1, :, :, 3 * a:3 * a + 3], basis[:])
            for k in range(3):
                v.tensor_copy(vu[:, k, :, :, :].rearrange("d b i r -> d (b i) r"),
                              basis[:, k, :, :].rearrange("d b i -> d (b i)").unsqueeze(2).broadcast_to([D, 12, NR]))
            for j in range(12):
                last = v.tensor_scalar(diag[:, j, :], ident[0:D, 0:D], rtc[:, 0, j:j + 1], None, ALU.mult)
            last.then_inc(s_basis, 1)
            link(
                 v.tensor_scalar(hm[:], rc[:], 0.5, None, ALU.mult))
            for c in range(CH):
                link(v.tensor_tensor(hm[:, :, c, :], hm[:, :, c, :],
                                     bm[0:P, 0, :].rearrange("p (b k) -> p b k", k=3), ALU.add))
            link(v.tensor_reduce(m1[:], hm[:], AX.X, ALU.add))
            link(v.tensor_scalar(m1[:], m1[:], 1.0 / 3, None, ALU.mult))
            hg = hm[:].rearrange("p b c k -> p (b c) k")
            ag = ak[:].rearrange("p b c k -> p (b c) k")
            mg = m1[:].rearrange("p b c -> p (b c)")
            link(v.tensor_tensor(ag, hg, mg.unsqueeze(2).broadcast_to([P, NT, 3]), ALU.subtract))
            link(v.tensor_tensor(aq[:], ak[:], ak[:], ALU.mult))
            link(v.tensor_reduce(rs[:], aq[:], AX.X, ALU.add))
            dve.wait_ge(s_v0, 1)
            link(v.tensor_reduce(v0[:], ps[3][:, 0:12].rearrange("p (b k) -> p b k", k=3), AX.X, ALU.add))
            link(v.tensor_tensor(rs[:], rs[:], v0[0:P, :].unsqueeze(2).broadcast_to([P, B, CH]), ALU.add))
            v.tensor_scalar(rs[:], rs[:], 1.0 / 3, EPS, ALU.mult, ALU.add).then_inc(s_var, 1)
            dve.wait_ge(s_std, 2)
            link(v.reciprocal(rs[:], rs[:]))
            rcb = rs[:].rearrange("p b c -> p c b")
            link(v.tensor_copy(phi[:, :, :, 1], rcb))
            for a in range(2):
                link(v.tensor_tensor(phi[:, :, :, 2 + a], rcb, ak[:, :, :, a].rearrange("p b c -> p c b"), ALU.mult))
            pg = phi[:].rearrange("p c b s -> p (c b) s")

            def product(out, n, a, src):
                link(v.tensor_tensor(pg[:, :, out:out + n], pg[:, :, 1 + a:2 + a].broadcast_to([P, NT, n]),
                                     pg[:, :, src:src + n], ALU.mult))

            product(4, 3, 0, 1)
            product(7, 2, 1, 2)
            product(9, 1, 2, 3)
            product(10, 6, 0, 4)
            product(16, 3, 1, 7)
            product(19, 1, 2, 9)
            v.sem_inc(s_phi, 1)
            dve.wait_ge(s_qk, 1)
            link(v.tensor_copy(qs[:], ps[4][:, 0:E]))
            link(v.tensor_tensor(qk[:], qs[:], ps[5][:, 0:E], ALU.mult))
            link(v.tensor_reduce(Mx[:], qk[:].rearrange("p (h f) -> p h f", f=FEAT), AX.X, ALU.add))
            link(v.tensor_scalar(Mx[:], Mx[:], 0.25, one9[:], ALU.mult, ALU.add))
            v.sem_inc(s_Mx, 1)
            dve.wait_ge(s_phic, 1)
            link(v.tensor_tensor_scan(S[:], ones[:], phiT[:], 0.0, ALU.mult, ALU.add))
            link(v.tensor_copy(v0[:, 0:1], S[:, L - 1:L]))
            v.tensor_scalar(S[:], S[:], v0[:, 0:1], None, ALU.add).then_inc(s_S, 1)
            dve.wait_ge(s_xy, 1)
            for b in range(B):
                link(v.tensor_copy(xs[:], ps[4][0:NR, b * H0:(b + 1) * H0]))
                link(v.tensor_tensor(T2[:, b, :], xs[:], ps[5][0:NR, b * H0:(b + 1) * H0], ALU.mult))
            for b in range(B):
                dve.wait_ge(s_vps, b + 1)
                if b >= 1:
                    dve.wait_ge(s_C, b)
                for i in range(3):
                    last = v.tensor_tensor(T3[:, i, :].rearrange("r (h e) -> r h e", e=FEAT),
                                           T2[:, b, :].unsqueeze(2).broadcast_to([NR, H0, FEAT]),
                                           ps[(2, 3, 6)[i]][0:NR, 0:E].rearrange("r (h e) -> r h e", e=FEAT), ALU.mult)
                last.then_inc(s_T3, 1)
            for b in range(B):
                dve.wait_ge(s_Gc, b + 1)
                for n in range(2):
                    at = slice(n * HALF, (n + 1) * HALF)
                    last = v.tensor_tensor(Ft[:, b, at], G1[:, at], ps[2 + n][0:NF, 0:HALF], ALU.mult)
                last.then_inc(s_F, 1)

            def residual(t):
                b, c = divmod(t, CH)
                dve.wait_ge(s_o, t + 1)
                link(v.tensor_tensor(h[:, t, :], ps[4 + t % 2][0:P, 0:E], u0row[:, b, :], ALU.add))
                hk = h[:, t, :].rearrange("p (k d) -> p k d", k=3)
                v.tensor_tensor(hk, hk, hm[:, b, c, :].unsqueeze(2).broadcast_to([P, 3, D]), ALU.add).then_inc(s_h, 1)

            for t in range(NT):
                dve.wait_ge(s_y, t + 1)
                if t >= 2:
                    dve.wait_ge(s_yt, t - 1)
                link(v.reciprocal(rden[:, t % 2, :], ps[t % 2][0:P, E:E + H0]))
                v.tensor_tensor(yn[:, t % 2, :].rearrange("p (h e) -> p h e", e=FEAT),
                                ps[t % 2][0:P, 0:E].rearrange("p (h e) -> p h e", e=FEAT),
                                rden[:, t % 2, :].unsqueeze(2).broadcast_to([P, H0, FEAT]), ALU.mult).then_inc(s_yn, 1)
                if t >= 1:
                    residual(t - 1)
            residual(NT - 1)
            dve.wait_ge(s_h, NT)


NE, SLOT = 8, 128
SLOT_BITS = SLOT.bit_length() - 1
BF16 = mybir.dt.bfloat16
RING = 4
NTOK = NT * P


class Moe:

    def __init__(self, name, top, width, gated):
        self.name, self.top, self.width, self.gated = name, top, width, gated
        self.tiles = (NT * P * top - NE) // SLOT + NE
        self.turns = (self.tiles - 2) // RING
        self.rest = self.tiles - RING * self.turns
        assert 2 <= self.rest
        self.cols = 2 * width if gated else width
        self.kc = width // 128


MOE0 = Moe("m0", 2, 384, True)
MOE1 = Moe("m1", 1, 768, False)


def moe(nc, keep, A, h, ident, cfg, out):
    name, top, S, turns, rest = cfg.name, cfg.top, cfg.tiles, cfg.turns, cfg.rest
    ctx = ExitStack()
    with ctx:
        def sb(n, shape, dt=F32):
            return ctx.enter_context(nc.sbuf_tensor(f"{name}_{n}", shape, dt))

        def sem(n):
            return keep.enter_context(nc.semaphore(f"{name}_{n}"))

        kx = 96 if cfg.gated else 97
        w1 = sb("w1", [kx, NE, 2, cfg.cols])
        w2 = sb("w2", [128, NE, cfg.kc, E])
        wr = sb("wr", [96, 2, NE])
        row = sb("row", [P, E if cfg.gated else NE])
        b2 = None if cfg.gated else sb("b2", [1, NE, E])
        n = sb("n", [P, NT, E])
        xn = sb("xn", [P, NT, E]) if cfg.gated else n
        got = [xn if cfg.gated else sb("got0", [P, NT, E]), sb("got1", [P, NT, E]) if top == 2 else None]
        posi = sb("posi", [P, 2, top, NT], I32)
        tile0 = sb("tile0", [P, top, NT, S], BF16)
        tile1 = sb("tile1", [P, top, NT, 2, S], BF16)
        at = sb("at", [P, top, NT], BF16)
        lane = sb("lane", [P, top, NT], BF16)
        lane1 = sb("lane1", [P, top, NT, SLOT], BF16)
        num_p = sb("num_p", [P, 1])
        num_t = sb("num_t", [P, top, NT], BF16)
        iott = sb("iott", [P, S], BF16)
        iotl = sb("iotl", [P, SLOT], BF16)
        padrow = sb("padrow", [128, S])
        who = sb("who", [128, 3, S])
        take = sb("take", [128, RING * (turns + 2)], U32)
        give = sb("give", [128, S], U32)
        rows = sb("rows", [128, RING, 2], U32)
        st = sb("st", [P, NT, 6])
        mv = sb("mv", [P, NT, 2])
        rstd = sb("rstd", [P, NT])
        msq = sb("msq", [P, NT])
        xnT = sb("xnT", [96, RING, 2, P])
        lg = sb("lg", [P, NT, NE])
        lm = sb("lm", [P, NT])
        pr = sb("pr", [P, NT, NE])
        tmp = sb("tmp", [P, NT, NE])
        oh = sb("oh", [P, 2, NT, NE])
        msk = sb("msk", [P, NT, NE])
        pe_ = sb("pe", [P, top, NT])
        idx = sb("idx", [P, NT])
        iotx = sb("iotx", [P, NT, NE])
        iot128 = sb("iot128", [128, NT])
        iots = sb("iots", [1, S + 2])
        zero = sb("zero", [128, E])
        tri = sb("tri", [P, P])
        ones = sb("ones", [128, NE * NT])
        tot = sb("tot", [128, NE, NT])
        inc = sb("inc", [128, NE, NT])
        exc = sb("exc", [128, NE, NT])
        cnt = sb("cnt", [128, NE])
        big = sb("big", [128, NE, NT])
        nt_ = sb("nt", [128, NE])
        cum = sb("cum", [128, NE])
        pos = sb("pos", [P, NT, NE])
        posf = sb("posf", [P, top, NT])
        ecmp = sb("ecmp", [1, S + 2, NE])
        eidf = sb("eidf", [1, S + 2])
        eid = sb("eid", [1, S + 2], I32)
        xg = sb("xg", [SLOT, RING, E])
        xgT = sb("xgT", [kx, 2, 2, SLOT])
        act_g = sb("act_g", [SLOT, cfg.width])
        hid = sb("hid", [SLOT, cfg.width])
        hidT = sb("hidT", [128, cfg.width])
        y = sb("y", [SLOT, RING, E])
        X = nc.dram_tensor(f"{name}_X", (NTOK, E), F32, kind="Internal").ap()
        Y = nc.dram_tensor(f"{name}_Y", (top * NTOK + (S + RING) * SLOT, E), F32, kind="Internal").ap()
        psX = ctx.enter_context(nc.psum_tensor(f"{name}_psX", [128, 512], F32))
        psG = [ctx.enter_context(nc.psum_tensor(f"{name}_psG{i}", [128, 2, 512], F32)) for i in range(2)]
        nH = cfg.width // 384
        psH = ctx.enter_context(nc.psum_tensor(f"{name}_psH", [128, nH, 512], F32))
        psY = ctx.enter_context(nc.psum_tensor(f"{name}_psY", [128, 512], F32))

        s_w, s_r, s_z, s_X, s_cst = sem("w"), sem("r"), sem("z"), sem("X"), sem("cst")
        s_v, s_ln, s_sd, s_n, s_xn = sem("v"), sem("ln"), sem("sd"), sem("n"), sem("xn")
        s_rt, s_rc, s_lg, s_ls, s_ex, s_m, s_rank, s_pos = (sem(k) for k in (
            "rt", "rc", "lg", "ls", "ex", "m", "rank", "pos"))
        s_eid, s_num, s_b, s_who = sem("eid"), sem("num"), sem("b"), sem("who")
        s_col, s_turn = sem("col"), sem("turn")
        s_in = [sem(f"in{j}") for j in range(RING)]
        s_st = [sem(f"st{j}") for j in range(RING)]
        s_xt, s_xc, s_gu, s_sg, s_h, s_ht, s_hc, s_c, s_y = (sem(k) for k in (
            "xt", "xc", "gu", "sg", "h", "ht", "hc", "c", "y"))
        s_got, s_out, s_res = [sem(f"got{b}") for b in range(B)], sem("out"), sem("res")
        block = ctx.enter_context(nc.Block())

        @block.sync
        def _(sp):
            sp.dma_start(wr[:], A[f"{name}_wr"]).then_inc(s_r, 16)
            sp.dma_start(row[:], A[f"{name}_row"].partition_broadcast(P)).then_inc(s_r, 16)
            for e in range(NE):
                sp.dma_start(w1[:, e], A[f"{name}_w1"][:, e]).then_inc(s_w, 16)
                sp.dma_start(w2[:, e], A[f"{name}_w2"][:, e]).then_inc(s_w, 16)
            if not cfg.gated:
                sp.dma_start(b2[:], A[f"{name}_b2"]).then_inc(s_w, 16)
            for b in range(B):
                sp.wait_ge(s_xn if cfg.gated else s_n, CH * (b + 1))
                sp.dma_start(X[b * L:(b + 1) * L, :].rearrange("(c p) e -> p c e", p=P),
                             xn[:, b * CH:(b + 1) * CH, :]).then_inc(s_X, 16)
            sp.wait_ge(s_X, 16 * B)
            for j in range(RING):
                sp.wait_ge(s_st[j], 16 * (turns + 1 + (j < rest)))
            for b in range(B):
                for k in range(top):
                    sp.dma_start(got[k][:, b * CH:(b + 1) * CH, :],
                                 Y[k * NTOK + b * L:k * NTOK + (b + 1) * L, :].rearrange("(c p) e -> p c e", p=P)
                                 ).then_inc(s_got[b], 16)
            for b in range(B):
                sp.wait_ge(s_got[b], 16 * top)
            if out is not None:
                for b in range(B):
                    sp.wait_ge(s_res, CH * (b + 1))
                    sp.dma_start(out[b].rearrange("(c p) e -> p c e", p=P),
                                 h[:, b * CH:(b + 1) * CH, :]).then_inc(s_out, 16)
                sp.wait_ge(s_out, 16 * B)

        @block.gpsimd
        def _(pool):
            if not cfg.gated:
                pool.memset(xgT[96:97, :, :, :], 1.0).then_inc(s_cst, 1)
                pool.wait_ge(s_cst, 1)
            pool.memset(zero[:], 0.0).then_inc(s_z, 1)
            pool.memset(ones[:], 1.0)
            pool.memset(take[:, S:], 0)
            pool.memset(tri[:], 1.0)
            pool.iota(iotx[:], pattern=[[0, NT], [1, NE]], base=NE, channel_multiplier=0, allow_small_or_imprecise_dtypes=True)
            pool.iota(iot128[:], pattern=[[SLOT, NT]], base=0, channel_multiplier=0,
                      allow_small_or_imprecise_dtypes=True)
            pool.iota(iott[:], pattern=[[1, S]], base=0, channel_multiplier=0,
                      allow_small_or_imprecise_dtypes=True)
            pool.iota(iotl[:], pattern=[[1, SLOT]], base=0, channel_multiplier=0,
                      allow_small_or_imprecise_dtypes=True)
            pool.iota(num_p[:], pattern=[[0, 1]], base=1, channel_multiplier=1, allow_small_or_imprecise_dtypes=True)
            pool.iota(num_t[:], pattern=[[NT, top], [1, NT]], base=0, channel_multiplier=0,
                      allow_small_or_imprecise_dtypes=True)
            pool.iota(padrow[:], pattern=[[SLOT, S]], base=top * NTOK + 1, channel_multiplier=1,
                      allow_small_or_imprecise_dtypes=True)
            pool.iota(iots[:], pattern=[[1, S + 2]], base=0, channel_multiplier=0,
                      allow_small_or_imprecise_dtypes=True).then_inc(s_z, 1)
            pool.wait_ge(s_z, 2)
            pool.affine_select(out=tri[:], in_=tri[:], compare_op=ALU.is_gt, fill=0.0, base=0,
                               pattern=[[1, P]], channel_multiplier=-1).then_inc(s_cst, 1)
            pool.wait_ge(s_z, 2)
            for j in range(RING):
                row0 = top * NTOK + (S + j) * SLOT
                pool.dma_start(Y[row0:row0 + SLOT, :], zero[:]).then_inc(s_st[j], 16)
            pool.wait_ge(s_num, 1)
            pool.tensor_tensor(tile1[:, :, :, 1, :].rearrange("p k t s -> p (k t) s"),
                               tile0[:].rearrange("p k t s -> p (k t) s"),
                               num_t[:].rearrange("p k t -> p (k t)").unsqueeze(2).broadcast_to([P, top * NT, S]),
                               ALU.mult).then_inc(s_who, 1)

            def gather(j):
                pool.indirect_dma_start(out=xg[:, j, :], out_offset=None, in_=X,
                                        in_offset=bass.IndirectOffsetOnAxis(ap=rows[:, j, 0:1], axis=0)
                                        ).then_inc(s_in[j], 16)

            def scatter(j):
                pool.indirect_dma_start(
                    out=Y, out_offset=bass.IndirectOffsetOnAxis(ap=rows[:, j, 1:2], axis=0),
                    in_=y[:, j, :], in_offset=None).then_inc(s_st[j], 16)

            pool.wait_ge(s_X, 16 * B)
            pool.wait_ge(s_pos, 1)
            pool.tensor_copy(rows[:, :, 0], take[:, 0:RING]).then_inc(s_col, 1)
            pool.wait_ge(s_col, 1)
            for j in range(RING):
                gather(j)
            with pool.Fori(0, turns) as i:
                for j in range(RING):
                    pool.wait_ge(s_xt, RING * i + (j + 1))
                    pool.wait_ge(s_st[j], 16 * i + 16)
                    pool.tensor_copy(rows[:, j, 0:1], take[:, bass.ds(RING * i + (RING + j), 1)]).then_inc(s_col, 1)
                    pool.tensor_copy(rows[:, j, 1:2], give[:, bass.ds(RING * i + j, 1)]).then_inc(s_col, 1)
                    pool.wait_ge(s_col, 2 * RING * i + (2 * j + 3))
                    pool.sem_inc(s_turn, 1)
                    gather(j)
                    pool.wait_ge(s_y, RING * i + (j + 2))
                    pool.sem_inc(s_turn, 1)
                    scatter(j)
            for j in range(rest):
                pool.wait_ge(s_st[j], 16 * (turns + 1))
            pool.tensor_copy(rows[:, 0:rest, 1], give[:, RING * turns:S]).then_inc(s_col, 1)
            pool.wait_ge(s_col, 2 * RING * turns + 2)
            for j in range(rest):
                pool.wait_ge(s_y, RING * turns + j + 2)
                scatter(j)
            for j in range(RING):
                pool.wait_ge(s_in[j], 16 * (turns + 1))
                pool.wait_ge(s_st[j], 16 * (turns + 1 + (j < rest)))

        @block.tensor
        def _(pe):
            pe.wait_ge(s_r, 32)

            def logits(t):
                pe.wait_ge(s_rc, t + 1)
                for k in range(2):
                    last = nc.tensor.matmul(psX[0:P, 256 + NE * t:256 + NE * t + NE], xnT[:, t % RING, k, :],
                                            wr[:, k, :], start=(k == 0), stop=(k == 1))
                last.then_inc(s_lg, 1)

            for t in range(NT):
                pe.wait_ge(s_xn if cfg.gated else s_n, t + 1)
                if t >= RING:
                    pe.wait_ge(s_rc, t - RING + 1)
                for k in range(2):
                    last = nc.tensor.transpose(psG[t % 2][0:96, t // 2 % 2, k * P:(k + 1) * P], xn[:, t, 96 * k:96 * k + 96],
                                               ident[0:P, 0:P])
                last.then_inc(s_rt, 1)
                if t >= 2:
                    logits(t - 2)
            logits(NT - 2)
            logits(NT - 1)
            pe.wait_ge(s_m, 1)
            pe.wait_ge(s_cst, 1 if cfg.gated else 2)
            mm = msk[:].rearrange("p t e -> p (t e)")
            nc.tensor.matmul(psG[0][0:P, 0, 0:NT * NE], tri[:], mm, start=True, stop=True)
            nc.tensor.matmul(psG[0][:, 1, 0:NT * NE], ones[0:P, 0:128], mm, start=True, stop=True).then_inc(s_rank, 1)

            pe.wait_ge(s_who, 2)
            for k in range(top):
                pe.wait_ge(s_b, k + 1)
                for t in range(NT):
                    last = nc.tensor.matmul(psY[:, 0:2 * S], lane1[:, k, t, :],
                                            tile1[:, k, t, :, :].rearrange("p n s -> p (n s)"),
                                            start=(k == 0 and t == 0), stop=(k == top - 1 and t == NT - 1))
            last.then_inc(s_rank, 1)

            def to_columns(buf):
                for k in range(2):
                    last = nc.tensor.transpose(psX[0:96, k * SLOT:(k + 1) * SLOT], xg[:, buf, 96 * k:96 * k + 96],
                                               ident[:])
                last.then_inc(s_xt, 1)

            def first_products(buf, e):
                half = cfg.cols // 2
                for g in range(2):
                    for k in range(2):
                        last = nc.tensor.matmul(psG[buf][:, g, 0:half], xgT[:, buf, k, :],
                                                w1[:, bass.ds(e, 1), k, g * half:(g + 1) * half].rearrange(
                                                    "d o f -> d (o f)"),
                                                start=(k == 0), stop=(k == 1))
                last.then_inc(s_gu, 1)

            pe.wait_ge(s_eid, 1)
            pe.wait_ge(s_w, 16 * (2 * NE + (0 if cfg.gated else 1)))
            for j in range(2):
                pe.wait_ge(s_in[j], 16)
                if j:
                    pe.wait_ge(s_xc, 1)
                to_columns(j)
            pe.wait_ge(s_xc, 2)
            pe.sem_inc(s_ht, 1)
            pe.sem_inc(s_c, 1)
            owner = [nc.tensor.alloc_register(f"{name}_owner{j}") for j in range(2)]
            nc.tensor.reg_load(owner[0], eid[0:1, 0:1])
            first_products(0, nc.tensor.snap(owner[0], min_val=0, max_val=NE - 1))

            def turn(i, count, ahead):
                for j in range(count):
                    if j < ahead:
                        pe.wait_ge(s_in[(j + 2) % RING], 16 * i + 16 * (1 + (j + 2) // RING))
                        pe.wait_ge(s_xc, RING * i + (j + 2))
                        to_columns((j + 2) % RING)
                    pe.wait_ge(s_h, RING * i + (j + 2))
                    pe.wait_ge(s_hc, RING * i + (j + 1))
                    for k in range(cfg.kc):
                        last = nc.tensor.transpose(psH[:, k // 3, (k % 3) * 128:(k % 3 + 1) * 128],
                                                   hid[:, k * 128:(k + 1) * 128], ident[:])
                    last.then_inc(s_ht, 1)
                    here = nc.tensor.snap(owner[j % 2], min_val=0, max_val=NE - 1)
                    if j < ahead + 1:
                        nc.tensor.reg_load(owner[1 - j % 2], eid[0:1, bass.ds(RING * i + (j + 1), 1)])
                        pe.wait_ge(s_xc, RING * i + (j + 2))
                        first_products(1 - j % 2, nc.tensor.snap(owner[1 - j % 2], min_val=0, max_val=NE - 1))
                    pe.wait_ge(s_hc, RING * i + (j + 2))
                    pe.wait_ge(s_y, RING * i + (j + 1))
                    for k in range(cfg.kc):
                        last = nc.tensor.matmul(psY[:, 0:E], hidT[:, k * 128:(k + 1) * 128],
                                                w2[:, bass.ds(here, 1), k, :].rearrange("f o e -> f (o e)"),
                                                start=(k == 0), stop=(cfg.gated and k == cfg.kc - 1))
                    if not cfg.gated:
                        last = nc.tensor.matmul(psY[:, 0:E], ones[0:1, 0:128],
                                                b2[:, bass.ds(here, 1), :].rearrange("f o e -> f (o e)"),
                                                start=False, stop=True)
                    last.then_inc(s_c, 1)

            with pe.Fori(0, turns) as i:
                turn(i, RING, RING)
            turn(turns, rest, rest - 2)

        @block.scalar
        def _(act):
            act.wait_ge(s_ln, 1)
            nc.scalar.activation(rstd[:], rstd[:], ACT.Sqrt).then_inc(s_sd, 1)
            if cfg.gated:
                act.wait_ge(s_ln, 2)
                nc.scalar.activation(msq[:], msq[:], ACT.Sqrt).then_inc(s_sd, 1)
            for t in range(NT):
                act.wait_ge(s_rt, t + 1)
                if t >= RING:
                    act.wait_ge(s_lg, t - RING + 1)
                nc.scalar.activation(xnT[:, t % RING, :, :].rearrange("d k p -> d (k p)"),
                                     psG[t % 2][0:96, t // 2 % 2, 0:2 * P], ACT.Copy).then_inc(s_rc, 1)
            act.wait_ge(s_ls, 1)
            nc.scalar.activation(lg[:], lg[:], ACT.Exp).then_inc(s_ex, 1)

            def columns(buf):
                nc.scalar.activation(xgT[0:96, buf, :, :].rearrange("d k p -> d (k p)"), psX[0:96, 0:2 * SLOT],
                                     ACT.Copy).then_inc(s_xc, 1)

            if not cfg.gated:
                act.wait_ge(s_z, 2)
            for j in range(2):
                act.wait_ge(s_xt, j + 1)
                columns(j)

            def turn(i, count, ahead):
                for j in range(count):
                    act.wait_ge(s_gu, RING * i + (j + 1))
                    if cfg.gated:
                        act.wait_ge(s_h, RING * i + (j + 1))
                        nc.scalar.activation(act_g[:], psG[j % 2][:, 0, 0:384], ACT.Silu).then_inc(s_sg, 1)
                    else:
                        act.wait_ge(s_ht, RING * i + (j + 1))
                        nc.scalar.activation(hid[:].rearrange("p (a f) -> p a f", a=2), psG[j % 2][:, :, 0:384],
                                             ACT.Gelu).then_inc(s_h, 1)
                    if j < ahead:
                        act.wait_ge(s_xt, RING * i + (j + 3))
                        columns(j % 2)

            with act.Fori(0, turns) as i:
                turn(i, RING, RING)
            turn(turns, rest, rest - 2)

        @block.vector
        def _(dve):
            v = nc.vector
            link = Chain(dve, s_v)
            for t in range(NT):
                v.bn_stats(st[:, t, :], h[:, t, :]).then_inc(s_v, 1)
            link.n += NT
            dve.wait_ge(s_v, link.n)
            for t in range(NT):
                v.bn_aggr(mv[:, t, :], st[:, t, :]).then_inc(s_v, 1)
            link.n += NT
            dve.wait_ge(s_v, link.n)
            v.tensor_scalar(rstd[:], mv[:, :, 1], EPS, None, ALU.add).then_inc(s_ln, 1)
            dve.wait_ge(s_sd, 1)
            link(v.reciprocal(rstd[:], rstd[:]))
            if cfg.gated:
                link(v.tensor_tensor(msq[:], rstd[:], rstd[:], ALU.mult))
                link(v.tensor_tensor(msq[:], msq[:], mv[:, :, 1], ALU.mult))
                v.tensor_scalar(msq[:], msq[:], 1e-6, None, ALU.add).then_inc(s_ln, 1)
            if cfg.gated:
                dve.wait_ge(s_sd, 2)
                link(v.reciprocal(msq[:], msq[:]))
                dve.wait_ge(s_r, 32)
            for t in range(NT + 1):
                if t < NT:
                    v.tensor_scalar(n[:, t, :], h[:, t, :], mv[:, t, 0:1], rstd[:, t:t + 1], ALU.subtract,
                                    ALU.mult).then_inc(s_n, 1)
                if cfg.gated and t:
                    dve.wait_ge(s_n, t)
                    v.scalar_tensor_tensor(xn[:, t - 1, :], n[:, t - 1, :], msq[:, t - 1:t], row[:], ALU.mult,
                                           ALU.mult).then_inc(s_xn, 1)
            dve.wait_ge(s_lg, NT)
            dve.wait_ge(s_r, 32)
            lps = psX[0:P, 256:256 + NT * NE].rearrange("p (t e) -> p t e", e=NE)
            if cfg.gated:
                link(v.tensor_copy(lg[:], lps))
            else:
                link(v.tensor_tensor(lg[:], lps, row[:].unsqueeze(1).broadcast_to([P, NT, NE]), ALU.add))
            link(v.tensor_reduce(lm[:], lg[:], AX.X, ALU.max))
            v.tensor_tensor(lg[:], lg[:], lm[:].unsqueeze(2).broadcast_to([P, NT, NE]), ALU.subtract).then_inc(s_ls, 1)
            dve.wait_ge(s_ex, 1)
            link(v.tensor_reduce(lm[:], lg[:], AX.X, ALU.add))
            link(v.reciprocal(lm[:], lm[:]))
            link(v.tensor_tensor(pr[:], lg[:], lm[:].unsqueeze(2).broadcast_to([P, NT, NE]), ALU.mult))
            dve.wait_ge(s_z, 2)
            for k in range(top):
                link(v.tensor_reduce(pe_[:, k, :], pr[:], AX.X, ALU.max))
                link(v.tensor_tensor(tmp[:], pr[:], pe_[:, k, :].unsqueeze(2).broadcast_to([P, NT, NE]), ALU.is_equal))
                link(v.scalar_tensor_tensor(tmp[:].rearrange("p t e -> p (t e)"), tmp[:].rearrange("p t e -> p (t e)"),
                                            -float(NE), iotx[:].rearrange("p t e -> p (t e)"), ALU.mult, ALU.add))
                link(v.tensor_reduce(idx[:], tmp[:], AX.X, ALU.min))
                link(v.tensor_scalar(idx[:], idx[:], float(NE), None, ALU.add))
                link(v.tensor_tensor(oh[:, k, :, :], iotx[:], idx[:].unsqueeze(2).broadcast_to([P, NT, NE]), ALU.is_equal))
                if k + 1 < top:
                    link(v.scalar_tensor_tensor(pr[:].rearrange("p t e -> p (t e)"),
                                                oh[:, k, :, :].rearrange("p t e -> p (t e)"), -2.0,
                                                pr[:].rearrange("p t e -> p (t e)"), ALU.mult, ALU.add))
            if top == 2:
                v.tensor_tensor(msk[:], oh[:, 0], oh[:, 1], ALU.add).then_inc(s_m, 1)
            else:
                v.tensor_copy(msk[:], oh[:, 0]).then_inc(s_m, 1)
            dve.wait_ge(s_rank, 1)
            flat = "p e t -> p (e t)"
            link(v.tensor_copy(tot[:], psG[0][:, 1, 0:NT * NE].rearrange("p (t e) -> p e t", e=NE)))
            link(v.tensor_tensor_scan(inc[:].rearrange(flat), ones[:], tot[:].rearrange(flat), 0.0, ALU.mult, ALU.add))
            link(v.tensor_tensor(exc[:], inc[:], tot[:], ALU.subtract))
            link(v.tensor_tensor(cnt[:], inc[:, :, NT - 1], exc[:, :, 0], ALU.subtract))
            link(v.tensor_tensor(big[:], cnt[:].unsqueeze(2).broadcast_to([128, NE, NT]),
                                 iot128[:].unsqueeze(1).broadcast_to([128, NE, NT]), ALU.is_gt))
            link(v.tensor_reduce(nt_[:], big[:], AX.X, ALU.add))
            link(v.tensor_tensor_scan(cum[:], ones[:, 0:NE], nt_[:], 0.0, ALU.mult, ALU.add))
            link(v.tensor_tensor(ecmp[:], iots[:].unsqueeze(2).broadcast_to([1, S + 2, NE]),
                                 cum[0:1, :].unsqueeze(1).broadcast_to([1, S + 2, NE]), ALU.is_ge))
            link(v.tensor_reduce(eidf[:], ecmp[:], AX.X, ALU.add))
            link(v.tensor_scalar(eidf[:], eidf[:], float(NE - 1), None, ALU.min))
            v.tensor_copy(eid[:], eidf[:]).then_inc(s_eid, 1)
            link(v.tensor_tensor(cnt[:], cum[:], nt_[:], ALU.subtract))
            link(v.tensor_scalar(cnt[:], cnt[:], float(SLOT), None, ALU.mult))
            link(v.tensor_tensor(cnt[:], cnt[:], exc[:, :, 0], ALU.subtract))
            link(v.tensor_tensor(exc[:], exc[:], cnt[:].unsqueeze(2).broadcast_to([128, NE, NT]), ALU.add))
            link(v.tensor_tensor(pos[:], exc[0:P].rearrange("p e t -> p t e"),
                                 psG[0][0:P, 0, 0:NT * NE].rearrange("p (t e) -> p t e", e=NE), ALU.add))
            for k in range(top):
                link(v.tensor_tensor(tmp[:], pos[:], oh[:, k], ALU.mult))
                link(v.tensor_reduce(posf[:, k, :], tmp[:], AX.X, ALU.add))
            shape = [P, top * NT, S]
            link(v.tensor_copy(posi[:, 0], posf[:]))
            link(v.tensor_scalar(posi[:, 1], posi[:, 0], SLOT_BITS, None, ALU.logical_shift_right))
            link(v.tensor_scalar(posi[:, 0], posi[:, 0], SLOT - 1, None, ALU.bitwise_and))
            link(v.tensor_copy(at[:], posi[:, 1]))
            link(v.tensor_copy(lane[:], posi[:, 0]))
            v.tensor_tensor(tile0[:].rearrange("p k t s -> p (k t) s"),
                            at[:].rearrange("p k t -> p (k t)").unsqueeze(2).broadcast_to(shape),
                            iott[:].unsqueeze(1).broadcast_to(shape), ALU.is_equal).then_inc(s_num, 1)
            for k in range(top):
                v.tensor_tensor(lane1[:, k], iotl[:].unsqueeze(1).broadcast_to([P, NT, SLOT]),
                                lane[:, k, :].unsqueeze(2).broadcast_to([P, NT, SLOT]), ALU.is_equal
                                ).then_inc(s_b, 1)
            dve.wait_ge(s_num, 1)
            v.tensor_scalar(tile1[:, :, :, 0, :].rearrange("p k t s -> p (k t) s"),
                            tile0[:].rearrange("p k t s -> p (k t) s"), num_p[:], None, ALU.mult).then_inc(s_who, 1)
            dve.wait_ge(s_rank, 2)
            link(v.tensor_copy(who[:, 2, :], psY[:, 0:S]))
            link(v.scalar_tensor_tensor(who[:, 0, :], psY[:, S:2 * S], float(P), who[:, 2, :], ALU.mult, ALU.add))
            link(v.tensor_scalar(who[:, 1, :], who[:, 0, :], 0.0, None, ALU.is_equal))
            link(v.tensor_tensor(who[:, 2, :], who[:, 1, :], padrow[:], ALU.mult))
            link(v.tensor_tensor(who[:, 2, :], who[:, 2, :], who[:, 0, :], ALU.add))
            link(v.tensor_scalar(who[:, 2, :], who[:, 2, :], -1.0, None, ALU.add))
            link(v.tensor_copy(give[:], who[:, 2, :]))
            link(v.tensor_tensor(who[:, 0, :], who[:, 0, :], who[:, 1, :], ALU.add))
            if top == 2:
                link(v.tensor_scalar(who[:, 1, :], who[:, 0, :], float(NTOK), -float(NTOK), ALU.is_gt, ALU.mult))
                link(v.tensor_tensor(who[:, 0, :], who[:, 0, :], who[:, 1, :], ALU.add))
            link(v.tensor_scalar(who[:, 0, :], who[:, 0, :], -1.0, None, ALU.add))
            v.tensor_copy(take[:, 0:S], who[:, 0, :]).then_inc(s_pos, 1)
            v.sem_inc(s_h, 1)
            v.sem_inc(s_hc, 1)
            v.sem_inc(s_y, 1)

            def gated_hidden(i, j):
                dve.wait_ge(s_sg, RING * i + (j + 1))
                dve.wait_ge(s_ht, RING * i + (j + 1))
                v.tensor_tensor(hid[:], act_g[:], psG[j % 2][:, 1, 0:384], ALU.mult).then_inc(s_h, 1)

            def hidden_columns(i, j):
                dve.wait_ge(s_ht, RING * i + (j + 2))
                dve.wait_ge(s_c, RING * i + (j + 1))
                v.tensor_copy(hidT[:].rearrange("p (a f) -> p a f", a=nH), psH[:, :, 0:384]).then_inc(s_hc, 1)

            def turn(i, count, ahead):
                for j in range(count):
                    if cfg.gated and j < ahead:
                        gated_hidden(i, j + 1)
                    dve.wait_ge(s_c, RING * i + (j + 2))
                    dve.wait_ge(s_st[j], 16 * i + 16)
                    v.tensor_copy(y[:, j, :], psY[:, 0:E]).then_inc(s_y, 1)
                    if j < ahead:
                        hidden_columns(i, j + 1)

            if cfg.gated:
                link(v.tensor_tensor(h[:], h[:], n[:], ALU.add))
                gated_hidden(0, 0)
            hidden_columns(0, 0)
            with dve.Fori(0, turns) as i:
                turn(i, RING, RING)
            turn(turns, rest, rest - 1)
            for t in range(NT):
                if t % CH == 0:
                    dve.wait_ge(s_got[t // CH], 16 * top)
                for k in range(top):
                    ins = v.scalar_tensor_tensor(h[:, t, :], got[k][:, t, :], pe_[:, k, t:t + 1], h[:, t, :], ALU.mult,
                                                 ALU.add)
                    if k + 1 < top:
                        link(ins)
                ins.then_inc(s_res, 1)
            dve.wait_ge(s_res, NT)


def moe_inputs(f):
    t = np.ascontiguousarray
    gu = np.concatenate([f["L0_ffn_gate_w"], f["L0_ffn_up_w"]], axis=1)
    w1 = f["L1_ffn_W1"].reshape(NE, 2, 96, 768).transpose(2, 0, 1, 3)
    w1b = np.zeros((97,) + w1.shape[1:], w1.dtype)
    w1b[:96] = w1
    w1b[96, :, 1] = f["L1_ffn_b1"]
    return {
        "m0_wr": t(f["L0_ffn_router_w"].T.reshape(2, 96, NE).transpose(1, 0, 2)),
        "m0_row": f["L0_ffn_norm_w"],
        "m0_w1": t(gu.transpose(2, 0, 1).reshape(2, 96, NE, 768).transpose(1, 2, 0, 3)),
        "m0_w2": t(f["L0_ffn_down_w"].transpose(2, 0, 1).reshape(3, 128, NE, E).transpose(1, 2, 0, 3)),
        "m1_wr": t(f["L1_ffn_Ws"].reshape(2, 96, NE).transpose(1, 0, 2)),
        "m1_row": f["L1_ffn_bs"],
        "m1_w1": w1b,
        "m1_w2": t(f["L1_ffn_W2"].reshape(NE, 6, 128, E).transpose(2, 0, 1, 3)),
        "m1_b2": t(f["L1_ffn_b2"].reshape(1, NE, E)),
    }


NH, HD, GRID, REACH = 12, 64, 27, 14
HG = 6
LP, HP = 752, 376
LW = 1 + 28 * GRID
NPR = HG // 2
NVG = -(-(L - 1) // GRID)
SCALE = HD ** -0.5
RV, RH, ONE = 64, 96, 127
V_SETS = [(range(a, min(a + 6, NVG - 1)), GRID) for a in range(0, NVG - 1, 6)] + [(range(NVG - 1, NVG), L - 1 - GRID * (NVG - 1))]
FULL = L - 1 - GRID * (NVG - 1)
H_SETS = [(range(a, min(a + 6, FULL)), NVG) for a in range(0, FULL, 6)] \
    + [(range(a, min(a + 6, GRID)), NVG - 1) for a in range(FULL, GRID, 6)]
NV, NHS = len(V_SETS), len(H_SETS)
NSET = NV + NHS + 1


def relative_inputs(f):
    def rows(table, n, g):
        at = np.zeros(n, int) if g is None else np.clip(np.arange(n) - g, -REACH, REACH) + REACH + 1
        return table[at]

    out = {}
    for key, v, hh in (("rq", f["L1_attn_rk_v"], f["L1_attn_rk_h"]), ("rv", f["L1_attn_rv_v"], f["L1_attn_rv_h"])):
        for side, table, n, count in (("v", v, NVG, NVG), ("h", hh, GRID, GRID)):
            t = np.zeros((128, count + 1, 64), table.dtype)
            for g in range(count + 1):
                r = np.concatenate([rows(table, n, None if g == 0 else g - 1), table[0:1]])
                if key == "rq":
                    t[0:64, g, 0:n + 1] = r.T
                    t[64:128, g, 32:33 + n] = r.T
                else:
                    at = RV if side == "v" else RH
                    t[at:at + n + 1, g] = r
                    if side == "v":
                        t[0:64, g] = np.eye(64, dtype=table.dtype)
            out[key + side] = t
    oh = np.zeros((64, L), np.float32)
    j = np.arange(1, L)
    oh[(j - 1) // GRID, j] = 1
    oh[RH - 64 + (j - 1) % GRID, j] = 1
    oh[NVG, 0] = oh[RH - 64 + GRID, 0] = 1
    oh[ONE - 64] = 1
    out["oh"] = oh
    out["ohT"] = np.ascontiguousarray(oh.T.reshape(CH, P, 64).transpose(1, 0, 2))
    t = np.ascontiguousarray
    for k in "qkv":
        out["w" + k] = t(f["L1_attn_w" + k].reshape(2, 96, NH * HD).transpose(1, 0, 2))
    out["wp"] = t(f["L1_attn_wproj"].reshape(NH // 2, 128, E).transpose(1, 0, 2))
    out["bp"] = f["L1_attn_bproj"]
    return {"a1_" + k: v for k, v in out.items()}


def window_attention(nc, keep, A, h, ident):
    ctx = ExitStack()
    with ctx:
        def sb(n, shape, dt=F32):
            return ctx.enter_context(nc.sbuf_tensor(f"a1_{n}", shape, dt))

        def sem(n):
            return keep.enter_context(nc.semaphore(f"a1_{n}"))

        w = {k: sb("w" + k, [96, 2, HG * HD]) for k in "qkv"}
        wp = sb("wp", [128, NPR, E])
        rqv, rvv = sb("rqv", [128, NVG + 1, 64]), sb("rvv", [128, NVG + 1, 64])
        rqh, rvh = sb("rqh", [128, GRID + 1, 64]), sb("rvh", [128, GRID + 1, 64])
        bp = sb("bp", [P, E])
        qhi, qlo = sb("qhi", [128, HG, LP], F32R), sb("qlo", [128, HG, LP], F32R)
        khi, klo = sb("khi", [128, HG, L], F32R), sb("klo", [128, HG, L], F32R)
        work = sb("work", [128, HG, LW])
        pairs = sb("pairs", [128, NPR, LW])
        vhi, vlo = sb("vhi", [P, CH, HG, 128], F32R), sb("vlo", [P, CH, HG, HD], F32R)
        hnT = sb("hnT", [96, 2, L])
        PT = sb("PT", [P, 2, LP])
        Phi, Plo = sb("Phi", [P, 2, LP], F32R), sb("Plo", [P, 2, LP], F32R)
        nb = pairs[0:P].rearrange("p a l -> p (a l)")[:, 0:CH * E].rearrange("p (c e) -> p c e", e=E)
        rdb = qhi[:].bitcast(F32)[:, 0:NPR, :]
        dcol = PT[0:LP // 8, 0, 0:HG * 8].rearrange("p (h s) -> p h s", s=8)
        oh = pairs[64:128, NPR - 1, 0:L]
        ohT = PT[:, 1, 0:CH * 64].rearrange("p (c d) -> p c d", d=64)
        st = PT[:, 0, 0:6 * NT].rearrange("p (t s) -> p t s", s=6)
        mean = sb("mean", [P, NT])
        rstd = sb("rstd", [P, NT])
        mv_ = PT[:, 0, 6 * NT:8 * NT].rearrange("p (t s) -> p t s", s=2)
        nmx = sb("nmx", [P, 2, CH])
        mrow = sb("mrow", [CH, 2, P], F32R)
        psS = [ctx.enter_context(nc.psum_tensor(f"a1_S{i}", [128, 2, 512], F32)) for i in range(2)]
        psM = ctx.enter_context(nc.psum_tensor("a1_M", [128, 2, 512], F32))
        psO = ctx.enter_context(nc.psum_tensor("a1_O", [128, 2, 512], F32))

        s_bp = sem("bp")
        s_wh, s_wp = sem("wh"), sem("wp")
        s_w, s_oh, s_oz, s_og = sem("w"), sem("oh"), sem("oz"), sem("og")
        s_v, s_ln, s_sd = sem("v"), sem("ln"), sem("sd")
        names = ("nb", "xt", "xc", "kp", "ka", "kd", "qp", "qa", "qd", "vp", "vc", "bg", "bga", "bgd", "sp", "m1", "mx", "mt", "mr",
                 "s", "e", "av", "o", "lo", "vd", "rg", "rga", "rgd", "pr", "g", "cp2", "rd", "nm")
        sg = {n: sem(n) for n in names}
        dens = nc.dram_tensor("a1_dens", (HG, LP), F32, kind="Internal").ap()
        rdens = nc.dram_tensor("a1_rdens", (HG, LP), F32, kind="Internal").ap()
        s_dr, s_dc, s_dw = sem("dr"), sem("dc"), sem("dw")
        s_md, s_db = [sem("md0"), sem("md1")], sem("db")
        PER = dict(nb=CH, xt=3, xc=3, kp=6, ka=6, kd=6, qp=6, qa=6, qd=6, vp=12, vc=12, bg=2 * NSET, bga=2 * NSET, bgd=2 * NSET,
                   sp=12, m1=72, mx=72, mt=12, mr=12, s=72, e=72, av=72, o=12, lo=72, vd=12, rg=2 * NSET, rga=2 * NV,
                   rgd=2 * (NHS + 1), pr=12, g=12, cp2=12, rd=2, nm=12)

        def waiter(eng, i):
            def wait(name, k):
                eng.wait_ge(sg[name], i * PER[name] + k)
            return wait

        k_banks = (psS[0], psS[1], psM)
        q_banks = (psS[1], psS[0], psO)
        rv_banks = (psO[:, 0], psO[:, 1], psS[0][:, 0], psS[0][:, 1])
        xt_banks = (psS[0][0:96, 0], psS[0][0:96, 1], psS[1][0:96, 0])
        t_banks = (psS[0][:, 0], psS[0][:, 1], psO[:, 0], psO[:, 1])
        block = ctx.enter_context(nc.Block())

        @block.sync
        def _(sp):
            def load_weights(half):
                for k in "qkv":
                    sp.dma_start(w[k][:], A["a1_w" + k][:, :, half * HG * HD:(half + 1) * HG * HD]).then_inc(s_wh, 16)

            load_weights(0)
            for t, k in ((rqv, "rqv"), (rqh, "rqh"), (rvv, "rvv"), (rvh, "rvh")):
                sp.dma_start(t[:], A["a1_" + k]).then_inc(s_w, 16)
            sp.dma_start(bp[:], A["a1_bp"].partition_broadcast(P)).then_inc(s_w, 16)
            sp.dma_start(oh, A["a1_oh"]).then_inc(s_oh, 16)
            sp.dma_start(ohT, A["a1_ohT"]).then_inc(s_oh, 16)
            with sp.Fori(0, B) as i:
                wait = waiter(sp, i)
                for half in range(2):
                    def max_row(u):
                        wait("mr", u + 1)
                        for c in range(CH):
                            sp.dma_start(qhi[ONE:ONE + 1, u % HG, c * P:(c + 1) * P].bitcast(F32),
                                         mrow[c:c + 1, u % 2, :].bitcast(F32)).then_inc(s_md[u % 2], 16)

                    u0 = half * HG
                    max_row(u0)
                    max_row(u0 + 1)
                    wait("vp", (half + 1) * CH)
                    load_weights(1 - half)
                    sp.dma_start(wp[:], A["a1_wp"][:, half * NPR:(half + 1) * NPR]).then_inc(s_wp, 16)
                    for u in range(u0, u0 + HG):
                        if u + 2 < u0 + HG:
                            max_row(u + 2)
                        wait("o", u + 1)
                        sp.dma_start(dens[u % HG:u % HG + 1, :], work[ONE:ONE + 1, u % HG, 0:LP]).then_inc(s_dr, 16)
                    sp.wait_ge(s_dr, (2 * i + half + 1) * (16 * HG))
                    sp.dma_start(dcol, dens.rearrange("h (p s) -> p h s", s=8)).then_inc(s_dc, 16)
                    wait("rd", half + 1)
                    sp.dma_start(rdens.rearrange("h (p s) -> p h s", s=8), dcol).then_inc(s_dw, 16)
                    sp.wait_ge(s_dw, (2 * i + half + 1) * 16)
                    for par in range(2):
                        sp.dma_start(rdb[64 * par:64 * par + 64, :, 0:L],
                                     rdens[par::2, 0:L].partition_broadcast(64)).then_inc(s_db, 16)
            sp.wait_ge(s_wh, 48 * (2 * B + 1))

        @block.gpsimd
        def _(pool):
            pool.memset(klo[:].bitcast(F32), 0.0)
            pool.memset(qlo[:].bitcast(F32), 0.0)
            pool.memset(qhi[:].bitcast(F32), 0.0)
            pool.memset(work[:], 0.0).then_inc(s_oz, 1)
            pool.wait_ge(s_oz, 1)
            with pool.Fori(0, B) as i:
                wait = waiter(pool, i)
                for u in range(2 * HG):
                    wait("cp2", u + 1)
                    pool.tensor_tensor(qlo[0:ONE, u % HG, 0:L], work[0:ONE, u % HG, 0:L],
                                       qhi[0:ONE, u % HG, 0:L].bitcast(F32), ALU.subtract).then_inc(sg["sp"], 1)

        def group_sets():
            for m, (gs, n) in enumerate(V_SETS):
                yield m, "v", gs, n
            for m, (gs, n) in enumerate(H_SETS):
                yield NV + m, "h", gs, n

        def tokens(view, side, g, n):
            if side == "v":
                return view[:, :, 1 + GRID * g:1 + GRID * g + n]
            return view[:, :, 1 + g:1 + g + GRID * (n - 1) + 1:GRID]

        def grid_rows(view, gs, n):
            lo = 1 + GRID * gs[0]
            return view[:, :, lo:lo + n * len(gs)].rearrange("p h (g n) -> p h g n", n=n)

        def relative_rows(eng, wait, half, par, copy, done):
            for m, side, gs, n in group_sets():
                wait("bg", half * NSET + m + 1)
                rows, at = (NVG + 1, RV) if side == "v" else (GRID + 1, RH)
                k = len(gs)
                dst = work[at:at + rows, par::2, :]
                src = t_banks[m % 4][32 * par:32 * par + rows, 0:k * NPR * n]
                if side == "v":
                    last = copy(grid_rows(dst, gs, n), src.rearrange("p (g h n) -> p h g n", h=NPR, n=n))
                else:
                    last = copy(grid_columns(dst, gs, n), src.rearrange("p (g h n) -> p h n g", h=NPR, n=n))
                last.then_inc(sg[done], 1)
            m = NSET - 1
            wait("bg", half * NSET + m + 1)
            copy(work[RV:RV + NVG + 1, par::2, 0], t_banks[m % 4][32 * par:32 * par + NVG + 1, 0:NPR])
            copy(work[RH:RH + GRID + 1, par::2, 0], t_banks[m % 4][32 * par:32 * par + GRID + 1, NPR:2 * NPR]
                 ).then_inc(sg[done], 1)

        def grid_columns(view, gs, n):
            return view[:, :, 1:1 + GRID * n].rearrange("p h (n g) -> p h n g", g=GRID)[:, :, :, gs[0]:gs[0] + len(gs)]

        @block.tensor
        def _(pe):
            pe.wait_ge(s_w, 16 * 5)
            pe.wait_ge(s_oz, 1)
            pe.wait_ge(s_og, 1)
            pe.wait_ge(s_oh, 32)

            def token_columns(i):
                wait = waiter(pe, i)
                for c in range(CH):
                    wait("nb", c + 1)
                    for k in range(2):
                        last = nc.tensor.transpose(xt_banks[c // 2][:, (2 * (c % 2) + k) * P:(2 * (c % 2) + k + 1) * P],
                                                   nb[:, c, 96 * k:96 * k + 96], ident[0:P, 0:P])
                    if c % 2:
                        last.then_inc(sg["xt"], 1)
                wait("xc", 3)

            def project(which, bank, half, pr, done):
                col = pr * 128
                for a in range(2):
                    for k in range(2):
                        last = nc.tensor.matmul(bank[:, a, 0:HALF], w[which][:, k, col:col + 128],
                                                hnT[:, k, a * HALF:(a + 1) * HALF], start=(k == 0), stop=(k == 1))
                last.then_inc(sg[done], 1)

            def keys(i, half):
                pe.wait_ge(s_wh, 96 * i + 48 * (half + 1))
                for pr in range(NPR):
                    project("k", k_banks[pr], half, pr, "kp")

            def turn(i, last_batch):
                wait = waiter(pe, i)
                for half in range(2):
                    u0 = half * HG
                    wait("ka", half * NPR + NPR)
                    wait("kd", half * NPR + NPR)
                    for pr in range(NPR):
                        project("q", q_banks[pr], half, pr, "qp")
                    wait("qa", half * NPR + NPR)
                    wait("qd", half * NPR + 2)

                    def bank_free(m):
                        if m == 2:
                            wait("qd", half * NPR + NPR)
                        if m >= 4:
                            wait("bga", half * NSET + m - 3)
                            wait("bgd", half * NSET + m - 3)

                    for m, side, gs, n in group_sets():
                        bank_free(m)
                        for a, g in enumerate(gs):
                            last = nc.tensor.matmul(t_banks[m % 4][0:64, a * NPR * n:(a + 1) * NPR * n],
                                                    (rqv if side == "v" else rqh)[:, g + 1, :],
                                                    tokens(pairs, side, g, n), start=True, stop=True)
                        last.then_inc(sg["bg"], 1)
                    m = NSET - 1
                    bank_free(m)
                    nc.tensor.matmul(t_banks[m % 4][0:64, 0:NPR], rqv[:, 0, :], pairs[:, :, 0], start=True, stop=True)
                    nc.tensor.matmul(t_banks[m % 4][0:64, NPR:2 * NPR], rqh[:, 0, :], pairs[:, :, 0], start=True,
                                     stop=True).then_inc(sg["bg"], 1)

                    def row_scores(u, c, bank):
                        for a in range(2):
                            last = nc.tensor.matmul(bank[0:P, a, 0:376],
                                                    qhi[0:ONE, u % HG, c * P:(c + 1) * P],
                                                    khi[0:ONE, u % HG, a * 374:a * 374 + 376],
                                                    start=True, stop=True)
                        last.then_inc(sg["m1"], 1)

                    def max_to_row(u, out):
                        wait("mx", (u + 1) * CH)
                        nc.tensor.transpose(out, nmx[:, u % 2, :], ident[0:P, 0:P]).then_inc(sg["mt"], 1)

                    def token_values(c):
                        if c >= 2:
                            wait("vd", half * CH + c - 1)
                        for k in range(2):
                            last = nc.tensor.matmul(psS[1][0:P, c % 2, 0:HG * HD], hnT[:, k, c * P:(c + 1) * P],
                                                    w["v"][:, k, :],
                                                    start=(k == 0), stop=(k == 1))
                        last.then_inc(sg["vp"], 1)

                    def scores(u, c):
                        wd = u * CH + c
                        if c == 0:
                            wait("sp", u + 1)
                            pe.wait_ge(s_md[u % 2], i * (96 * 6) + 96 * (u // 2 + 1))
                        if wd >= u0 * CH + 2:
                            wait("e", wd - 1)
                        at = slice(c * P, (c + 1) * P)
                        for x, (kk, qq) in enumerate(((khi, qhi), (khi, qlo), (klo, qhi))):
                            for a in range(2):
                                last = nc.tensor.matmul(psS[wd % 2][0:P, a, 0:HP], kk[:, u % HG, at],
                                                        qq[:, u % HG, a * HP:(a + 1) * HP], start=(x == 0),
                                                        stop=(x == 2))
                        last.then_inc(sg["s"], 1)

                    def values(u, c):
                        wd = u * CH + c
                        wait("lo", wd + 1)
                        if c == 0 and u > u0:
                            wait("o", u)
                        for a in range(2):
                            at = slice(a * HP, (a + 1) * HP)
                            nc.tensor.matmul(psO[:, a, 0:HP], vhi[:, c, u % HG, :], Phi[:, wd % 2, at],
                                             start=(c == 0), stop=False)
                            nc.tensor.matmul(psO[0:HD, a, 0:HP], vlo[:, c, u % HG, :], Phi[:, wd % 2, at],
                                             start=False, stop=False)
                            last = nc.tensor.matmul(psO[:, a, 0:HP], vhi[:, c, u % HG, :], Plo[:, wd % 2, at],
                                                    start=False, stop=(c == CH - 1))
                        last.then_inc(sg["av"], 1)

                    wait("qd", half * NPR + NPR)
                    for x in range(2 * CH):
                        if x % CH == 0:
                            wait("cp2", u0 + x // CH + 1)
                        if x >= 2:
                            wait("mx", u0 * CH + x - 1)
                        row_scores(u0 + x // CH, x % CH, (psM, psS[0])[x % 2])
                        if x % 2:
                            token_values(x // 2)
                        if x == CH:
                            max_to_row(u0, psO[0:CH, 0, 0:P])
                    max_to_row(u0 + 1, psO[0:CH, 1, 0:P])
                    scores(u0, 0)
                    wait("vd", (half + 1) * CH)
                    for wd in range(u0 * CH, (u0 + HG) * CH):
                        u, c = divmod(wd, CH)
                        if wd + 1 < (u0 + HG) * CH:
                            scores(*divmod(wd + 1, CH))
                        if u + 2 < u0 + HG:
                            if c == 0:
                                wait("cp2", u + 3)
                                wait("mr", u + 2)
                            wait("mx", (u + 2) * CH + c)
                            row_scores(u + 2, c, psM)
                        if wd > u0 * CH:
                            values(*divmod(wd - 1, CH))
                        if c == CH - 1 and u + 2 < u0 + HG:
                            max_to_row(u + 2, psM[0:CH, 0, 384:384 + P])
                    values(u0 + HG - 1, CH - 1)
                    wait("e", (half + 1) * 36)
                    if half == 0:
                        keys(i, 1)
                    elif not last_batch:
                        token_columns(i + 1)
                        keys(i + 1, 0)
                    ahead = half == 0 or not last_batch
                    wait("o", u0 + HG)

                    def out_bank(m):
                        return rv_banks[m % 4]

                    def bank_done(m):
                        if ahead and m == 2:
                            wait("ka", half * NPR + NPR + 1)
                            wait("kd", half * NPR + NPR + 1)
                        if m >= 4:
                            k = m - 4
                            if k < NV:
                                wait("rga", half * NV + k + 1)
                            else:
                                wait("rgd", half * (NHS + 1) + k - NV + 1)

                    for m, side, gs, n in group_sets():
                        bank_done(m)
                        for a, g in enumerate(gs):
                            for par in range(2):
                                last = nc.tensor.matmul(
                                    out_bank(m)[64 * par:64 * par + 64, a * NPR * n:(a + 1) * NPR * n],
                                    (rvv if side == "v" else rvh)[:, g + 1, :],
                                    tokens(work[:, par::2, :], side, g, n), start=True, stop=True)
                        last.then_inc(sg["rg"], 1)
                    m = NSET - 1
                    bank_done(m)
                    for par in range(2):
                        for x, table in enumerate((rvv, rvh)):
                            last = nc.tensor.matmul(out_bank(m)[64 * par:64 * par + 64, 0:NPR], table[:, 0, :],
                                                    work[:, par::2, 0], start=(x == 0), stop=(x == 1))
                    last.then_inc(sg["rg"], 1)
                    pe.wait_ge(s_wp, 32 * i + 16 * (half + 1))
                    if ahead:
                        wait("ka", half * NPR + 2 * NPR)
                        wait("kd", half * NPR + 2 * NPR)
                    for c in range(CH):
                        wait("nm", half * CH + c + 1)
                        if c >= 2:
                            wait("g", half * CH + c - 1)
                        for pr in range(NPR):
                            last = nc.tensor.matmul(psM[0:P, c % 2, 0:E], pairs[:, pr, c * P:(c + 1) * P],
                                                    wp[:, pr, :], start=(pr == 0), stop=(pr == NPR - 1))
                        last.then_inc(sg["pr"], 1)

            token_columns(0)
            keys(0, 0)
            with pe.Fori(0, B - 1) as i:
                turn(i, False)
            turn(B - 1, True)

        @block.scalar
        def _(act):
            act.wait_ge(s_ln, 1)
            nc.scalar.activation(rstd[:], rstd[:], ACT.Sqrt).then_inc(s_sd, 1)
            act.wait_ge(s_oh, 32)
            for hh in range(HG):
                nc.scalar.activation(khi[64:128, hh, :], oh, ACT.Copy)
                last = nc.scalar.activation(vhi[:, :, hh, 64:128], ohT, ACT.Copy)
            last.then_inc(s_og, 1)

            def token_columns(i):
                wait = waiter(act, i)
                for g in range(3):
                    wait("xt", g + 1)
                    nc.scalar.activation(
                        hnT[:, :, 2 * g * P:2 * (g + 1) * P].rearrange("d k (c p) -> d c k p", p=P),
                        xt_banks[g][:, 0:4 * P].rearrange("d (c k p) -> d c k p", c=2, k=2), ACT.Copy
                        ).then_inc(sg["xc"], 1)

            def keys(i, half):
                wait = waiter(act, i)
                for pr in range(NPR):
                    wait("kp", half * NPR + pr + 1)
                    for par in range(2):
                        last = nc.scalar.activation(
                            khi[0:64, 2 * pr + par, :].rearrange("p (a l) -> p a l", a=2),
                            k_banks[pr][64 * par:64 * par + 64, :, 0:HALF], ACT.Copy)
                    last.then_inc(sg["ka"], 1)

            def turn(i, last_batch):
                wait = waiter(act, i)
                for half in range(2):
                    u0 = half * HG
                    for pr in range(NPR):
                        wait("qp", half * NPR + pr + 1)
                        nc.scalar.activation(pairs[:, pr, 0:L].rearrange("p (a l) -> p a l", a=2),
                                             q_banks[pr][:, :, 0:HALF], ACT.Copy).then_inc(sg["qa"], 1)
                    relative_rows(act, wait, half, 0, lambda o, x: nc.scalar.activation(o, x, ACT.Copy), "bga")
                    wait("bga", (half + 1) * NSET)
                    wait("bgd", (half + 1) * NSET)
                    wait("qd", half * NPR + NPR)
                    for hh in range(HG):
                        nc.scalar.activation(qhi[0:ONE, hh, 0:L], work[0:ONE, hh, 0:L], ACT.Copy
                                             ).then_inc(sg["cp2"], 1)
                    for c in range(CH):
                        wait("vp", half * CH + c + 1)
                        nc.scalar.activation(vhi[:, c, :, 0:64],
                                             psS[1][0:P, c % 2, 0:HG * HD].rearrange("p (h d) -> p h d", d=HD),
                                             ACT.Copy).then_inc(sg["vc"], 1)
                    for u in range(u0, u0 + HG):
                        for c in range(CH):
                            wd = u * CH + c
                            wait("s", wd + 1)
                            if wd >= u0 * CH + 2:
                                wait("av", wd - 1)
                            for to in (Phi, PT):
                                last = nc.scalar.activation(to[:, wd % 2, :].rearrange("p (a l) -> p a l", a=2),
                                                            psS[wd % 2][0:P, :, 0:HP], ACT.Exp, scale=SCALE)
                            last.then_inc(sg["e"], 1)
                    if half == 0:
                        keys(i, 1)
                    elif not last_batch:
                        token_columns(i + 1)
                        keys(i + 1, 0)
                    for m, (gs, n) in enumerate(V_SETS):
                        wait("rg", half * NSET + m + 1)
                        k = len(gs)
                        nc.scalar.activation(
                            grid_rows(pairs, gs, n),
                            rv_banks[m % 4][:, 0:k * NPR * n].rearrange("p (g h n) -> p h g n", h=NPR, n=n),
                            ACT.Copy).then_inc(sg["rga"], 1)

            token_columns(0)
            keys(0, 0)
            with act.Fori(0, B - 1) as i:
                turn(i, False)
            turn(B - 1, True)

        @block.vector
        def _(dve):
            v = nc.vector
            link = Chain(dve, s_v)
            for t in range(NT):
                v.bn_stats(st[:, t, :], h[:, t, :]).then_inc(s_v, 1)
            link.n += NT
            dve.wait_ge(s_v, link.n)
            for t in range(NT):
                v.bn_aggr(mv_[:, t, :], st[:, t, :]).then_inc(s_v, 1)
            link.n += NT
            dve.wait_ge(s_v, link.n)
            link(v.tensor_copy(mean[:], mv_[:, :, 0]))
            v.tensor_scalar(rstd[:], mv_[:, :, 1], EPS, None, ALU.add).then_inc(s_ln, 1)
            dve.wait_ge(s_sd, 1)
            link(v.reciprocal(rstd[:], rstd[:]))
            dve.wait_ge(s_w, 16 * 5)
            dve.wait_ge(s_og, 1)
            dve.wait_ge(s_oz, 1)

            def normalise(i):
                for c in range(CH):
                    t = i * CH + c
                    v.tensor_scalar(nb[:, c, :], h[:, bass.ds(t, 1), :].rearrange("p o e -> p (o e)"),
                                    mean[:, bass.ds(t, 1)], rstd[:, bass.ds(t, 1)], ALU.subtract,
                                    ALU.mult).then_inc(sg["nb"], 1)
                waiter(dve, i)("nb", CH)
                hb = h[:, bass.ds(i * CH, CH), :]
                v.tensor_tensor(hb, hb, bp[:].unsqueeze(1).broadcast_to([P, CH, E]), ALU.add).then_inc(s_bp, 1)

            def keys(i, half):
                wait = waiter(dve, i)
                for pr in range(NPR):
                    wait("ka", half * NPR + pr + 1)
                    for par in range(2):
                        last = v.tensor_tensor(
                            klo[0:64, 2 * pr + par, :].rearrange("p (a l) -> p a l", a=2),
                            k_banks[pr][64 * par:64 * par + 64, :, 0:HALF],
                            khi[0:64, 2 * pr + par, :].bitcast(F32).rearrange("p (a l) -> p a l", a=2),
                            ALU.subtract)
                    last.then_inc(sg["kd"], 1)

            def turn(i, last_batch):
                wait = waiter(dve, i)
                for half in range(2):
                    u0 = half * HG
                    for pr in range(NPR):
                        wait("qa", half * NPR + pr + 1)
                        for par in range(2):
                            last = v.tensor_copy(work[0:64, 2 * pr + par, 0:L], pairs[64 * par:64 * par + 64, pr, 0:L])
                        last.then_inc(sg["qd"], 1)
                    relative_rows(dve, wait, half, 1, lambda o, x: v.tensor_copy(o, x), "bgd")

                    def maxima(u, c, bank):
                        wait("m1", u * CH + c + 1)
                        v.tensor_reduce(nmx[:, u % 2, c:c + 1], bank[0:P, :, 0:376], AX.XY, ALU.max,
                                        negate=True).then_inc(sg["mx"], 1)

                    def to_row(u, src):
                        wait("mt", u + 1)
                        v.tensor_copy(mrow[:, u % 2, :], src).then_inc(sg["mr"], 1)

                    for x in range(2 * CH):
                        maxima(u0 + x // CH, x % CH, (psM, psS[0])[x % 2])
                        if x == CH:
                            to_row(u0, psO[0:CH, 0, 0:P])
                        if x % 2:
                            c = x // 2
                            wait("vc", half * CH + c + 1)
                            v.tensor_tensor(vlo[:, c, :, :],
                                            psS[1][0:P, c % 2, 0:HG * HD].rearrange("p (h d) -> p h d", d=HD),
                                            vhi[:, c, :, 0:64].bitcast(F32), ALU.subtract).then_inc(sg["vd"], 1)
                    to_row(u0 + 1, psO[0:CH, 1, 0:P])
                    def output(u):
                        wait("av", (u + 1) * CH)
                        v.tensor_copy(work[:, u % HG, 0:LP].rearrange("p (a l) -> p a l", a=2), psO[:, :, 0:HP]
                                      ).then_inc(sg["o"], 1)

                    for u in range(u0, u0 + HG):
                        if half == 1 and not last_batch and u == u0 + HG - 2:
                            normalise(i + 1)
                        for c in range(CH):
                            if u + 2 < u0 + HG:
                                if c == 0:
                                    dve.wait_ge(s_md[u % 2], i * (96 * 6) + 96 * (u // 2 + 1))
                                maxima(u + 2, c, psM)
                            wd = u * CH + c
                            wait("e", wd + 1)
                            v.tensor_tensor(Plo[:, wd % 2, :], PT[:, wd % 2, :], Phi[:, wd % 2, :].bitcast(F32),
                                            ALU.subtract).then_inc(sg["lo"], 1)
                            if c == 0 and u > u0:
                                output(u - 1)
                        if u + 2 < u0 + HG:
                            to_row(u + 2, psM[0:CH, 0, 384:384 + P])
                    output(u0 + HG - 1)
                    if half == 0:
                        keys(i, 1)
                    elif not last_batch:
                        keys(i + 1, 0)
                    dve.wait_ge(s_dc, (2 * i + half + 1) * 16)
                    v.reciprocal(dcol, dcol).then_inc(sg["rd"], 1)
                    wait("rga", (half + 1) * NV)
                    for m, (gs, n) in enumerate(H_SETS):
                        mm = NV + m
                        wait("rg", half * NSET + mm + 1)
                        k = len(gs)
                        dst = grid_columns(pairs, gs, n)
                        v.tensor_tensor(dst, dst, rv_banks[mm % 4][:, 0:k * NPR * n].rearrange(
                            "p (g h n) -> p h n g", h=NPR, n=n), ALU.add).then_inc(sg["rgd"], 1)
                    mm = NSET - 1
                    wait("rg", half * NSET + mm + 1)
                    v.tensor_copy(pairs[:, :, 0], rv_banks[mm % 4][:, 0:NPR]).then_inc(sg["rgd"], 1)
                    wait("rgd", (half + 1) * (NHS + 1))
                    dve.wait_ge(s_db, (2 * i + half + 1) * 32)
                    for c in range(CH):
                        at = slice(c * P, (c + 1) * P)
                        v.tensor_tensor(pairs[:, :, at], pairs[:, :, at], rdb[:, :, at], ALU.mult
                                        ).then_inc(sg["nm"], 1)
                    dve.wait_ge(s_bp, i + 1)
                    for c in range(CH):
                        wait("pr", half * CH + c + 1)
                        if half == 1:
                            wait("g", c + 1)
                        hc = h[:, bass.ds(i * CH + c, 1), :].rearrange("p o e -> p (o e)")
                        v.tensor_tensor(hc, hc, psM[0:P, c % 2, 0:E], ALU.add).then_inc(sg["g"], 1)
                    wait("g", (half + 1) * CH)

            normalise(0)
            keys(0, 0)
            with dve.Fori(0, B - 1) as i:
                turn(i, False)
            turn(B - 1, True)


def host_inputs(i):
    sel, xy, merge, one9 = moment_constants()
    t = np.ascontiguousarray
    f = {k: np.asarray(v) for k, v in i.items()}
    return {
        "x": f["x"],
        "wt": conv_weights([f[f"L0_tok_w_t{k}"] for k in KS], [f[f"L0_tok_b_t{k}"] for k in KS]),
        "wc": conv_weights([f[f"L0_tok_w_c{k}"] for k in KS], [f[f"L0_tok_b_c{k}"] for k in KS]),
        "Wq0T": t(f["L0_attn_Wq"].T), "Wk0T": t(f["L0_attn_Wk"].T), "Wv0T": t(f["L0_attn_Wv"].T),
        "Wo0T": t(f["L0_attn_Wo"].T),
        "sel": sel, "selxy": xy, "merge": merge, "one9": one9,
        **moe_inputs(f),
        **relative_inputs(f),
    }


def build(nc, A, out):
    ctx = ExitStack()
    with ctx:
        h = ctx.enter_context(nc.sbuf_tensor("h", [P, NT, E], F32))
        ident = ctx.enter_context(nc.sbuf_tensor("ident", [128, 128], F32))
        for run in (lambda keep: token_mixer_and_attention(nc, keep, A, h, ident),
                    lambda keep: moe(nc, keep, A, h, ident, MOE0, None),
                    lambda keep: window_attention(nc, keep, A, h, ident)):
            stage = Stage(nc)
            run(stage)
            stage.close()
        moe(nc, ctx, A, h, ident, MOE1, out)


def kernel(**inputs):
    import concourse.bacc as bacc
    from concourse.bass_utils import run_bass_kernel_spmd

    nc = bacc.Bacc("TRN2", target_bir_lowering=False, num_devices=1)
    arrays, A = {}, {}
    for name, a in host_inputs(inputs).items():
        a = np.ascontiguousarray(a)
        arrays[f"in_{name}"] = a
        A[name] = nc.dram_tensor(f"in_{name}", a.shape, mybir.dt.from_np(a.dtype), kind="ExternalInput").ap()
    out = nc.dram_tensor("out_0", (B, L, E), F32, kind="ExternalOutput").ap()
    build(nc, A, out)
    r = run_bass_kernel_spmd(nc, [arrays], core_ids=[0])
    return r.results[0]["out_0"]
```

```python
import itertools

import numpy as np

import concourse.bass as bass
from concourse import mybir
from contextlib import ExitStack

F32 = mybir.dt.float32
F32R = mybir.dt.float32r
I32 = mybir.dt.int32
U32 = mybir.dt.uint32
ALU = mybir.AluOpType
ACT = mybir.ActivationFunctionType
AX = mybir.AxisListType

B, D, L = 4, 64, 750
KS = (3, 5, 7)
E = len(KS) * D
CH, P = 6, 125
NT = B * CH
H0, FEAT = 12, 16
EPS = 1e-5
HALF = L // 2

MONO = [()] + [(a,) for a in range(3)] + list(itertools.combinations_with_replacement(range(3), 2)) \
    + list(itertools.combinations_with_replacement(range(3), 3))
MI = {m: i for i, m in enumerate(MONO)}
NM = len(MONO)
FEATS = [(a, m) for a in MONO if len(a) == 2 for m in MONO if len(m) == 3] \
    + [(a, m) for a in MONO if len(a) == 1 for m in MONO if len(m) == 2] \
    + [((), m) for m in MONO if len(m) == 1] \
    + [(a, m) for a in MONO if len(a) == 2 for m in MONO if len(m) == 2] \
    + [(a, m) for a in MONO if len(a) == 1 for m in MONO if len(m) == 1] + [((), ())]
FI = {f: i for i, f in enumerate(FEATS)}
NF = len(FEATS)
ROWS = [(a, b, c, d) for a in range(3) for b in range(3) for c in range(3) for d in range(3)] \
    + [(a, b) for a in range(3) for b in range(3)] + [()]
NR = len(ROWS)


def moment_constants():
    sel = np.zeros((128, B, 2, NF), np.float32)
    for b in range(B):
        for f, (a, m) in enumerate(FEATS):
            sel[32 * b + MI[a], b, 0, f] = 1.0
            sel[32 * b + MI[m], b, 1, f] = 1.0
    xy = np.zeros((128, B, 2, NR), np.float32)
    merge = np.zeros((NR, 4, NF), np.float32)
    for r, row in enumerate(ROWS):
        ab = [row[0:2], row[2:4]]
        for side in range(2):
            j = 3 * ab[side][0] + ab[side][1] if ab[side] else 9
            for b in range(B):
                xy[32 * b + j, b, side, r] = 1.0
        left = tuple(sorted(row[0::2]))
        right = row[1::2]
        w = 0.5 if len(row) == 4 else 1.0
        for i in range(3):
            merge[r, i, FI[(left, tuple(sorted(right + (i,))))]] += w
        merge[r, 3, FI[(left, tuple(sorted(right)))]] += w
    one9 = np.zeros((128, 1), np.float32)
    one9[9::32] = 1.0
    return sel, xy, merge, one9


def conv_weights(w, b):
    out = np.zeros((17, 7, 4, 3), w[0].dtype)
    for k, width in enumerate(KS):
        at = 3 - width // 2
        for i in range(B):
            out[4 * i:4 * i + 4, at:at + width, i, k] = w[k][0]
        out[16, 3, :, k] = b[k][0]
    return out.reshape(17, 7, 12)


class Chain:

    def __init__(self, eng, sem):
        self.eng, self.sem, self.n = eng, sem, 0

    def __call__(self, ins):
        self.n += 1
        ins.then_inc(self.sem, 1)
        self.eng.wait_ge(self.sem, self.n)


class Stage:

    def __init__(self, nc):
        self.nc, self.stack, self.all = nc, ExitStack(), []

    def enter_context(self, semaphore):
        self.all.append(self.stack.enter_context(semaphore))
        return self.all[-1]

    def close(self):
        with self.nc.Block() as block:
            @block.gpsimd
            def _(pool):
                for s in self.all:
                    pool.sem_clear(s)
        self.stack.close()


def token_mixer_and_attention(nc, keep, A, h, ident):
    ctx = ExitStack()
    with ctx:
        def sb(name, shape, dt=F32):
            return ctx.enter_context(nc.sbuf_tensor(name, shape, dt))

        def sem(name):
            return keep.enter_context(nc.semaphore(name))

        xd = sb("xd", [D, B, L])
        xT = sb("xT", [P, CH, B, D])
        xc = sb("xc", [P, CH, B, D])
        wt = sb("wt", [17, 7, 12])
        wc = sb("wc", [17, 7, 12])
        wqk = sb("wqk", [128, 2, 2, E])
        wv = sb("wv", [128, 2, E])
        wo = sb("wo", [96, 2, E])
        sel = sb("sel", [128, B, 2, NF])
        selxy = sb("selxy", [128, B, 2, NR])
        merge = sb("merge", [NR, 4, NF])
        one9 = sb("one9", [128, 1])
        statT = sb("statT", [P, CH, 17])
        statC = sb("statC", [D, 17])
        smean = sb("smean", [D, B])
        nmean = sb("nmean", [D, B])
        ssq = sb("ssq", [D, B])
        mtok = sb("mtok", [P, NT])
        sqd = sb("sqd", [D, L])
        poolT = sb("poolT", [17, L + 6])
        poolC = sb("poolC", [17, D + 6])
        wgtT = sb("wgtT", [P, CH, 12])
        wgtC = sb("wgtC", [D, 12])
        ones64 = sb("ones64", [D, 128])
        rt = sb("rt", [D, 12])
        rtc = sb("rtc", [D, 2, 12])
        bm = sb("bm", [128, 2, 12])
        v0 = sb("v0", [128, B])
        rc = sb("rc", [P, B, CH, 3])
        hm = sb("hm", [P, B, CH, 3])
        ak = sb("ak", [P, B, CH, 3])
        aq = sb("aq", [P, B, CH, 3])
        m1 = sb("m1", [P, B, CH])
        rs = sb("rs", [P, B, CH])
        phi = sb("phi", [P, CH, B, 32])
        phiT = sb("phiT", [128, L])
        ones = sb("ones", [128, L])
        S = sb("S", [128, L])
        basis = sb("basis", [D, 3, B, 3])
        qku = sb("qku", [128, 2, 2, B, 32])
        vu = sb("vu", [128, 2, B, 3, NR])
        qs = sb("qs", [128, E])
        qk = sb("qk", [128, E])
        Mx = sb("Mx", [128, H0])
        xs = sb("xs", [NR, H0])
        T2 = sb("T2", [NR, B, H0])
        T3 = sb("T3", [NR, 3, E])
        C = sb("C", [NF, B, E + H0])
        G1 = sb("G1", [NF, L])
        Ft = sb("Ft", [NF, B, L])
        diag = sb("diag", [D, 12, D])
        u0row = sb("u0row", [P, B, E])
        rden = sb("rden", [P, 2, H0])
        yn = sb("yn", [P, 2, E])
        yT = sb("yT", [96, 2, 2, P])
        ps = [ctx.enter_context(nc.psum_tensor(f"psA{i}", [128, 512], F32)) for i in range(8)]

        s_x, s_w, s_cst = sem("s_x"), sem("s_w"), sem("s_cst")
        s_id = sem("s_id")
        s_a, s_v, s_g = sem("s_a"), sem("s_v"), sem("s_g")
        s_xt, s_xtc = sem("s_xt"), sem("s_xtc")
        s_mean, s_var = sem("s_mean"), sem("s_var")
        s_std, s_sd = sem("s_std"), sem("s_sd")
        s_stat, s_statT, s_pool = sem("s_stat"), sem("s_statT"), sem("s_pool")
        s_conv, s_wgt, s_rows, s_rowc = sem("s_conv"), sem("s_wgt"), sem("s_rows"), sem("s_rowc")
        s_bm, s_usq, s_v0, s_phi, s_phiT, s_phic, s_S = (sem(n) for n in (
            "s_bm", "s_usq", "s_v0", "s_phi", "s_phiT", "s_phic", "s_S"))
        s_basis, s_qk, s_Mx, s_xy = (sem(n) for n in ("s_basis", "s_qk", "s_Mx", "s_xy"))
        s_vps, s_T3, s_C, s_Cc = sem("s_vps"), sem("s_T3"), sem("s_C"), sem("s_Cc")
        s_G, s_Gc, s_F = sem("s_G"), sem("s_Gc"), sem("s_F")
        s_u0, s_u0c = sem("s_u0"), sem("s_u0c")
        s_y, s_yn, s_yt, s_ytc, s_o, s_h = (sem(n) for n in ("s_y", "s_yn", "s_yt", "s_ytc", "s_o", "s_h"))
        block = ctx.enter_context(nc.Block())

        @block.sync
        def _(sp):
            for b in range(B):
                sp.dma_start(xd[:, b, :], A["x"][b]).then_inc(s_x, 16)
            sp.dma_start(wt[:], A["wt"]).then_inc(s_w, 16)
            sp.dma_start(wc[:], A["wc"]).then_inc(s_w, 16)
            sp.dma_start(sel[:], A["sel"]).then_inc(s_w, 16)
            sp.dma_start(selxy[:], A["selxy"]).then_inc(s_w, 16)
            sp.dma_start(merge[:], A["merge"]).then_inc(s_w, 16)
            sp.dma_start(one9[:], A["one9"]).then_inc(s_w, 16)
            sp.dma_start(wo[:], A["Wo0T"].rearrange("(k f) e -> f k e", f=96)).then_inc(s_w, 16)
            sp.wait_ge(s_g, 2)
            for to, k in ((wqk[:, 0], "Wq0T"), (wqk[:, 1], "Wk0T"), (wv, "Wv0T")):
                sp.dma_start(to[:, 0, :], A[k][0:128, :]).then_inc(s_w, 16)
                sp.dma_start(to[0:D, 1, :], A[k][128:E, :]).then_inc(s_w, 16)
            sp.wait_ge(s_x, 64)
            sp.wait_ge(s_w, 208)

        @block.gpsimd
        def _(pool):
            pool.memset(ident[:], 0.0).then_inc(s_g, 1)
            pool.wait_ge(s_g, 1)
            pool.affine_select(out=ident[:], in_=ident[:], compare_op=ALU.not_equal, fill=1.0, base=0,
                               pattern=[[-1, 128]], channel_multiplier=1).then_inc(s_id, 1)
            pool.memset(statT[:], 1.0)
            pool.memset(statC[:], 1.0)
            pool.memset(poolT[:], 0.0)
            pool.memset(poolC[:], 0.0)
            pool.memset(ones64[:], 1.0 / D)
            pool.memset(ones[:], 1.0)
            pool.memset(phi[:], 0.0)
            pool.memset(qku[:], 0.0)
            pool.memset(vu[:, 1], 0.0)
            pool.memset(wqk[:, :, 1, :], 0.0)
            pool.memset(wv[:, 1, :], 0.0)
            pool.memset(basis[:], 0.0).then_inc(s_g, 1)
            pool.wait_ge(s_g, 2)
            pool.memset(phi[:, :, :, 0:1], 1.0)
            pool.memset(basis[:, 0, :, 1:2], 1.0)
            pool.memset(basis[:, 1, :, 2:3], 1.0)
            pool.memset(basis[:, 2, :, 1:3], -1.0).then_inc(s_cst, 1)

        @block.tensor
        def _(pe):
            pe.wait_ge(s_x, 16 * B)
            pe.wait_ge(s_id, 1)
            for c in range(CH):
                for b in range(B):
                    g = c * B + b
                    last = nc.tensor.transpose(ps[g // 8][0:P, (g % 8) * D:(g % 8 + 1) * D],
                                               xd[:, b, c * P:(c + 1) * P], ident[0:D, 0:D])
                    if g % 8 == 7:
                        last.then_inc(s_xt, 1)
            pe.wait_ge(s_stat, 2)
            for c in range(CH):
                nc.tensor.transpose(ps[3 + c // 4][0:17, (c % 4) * P:(c % 4 + 1) * P], statT[:, c, :],
                                    ident[0:P, 0:P])
            nc.tensor.transpose(ps[5][0:17, 0:D], statC[:], ident[0:D, 0:D]).then_inc(s_statT, 1)
            pe.wait_ge(s_w, 208)
            pe.wait_ge(s_pool, 1)
            for c in range(CH):
                for t in range(7):
                    nc.tensor.matmul(ps[6][0:P, 12 * c:12 * c + 12], poolT[:, c * P + t:c * P + t + P], wt[:, t, :],
                                     start=(t == 0), stop=(t == 6))
            for t in range(7):
                last = nc.tensor.matmul(ps[7][0:D, 0:12], poolC[:, t:t + D], wc[:, t, :],
                                        start=(t == 0), stop=(t == 6))
            last.then_inc(s_conv, 1)
            pe.wait_ge(s_wgt, 1)
            for b in range(B):
                for c in range(CH):
                    nc.tensor.matmul(ps[0][0:D, 3 * b:3 * b + 3], xT[:, c, b, :], wgtT[:, c, 3 * b:3 * b + 3],
                                     start=(c == 0), stop=(c == CH - 1))
            for b in range(B):
                for c in range(CH):
                    at = 3 * (b * CH + c)
                    last = nc.tensor.matmul(ps[1][0:P, at:at + 3], xd[:, b, c * P:(c + 1) * P],
                                            wgtC[:, 3 * b:3 * b + 3], start=True, stop=True)
            last.then_inc(s_rows, 1)
            pe.wait_ge(s_rowc, 1)
            pe.wait_ge(s_cst, 1)
            nc.tensor.matmul(ps[2][:, 0:12], ones64[:], rt[:], start=True, stop=True).then_inc(s_bm, 1)
            pe.wait_ge(s_usq, 1)
            nc.tensor.matmul(ps[3][:, 0:12], ones64[:], rtc[:, 1, :], start=True, stop=True).then_inc(s_v0, 1)
            pe.wait_ge(s_basis, 1)
            for j in range(2):
                for k in range(2):
                    last = nc.tensor.matmul(ps[4 + j][:, 0:E], qku[:, j, k, :, :].rearrange("d b r -> d (b r)"),
                                            wqk[:, j, k, :], start=(k == 0), stop=(k == 1))
            last.then_inc(s_qk, 1)
            for b in range(B):
                for k in range(3):
                    bank = 6 + b // 2
                    last = nc.tensor.matmul(ps[bank][0:P, (b % 2) * E + k * D:(b % 2) * E + (k + 1) * D],
                                            ones[0:D, 0:P], diag[:, 3 * b + k, :], start=True, stop=True)
            last.then_inc(s_u0, 1)
            pe.wait_ge(s_phi, 1)
            for c in range(CH):
                last = nc.tensor.transpose(ps[c // 4][:, (c % 4) * P:(c % 4 + 1) * P],
                                           phi[:, c, :, :].rearrange("p b s -> p (b s)"), ident[0:P, 0:P])
            last.then_inc(s_phiT, 1)
            pe.wait_ge(s_Mx, 1)
            for b in range(B):
                for side in range(2):
                    last = nc.tensor.matmul(ps[4 + side][0:NR, b * H0:(b + 1) * H0], selxy[:, b, side, :],
                                            Mx[:], start=True, stop=True)
            last.then_inc(s_xy, 1)
            for b in range(B):
                if b >= 1:
                    pe.wait_ge(s_T3, b)
                else:
                    pe.wait_ge(s_phic, 1)
                    pe.wait_ge(s_u0c, 1)
                for i in range(3):
                    bank = (2, 3, 6)[i]
                    for k in range(2):
                        last = nc.tensor.matmul(ps[bank][0:NR, 0:E], vu[:, k, b, i, :], wv[:, k, :],
                                                start=(k == 0), stop=(k == 1))
                last.then_inc(s_vps, 1)
                pe.wait_ge(s_T3, b + 1)
                if b >= 1:
                    pe.wait_ge(s_Cc, b)
                for i in range(3):
                    nc.tensor.matmul(ps[7][0:NF, 0:E], merge[:, i, :], T3[:, i, :], start=(i == 0), stop=(i == 2))
                nc.tensor.matmul(ps[7][0:NF, E:E + H0], merge[:, 3, :], T2[:, b, :], start=True,
                                 stop=True).then_inc(s_C, 1)
            pe.wait_ge(s_S, 1)
            for b in range(B):
                if b >= 1:
                    pe.wait_ge(s_Gc, b)
                    pe.wait_ge(s_F, b)
                for f in range(2):
                    for n in range(2):
                        last = nc.tensor.matmul(ps[2 * f + n][0:NF, 0:HALF], sel[:, b, f, :],
                                                (phiT if f == 0 else S)[:, n * HALF:(n + 1) * HALF],
                                                start=True, stop=True)
                    if f == 1:
                        last.then_inc(s_G, 1)
            pe.wait_ge(s_Cc, B)
            pe.wait_ge(s_F, B)

            for t in range(NT + 2):
                if t < NT:
                    b, c = divmod(t, CH)
                    if t >= 2:
                        pe.wait_ge(s_yn, t - 1)
                    nc.tensor.matmul(ps[t % 2][0:P, 0:E + H0], Ft[:, b, c * P:(c + 1) * P], C[:, b, :],
                                     start=True, stop=True).then_inc(s_y, 1)
                if 1 <= t <= NT:
                    u = t - 1
                    pe.wait_ge(s_yn, u + 1)
                    if u >= 2:
                        pe.wait_ge(s_ytc, u - 1)
                    for k in range(2):
                        last = nc.tensor.transpose(ps[6 + u % 2][0:96, k * P:(k + 1) * P],
                                                   yn[:, u % 2, 96 * k:96 * k + 96], ident[0:P, 0:P])
                    last.then_inc(s_yt, 1)
                if t >= 2:
                    u = t - 2
                    pe.wait_ge(s_ytc, u + 1)
                    if u >= 2:
                        pe.wait_ge(s_h, u - 1)
                    for k in range(2):
                        last = nc.tensor.matmul(ps[4 + u % 2][0:P, 0:E], yT[:, u % 2, k, :], wo[:, k, :],
                                                start=(k == 0), stop=(k == 1))
                    last.then_inc(s_o, 1)

        @block.scalar
        def _(act):
            link = Chain(act, s_a)
            for g in range(3):
                act.wait_ge(s_xt, g + 1)
                nc.scalar.activation(xT[:].rearrange("p c b d -> p (c b d)")[:, g * 512:(g + 1) * 512],
                                     ps[g][0:P, :], ACT.Copy).then_inc(s_xtc, 1)
            act.wait_ge(s_mean, 1)
            for b in range(B):
                link(nc.scalar.activation(sqd[:], xd[:, b, :], ACT.Square, bias=nmean[:, b:b + 1],
                                          accum_out=ssq[:, b:b + 1]))
            act.wait_ge(s_cst, 1)
            nc.scalar.activation(statC[:, 1:16:4], ssq[:], ACT.Sqrt, scale=1.0 / (L - 1)).then_inc(s_stat, 1)
            act.wait_ge(s_var, 1)
            nc.scalar.activation(statT[:, :, 1:16:4], m1[:].rearrange("p b c -> p (b c)").rearrange(
                "p (c b) -> p c b", b=B), ACT.Sqrt, scale=1.0 / (D - 1)).then_inc(s_std, 1)
            act.wait_ge(s_statT, 1)
            nc.scalar.activation(poolT[:, 3:3 + 4 * P], ps[3][0:17, 0:4 * P], ACT.Copy)
            nc.scalar.activation(poolT[:, 3 + 4 * P:3 + L], ps[4][0:17, 0:2 * P], ACT.Copy)
            nc.scalar.activation(poolC[:, 3:3 + D], ps[5][0:17, 0:D], ACT.Copy).then_inc(s_pool, 1)
            act.wait_ge(s_conv, 1)
            nc.scalar.activation(wgtT[:].rearrange("p c k -> p (c k)"), ps[6][0:P, 0:72], ACT.Relu)
            nc.scalar.activation(wgtC[:], ps[7][0:D, 0:12], ACT.Relu).then_inc(s_wgt, 1)
            act.wait_ge(s_var, 2)
            nc.scalar.activation(rs[:], rs[:], ACT.Sqrt).then_inc(s_std, 1)
            act.wait_ge(s_phiT, 1)
            nc.scalar.activation(phiT[:, 0:4 * P], ps[0][:, 0:4 * P], ACT.Copy)
            nc.scalar.activation(phiT[:, 4 * P:L], ps[1][:, 0:2 * P], ACT.Copy).then_inc(s_phic, 1)
            act.wait_ge(s_u0, 1)
            nc.scalar.activation(u0row[:, 0:2, :].rearrange("p b e -> p (b e)"), ps[6][0:P, 0:2 * E], ACT.Copy)
            nc.scalar.activation(u0row[:, 2:4, :].rearrange("p b e -> p (b e)"), ps[7][0:P, 0:2 * E],
                                 ACT.Copy).then_inc(s_u0c, 1)
            for b in range(B):
                act.wait_ge(s_C, b + 1)
                nc.scalar.activation(C[:, b, :], ps[7][0:NF, 0:E + H0], ACT.Copy).then_inc(s_Cc, 1)
            for b in range(B):
                act.wait_ge(s_G, b + 1)
                if b >= 1:
                    act.wait_ge(s_F, b)
                for n in range(2):
                    last = nc.scalar.activation(G1[:, n * HALF:(n + 1) * HALF], ps[n][0:NF, 0:HALF], ACT.Copy)
                last.then_inc(s_Gc, 1)
            for t in range(NT):
                act.wait_ge(s_yt, t + 1)
                if t >= 2:
                    act.wait_ge(s_o, t - 1)
                nc.scalar.activation(yT[:, t % 2, :, :].rearrange("f k p -> f (k p)"), ps[6 + t % 2][0:96, 0:2 * P],
                                     ACT.Copy).then_inc(s_ytc, 1)

        @block.vector
        def _(dve):
            v = nc.vector
            link = Chain(dve, s_v)
            dve.wait_ge(s_x, 16 * B)
            dve.wait_ge(s_cst, 1)
            link(v.tensor_reduce(smean[:], xd[:], AX.X, ALU.add))
            v.tensor_scalar(nmean[:], smean[:], -1.0 / L, None, ALU.mult).then_inc(s_mean, 1)
            v.tensor_scalar(statC[:, 0:16:4], smean[:], 1.0 / L, None, ALU.mult)
            v.tensor_reduce(statC[:, 2:16:4], xd[:], AX.X, ALU.max)
            link(v.tensor_reduce(statC[:, 3:16:4], xd[:], AX.X, ALU.min))
            dve.wait_ge(s_xtc, 3)
            xg = xT[:].rearrange("p c b d -> p (c b) d")
            cg = xc[:].rearrange("p c b d -> p (c b) d")
            link(v.tensor_reduce(mtok[:], xg, AX.X, ALU.add))
            link(v.tensor_scalar(mtok[:], mtok[:], 1.0 / D, None, ALU.mult))
            link(v.tensor_tensor(cg, xg, mtok[:].unsqueeze(2).broadcast_to([P, NT, D]), ALU.subtract))
            link(v.tensor_tensor(cg, cg, cg, ALU.mult))
            v.tensor_reduce(m1[:].rearrange("p b c -> p (b c)"), cg, AX.X, ALU.add).then_inc(s_var, 1)
            v.tensor_copy(statT[:, :, 0:16:4], mtok[:].rearrange("p (c b) -> p c b", b=B))
            v.tensor_reduce(statT[:, :, 2:16:4], xT[:], AX.X, ALU.max)
            link(v.tensor_reduce(statT[:, :, 3:16:4], xT[:], AX.X, ALU.min))
            dve.wait_ge(s_std, 1)
            v.sem_inc(s_stat, 1)
            dve.wait_ge(s_rows, 1)
            v.tensor_copy(rt[:], ps[0][0:D, 0:12]).then_inc(s_rowc, 1)
            link(v.tensor_copy(rc[:].rearrange("p b c k -> p (b c k)"), ps[1][0:P, 0:72]))
            dve.wait_ge(s_bm, 1)
            link(v.tensor_scalar(bm[:, 0, :], ps[2][:, 0:12], 0.5, None, ALU.mult))
            link(v.tensor_scalar(rtc[:, 0, :], rt[:], 0.5, None, ALU.mult))
            link(v.tensor_tensor(rtc[:, 0, :], rtc[:, 0, :], bm[0:D, 0, :], ALU.subtract))
            v.tensor_tensor(rtc[:, 1, :], rtc[:, 0, :], rtc[:, 0, :], ALU.mult).then_inc(s_usq, 1)
            link(v.tensor_copy(basis[:, :, :, 0], rtc[:, 0, :].rearrange("d (b k) -> d k b", k=3)))
            for k in range(3):
                rows, slot = (slice(0, D), slice(D, 2 * D))[k % 2], k // 2
                for a in range(3):
                    v.tensor_copy(qku[rows, 0, slot, :, 3 * a:3 * a + 3],
                                  basis[:, k, :, a:a + 1].broadcast_to([D, B, 3]))
                    v.tensor_copy(qku[rows, 1, slot, :, 3 * a:3 * a + 3], basis[:, k])
                v.tensor_copy(vu[rows, slot].rearrange("d b i r -> d (b i) r"),
                              basis[:, k, :, :].rearrange("d b i -> d (b i)").unsqueeze(2).broadcast_to([D, 12, NR]))
            for j in range(12):
                last = v.tensor_scalar(diag[:, j, :], ident[0:D, 0:D], rtc[:, 0, j:j + 1], None, ALU.mult)
            last.then_inc(s_basis, 1)
            link(v.tensor_scalar(hm[:], rc[:], 0.5, None, ALU.mult))
            for c in range(CH):
                link(v.tensor_tensor(hm[:, :, c, :], hm[:, :, c, :],
                                     bm[0:P, 0, :].rearrange("p (b k) -> p b k", k=3), ALU.add))
            link(v.tensor_reduce(m1[:], hm[:], AX.X, ALU.add))
            link(v.tensor_scalar(m1[:], m1[:], 1.0 / 3, None, ALU.mult))
            hg = hm[:].rearrange("p b c k -> p (b c) k")
            ag = ak[:].rearrange("p b c k -> p (b c) k")
            mg = m1[:].rearrange("p b c -> p (b c)")
            link(v.tensor_tensor(ag, hg, mg.unsqueeze(2).broadcast_to([P, NT, 3]), ALU.subtract))
            link(v.tensor_tensor(aq[:], ak[:], ak[:], ALU.mult))
            link(v.tensor_reduce(rs[:], aq[:], AX.X, ALU.add))
            dve.wait_ge(s_v0, 1)
            link(v.tensor_reduce(v0[:], ps[3][:, 0:12].rearrange("p (b k) -> p b k", k=3), AX.X, ALU.add))
            link(v.tensor_tensor(rs[:], rs[:], v0[0:P, :].unsqueeze(2).broadcast_to([P, B, CH]), ALU.add))
            v.tensor_scalar(rs[:], rs[:], 1.0 / 3, EPS, ALU.mult, ALU.add).then_inc(s_var, 1)
            dve.wait_ge(s_std, 2)
            link(v.reciprocal(rs[:], rs[:]))
            rcb = rs[:].rearrange("p b c -> p c b")
            link(v.tensor_copy(phi[:, :, :, 1], rcb))
            for a in range(2):
                link(v.tensor_tensor(phi[:, :, :, 2 + a], rcb, ak[:, :, :, a].rearrange("p b c -> p c b"), ALU.mult))
            pg = phi[:].rearrange("p c b s -> p (c b) s")

            def product(out, n, a, src):
                link(v.tensor_tensor(pg[:, :, out:out + n], pg[:, :, 1 + a:2 + a].broadcast_to([P, NT, n]),
                                     pg[:, :, src:src + n], ALU.mult))

            product(4, 3, 0, 1)
            product(7, 2, 1, 2)
            product(9, 1, 2, 3)
            product(10, 6, 0, 4)
            product(16, 3, 1, 7)
            product(19, 1, 2, 9)
            v.sem_inc(s_phi, 1)
            dve.wait_ge(s_qk, 1)
            link(v.tensor_copy(qs[:], ps[4][:, 0:E]))
            link(v.tensor_tensor(qk[:], qs[:], ps[5][:, 0:E], ALU.mult))
            link(v.tensor_reduce(Mx[:], qk[:].rearrange("p (h f) -> p h f", f=FEAT), AX.X, ALU.add))
            link(v.tensor_scalar(Mx[:], Mx[:], 0.25, one9[:], ALU.mult, ALU.add))
            v.sem_inc(s_Mx, 1)
            dve.wait_ge(s_phic, 1)
            link(v.tensor_tensor_scan(S[:], ones[:], phiT[:], 0.0, ALU.mult, ALU.add))
            link(v.tensor_copy(v0[:, 0:1], S[:, L - 1:L]))
            v.tensor_scalar(S[:], S[:], v0[:, 0:1], None, ALU.add).then_inc(s_S, 1)
            dve.wait_ge(s_xy, 1)
            for b in range(B):
                link(v.tensor_copy(xs[:], ps[4][0:NR, b * H0:(b + 1) * H0]))
                link(v.tensor_tensor(T2[:, b, :], xs[:], ps[5][0:NR, b * H0:(b + 1) * H0], ALU.mult))
            for b in range(B):
                dve.wait_ge(s_vps, b + 1)
                if b >= 1:
                    dve.wait_ge(s_C, b)
                for i in range(3):
                    last = v.tensor_tensor(T3[:, i, :].rearrange("r (h e) -> r h e", e=FEAT),
                                           T2[:, b, :].unsqueeze(2).broadcast_to([NR, H0, FEAT]),
                                           ps[(2, 3, 6)[i]][0:NR, 0:E].rearrange("r (h e) -> r h e", e=FEAT), ALU.mult)
                last.then_inc(s_T3, 1)
            for b in range(B):
                dve.wait_ge(s_Gc, b + 1)
                for n in range(2):
                    at = slice(n * HALF, (n + 1) * HALF)
                    last = v.tensor_tensor(Ft[:, b, at], G1[:, at], ps[2 + n][0:NF, 0:HALF], ALU.mult)
                last.then_inc(s_F, 1)

            def residual(t):
                b, c = divmod(t, CH)
                dve.wait_ge(s_o, t + 1)
                link(v.tensor_tensor(h[:, t, :], ps[4 + t % 2][0:P, 0:E], u0row[:, b, :], ALU.add))
                hk = h[:, t, :].rearrange("p (k d) -> p k d", k=3)
                v.tensor_tensor(hk, hk, hm[:, b, c, :].unsqueeze(2).broadcast_to([P, 3, D]), ALU.add).then_inc(s_h, 1)

            for t in range(NT):
                dve.wait_ge(s_y, t + 1)
                if t >= 2:
                    dve.wait_ge(s_yt, t - 1)
                link(v.reciprocal(rden[:, t % 2, :], ps[t % 2][0:P, E:E + H0]))
                v.tensor_tensor(yn[:, t % 2, :].rearrange("p (h e) -> p h e", e=FEAT),
                                ps[t % 2][0:P, 0:E].rearrange("p (h e) -> p h e", e=FEAT),
                                rden[:, t % 2, :].unsqueeze(2).broadcast_to([P, H0, FEAT]), ALU.mult).then_inc(s_yn, 1)
                if t >= 2:
                    residual(t - 2)
            residual(NT - 2)
            residual(NT - 1)
            dve.wait_ge(s_h, NT)


NE, SLOT = 8, 128
SLOT_BITS = SLOT.bit_length() - 1
BF16 = mybir.dt.bfloat16
RING = 4
NTOK = NT * P


class Moe:

    def __init__(self, name, top, width, gated):
        self.name, self.top, self.width, self.gated = name, top, width, gated
        self.tiles = (NT * P * top - NE) // SLOT + NE
        self.turns = (self.tiles - 2) // RING
        self.rest = self.tiles - RING * self.turns
        assert 2 <= self.rest
        self.cols = 2 * width if gated else width
        self.kc = width // 128


MOE0 = Moe("m0", 2, 384, True)
MOE1 = Moe("m1", 1, 768, False)


def moe(nc, keep, A, h, ident, cfg, out):
    name, top, S, turns, rest = cfg.name, cfg.top, cfg.tiles, cfg.turns, cfg.rest
    ctx = ExitStack()
    with ctx:
        def sb(n, shape, dt=F32):
            return ctx.enter_context(nc.sbuf_tensor(f"{name}_{n}", shape, dt))

        def sem(n):
            return keep.enter_context(nc.semaphore(f"{name}_{n}"))

        kx = 96 if cfg.gated else 97
        w1 = sb("w1", [kx, NE, 2, cfg.cols])
        w2 = sb("w2", [128, NE, cfg.kc, E])
        wr = sb("wr", [96, 2, NE])
        row = sb("row", [P, E if cfg.gated else NE])
        b2 = None if cfg.gated else sb("b2", [1, NE, E])
        n = sb("n", [P, NT, E])
        xn = sb("xn", [P, NT, E]) if cfg.gated else n
        got = [xn if cfg.gated else sb("got0", [P, NT, E]), sb("got1", [P, NT, E]) if top == 2 else None]
        posi = sb("posi", [P, 2, top, NT], I32)
        tile0 = sb("tile0", [P, top, NT, S], BF16)
        tile1 = sb("tile1", [P, top, NT, 2, S], BF16)
        at = sb("at", [P, top, NT], BF16)
        lane = sb("lane", [P, top, NT], BF16)
        lane1 = sb("lane1", [P, top, NT, SLOT], BF16)
        num_p = sb("num_p", [P, 1])
        num_t = sb("num_t", [P, top, NT], BF16)
        iott = sb("iott", [P, S], BF16)
        iotl = sb("iotl", [P, SLOT], BF16)
        padrow = sb("padrow", [128, S])
        who = sb("who", [128, 3, S])
        take = sb("take", [128, RING * (turns + 2)], U32)
        give = sb("give", [128, S], U32)
        rows = sb("rows", [128, RING, 2], U32)
        st = sb("st", [P, NT, 6])
        mv = sb("mv", [P, NT, 2])
        rstd = sb("rstd", [P, NT])
        msq = sb("msq", [P, NT])
        xnT = sb("xnT", [96, RING, 2, P])
        lg = sb("lg", [P, NT, NE])
        lm = sb("lm", [P, NT])
        pr = sb("pr", [P, NT, NE])
        tmp = sb("tmp", [P, NT, NE])
        oh = sb("oh", [P, 2, NT, NE])
        msk = sb("msk", [P, NT, NE])
        pe_ = sb("pe", [P, top, NT])
        idx = sb("idx", [P, NT])
        iotx = sb("iotx", [P, NT, NE])
        iot128 = sb("iot128", [128, NT])
        iots = sb("iots", [1, S + 2])
        zero = sb("zero", [128, E])
        tri = sb("tri", [P, P])
        ones = sb("ones", [128, NE * NT])
        tot = sb("tot", [128, NE, NT])
        inc = sb("inc", [128, NE, NT])
        exc = sb("exc", [128, NE, NT])
        cnt = sb("cnt", [128, NE])
        big = sb("big", [128, NE, NT])
        nt_ = sb("nt", [128, NE])
        cum = sb("cum", [128, NE])
        pos = sb("pos", [P, NT, NE])
        posf = sb("posf", [P, top, NT])
        ecmp = sb("ecmp", [1, S + 2, NE])
        eidf = sb("eidf", [1, S + 2])
        eid = sb("eid", [1, S + 2], I32)
        xg = sb("xg", [SLOT, RING, E])
        xgT = sb("xgT", [kx, 2, 2, SLOT])
        act_g = sb("act_g", [SLOT, cfg.width])
        hid = sb("hid", [SLOT, cfg.width])
        hidT = sb("hidT", [128, cfg.width])
        y = sb("y", [SLOT, RING, E])
        X = nc.dram_tensor(f"{name}_X", (NTOK, E), F32, kind="Internal").ap()
        Y = nc.dram_tensor(f"{name}_Y", (top * NTOK + (S + RING) * SLOT, E), F32, kind="Internal").ap()
        psX = ctx.enter_context(nc.psum_tensor(f"{name}_psX", [128, 512], F32))
        psG = [ctx.enter_context(nc.psum_tensor(f"{name}_psG{i}", [128, 2, 512], F32)) for i in range(2)]
        nH = cfg.width // 384
        psH = ctx.enter_context(nc.psum_tensor(f"{name}_psH", [128, nH, 512], F32))
        psY = ctx.enter_context(nc.psum_tensor(f"{name}_psY", [128, 512], F32))

        s_w, s_r, s_z, s_X, s_cst = sem("w"), sem("r"), sem("z"), sem("X"), sem("cst")
        s_v, s_ln, s_sd, s_n, s_xn = sem("v"), sem("ln"), sem("sd"), sem("n"), sem("xn")
        s_rt, s_rc, s_lg, s_ls, s_ex, s_m, s_rank, s_pos = (sem(k) for k in (
            "rt", "rc", "lg", "ls", "ex", "m", "rank", "pos"))
        s_eid, s_num, s_b, s_who = sem("eid"), sem("num"), sem("b"), sem("who")
        s_col, s_turn = sem("col"), sem("turn")
        s_in = [sem(f"in{j}") for j in range(RING)]
        s_st = [sem(f"st{j}") for j in range(RING)]
        s_xt, s_xc, s_gu, s_sg, s_h, s_ht, s_hc, s_c, s_y = (sem(k) for k in (
            "xt", "xc", "gu", "sg", "h", "ht", "hc", "c", "y"))
        s_got, s_out, s_res = [sem(f"got{b}") for b in range(B)], sem("out"), sem("res")
        block = ctx.enter_context(nc.Block())

        @block.sync
        def _(sp):
            sp.dma_start(wr[:], A[f"{name}_wr"]).then_inc(s_r, 16)
            sp.dma_start(row[:], A[f"{name}_row"].partition_broadcast(P)).then_inc(s_r, 16)
            for e in range(NE):
                sp.dma_start(w1[:, e], A[f"{name}_w1"][:, e]).then_inc(s_w, 16)
                sp.dma_start(w2[:, e], A[f"{name}_w2"][:, e]).then_inc(s_w, 16)
            if not cfg.gated:
                sp.dma_start(b2[:], A[f"{name}_b2"]).then_inc(s_w, 16)
            for b in range(B):
                sp.wait_ge(s_xn if cfg.gated else s_n, CH * (b + 1))
                sp.dma_start(X[b * L:(b + 1) * L, :].rearrange("(c p) e -> p c e", p=P),
                             xn[:, b * CH:(b + 1) * CH, :]).then_inc(s_X, 16)
            sp.wait_ge(s_X, 16 * B)
            for j in range(RING):
                sp.wait_ge(s_st[j], 16 * (turns + 1 + (j < rest)))
            for b in range(B):
                for k in range(top):
                    sp.dma_start(got[k][:, b * CH:(b + 1) * CH, :],
                                 Y[k * NTOK + b * L:k * NTOK + (b + 1) * L, :].rearrange("(c p) e -> p c e", p=P)
                                 ).then_inc(s_got[b], 16)
            for b in range(B):
                sp.wait_ge(s_got[b], 16 * top)
            if out is not None:
                for b in range(B):
                    sp.wait_ge(s_res, CH * (b + 1))
                    sp.dma_start(out[b].rearrange("(c p) e -> p c e", p=P),
                                 h[:, b * CH:(b + 1) * CH, :]).then_inc(s_out, 16)
                sp.wait_ge(s_out, 16 * B)

        @block.gpsimd
        def _(pool):
            if not cfg.gated:
                pool.memset(xgT[96:97, :, :, :], 1.0).then_inc(s_cst, 1)
                pool.wait_ge(s_cst, 1)
            pool.memset(zero[:], 0.0).then_inc(s_z, 1)
            pool.memset(ones[:], 1.0)
            pool.memset(take[:, S:], 0)
            pool.memset(tri[:], 1.0)
            pool.iota(iotx[:], pattern=[[0, NT], [1, NE]], base=NE, channel_multiplier=0,
                      allow_small_or_imprecise_dtypes=True)
            pool.iota(iot128[:], pattern=[[SLOT, NT]], base=0, channel_multiplier=0,
                      allow_small_or_imprecise_dtypes=True)
            pool.iota(iott[:], pattern=[[1, S]], base=0, channel_multiplier=0,
                      allow_small_or_imprecise_dtypes=True)
            pool.iota(iotl[:], pattern=[[1, SLOT]], base=0, channel_multiplier=0,
                      allow_small_or_imprecise_dtypes=True)
            pool.iota(num_p[:], pattern=[[0, 1]], base=1, channel_multiplier=1, allow_small_or_imprecise_dtypes=True)
            pool.iota(num_t[:], pattern=[[NT, top], [1, NT]], base=0, channel_multiplier=0,
                      allow_small_or_imprecise_dtypes=True)
            pool.iota(padrow[:], pattern=[[SLOT, S]], base=top * NTOK + 1, channel_multiplier=1,
                      allow_small_or_imprecise_dtypes=True)
            pool.iota(iots[:], pattern=[[1, S + 2]], base=0, channel_multiplier=0,
                      allow_small_or_imprecise_dtypes=True).then_inc(s_z, 1)
            pool.wait_ge(s_z, 2)
            pool.affine_select(out=tri[:], in_=tri[:], compare_op=ALU.is_gt, fill=0.0, base=0,
                               pattern=[[1, P]], channel_multiplier=-1).then_inc(s_cst, 1)
            pool.wait_ge(s_z, 2)
            for j in range(RING):
                row0 = top * NTOK + (S + j) * SLOT
                pool.dma_start(Y[row0:row0 + SLOT, :], zero[:]).then_inc(s_st[j], 16)
            pool.wait_ge(s_num, 1)
            pool.tensor_tensor(tile1[:, :, :, 1, :].rearrange("p k t s -> p (k t) s"),
                               tile0[:].rearrange("p k t s -> p (k t) s"),
                               num_t[:].rearrange("p k t -> p (k t)").unsqueeze(2).broadcast_to([P, top * NT, S]),
                               ALU.mult).then_inc(s_who, 1)

            def gather(j):
                pool.indirect_dma_start(out=xg[:, j, :], out_offset=None, in_=X,
                                        in_offset=bass.IndirectOffsetOnAxis(ap=rows[:, j, 0:1], axis=0)
                                        ).then_inc(s_in[j], 16)

            def scatter(j):
                pool.indirect_dma_start(
                    out=Y, out_offset=bass.IndirectOffsetOnAxis(ap=rows[:, j, 1:2], axis=0),
                    in_=y[:, j, :], in_offset=None).then_inc(s_st[j], 16)

            pool.wait_ge(s_X, 16 * B)
            pool.wait_ge(s_pos, 1)
            pool.tensor_copy(rows[:, :, 0], take[:, 0:RING]).then_inc(s_col, 1)
            pool.wait_ge(s_col, 1)
            for j in range(RING):
                gather(j)
            with pool.Fori(0, turns) as i:
                for j in range(RING):
                    pool.wait_ge(s_xt, RING * i + (j + 1))
                    pool.wait_ge(s_st[j], 16 * i + 16)
                    pool.tensor_copy(rows[:, j, 0:1], take[:, bass.ds(RING * i + (RING + j), 1)]).then_inc(s_col, 1)
                    pool.tensor_copy(rows[:, j, 1:2], give[:, bass.ds(RING * i + j, 1)]).then_inc(s_col, 1)
                    pool.wait_ge(s_col, 2 * RING * i + (2 * j + 3))
                    pool.sem_inc(s_turn, 1)
                    gather(j)
                    pool.wait_ge(s_y, RING * i + (j + 2))
                    pool.sem_inc(s_turn, 1)
                    scatter(j)
            for j in range(rest):
                pool.wait_ge(s_st[j], 16 * (turns + 1))
            pool.tensor_copy(rows[:, 0:rest, 1], give[:, RING * turns:S]).then_inc(s_col, 1)
            pool.wait_ge(s_col, 2 * RING * turns + 2)
            for j in range(rest):
                pool.wait_ge(s_y, RING * turns + j + 2)
                scatter(j)
            for j in range(RING):
                pool.wait_ge(s_in[j], 16 * (turns + 1))
                pool.wait_ge(s_st[j], 16 * (turns + 1 + (j < rest)))

        @block.tensor
        def _(pe):
            pe.wait_ge(s_r, 32)

            def logits(t):
                pe.wait_ge(s_rc, t + 1)
                for k in range(2):
                    last = nc.tensor.matmul(psX[0:P, 256 + NE * t:256 + NE * t + NE], xnT[:, t % RING, k, :],
                                            wr[:, k, :], start=(k == 0), stop=(k == 1))
                last.then_inc(s_lg, 1)

            for t in range(NT):
                pe.wait_ge(s_xn if cfg.gated else s_n, t + 1)
                if t >= RING:
                    pe.wait_ge(s_rc, t - RING + 1)
                for k in range(2):
                    last = nc.tensor.transpose(psG[t % 2][0:96, t // 2 % 2, k * P:(k + 1) * P],
                                               xn[:, t, 96 * k:96 * k + 96], ident[0:P, 0:P])
                last.then_inc(s_rt, 1)
                if t >= 2:
                    logits(t - 2)
            logits(NT - 2)
            logits(NT - 1)
            pe.wait_ge(s_m, 1)
            pe.wait_ge(s_cst, 1 if cfg.gated else 2)
            mm = msk[:].rearrange("p t e -> p (t e)")
            nc.tensor.matmul(psG[0][0:P, 0, 0:NT * NE], tri[:], mm, start=True, stop=True)
            nc.tensor.matmul(psG[0][:, 1, 0:NT * NE], ones[0:P, 0:128], mm, start=True, stop=True).then_inc(s_rank, 1)

            pe.wait_ge(s_who, 2)
            for k in range(top):
                pe.wait_ge(s_b, k + 1)
                for t in range(NT):
                    last = nc.tensor.matmul(psY[:, 0:2 * S], lane1[:, k, t, :],
                                            tile1[:, k, t, :, :].rearrange("p n s -> p (n s)"),
                                            start=(k == 0 and t == 0), stop=(k == top - 1 and t == NT - 1))
            last.then_inc(s_rank, 1)

            def to_columns(buf):
                for k in range(2):
                    last = nc.tensor.transpose(psX[0:96, k * SLOT:(k + 1) * SLOT], xg[:, buf, 96 * k:96 * k + 96],
                                               ident[:])
                last.then_inc(s_xt, 1)

            def first_products(buf, e):
                half = cfg.cols // 2
                for g in range(2):
                    for k in range(2):
                        last = nc.tensor.matmul(psG[buf][:, g, 0:half], xgT[:, buf, k, :],
                                                w1[:, bass.ds(e, 1), k, g * half:(g + 1) * half].rearrange(
                                                    "d o f -> d (o f)"),
                                                start=(k == 0), stop=(k == 1))
                last.then_inc(s_gu, 1)

            pe.wait_ge(s_eid, 1)
            pe.wait_ge(s_w, 16 * (2 * NE + (0 if cfg.gated else 1)))
            for j in range(2):
                pe.wait_ge(s_in[j], 16)
                if j:
                    pe.wait_ge(s_xc, 1)
                to_columns(j)
            pe.wait_ge(s_xc, 2)
            pe.sem_inc(s_ht, 1)
            pe.sem_inc(s_c, 1)
            owner = [nc.tensor.alloc_register(f"{name}_owner{j}") for j in range(2)]
            nc.tensor.reg_load(owner[0], eid[0:1, 0:1])
            first_products(0, nc.tensor.snap(owner[0], min_val=0, max_val=NE - 1))

            def turn(i, count, ahead):
                for j in range(count):
                    if j < ahead:
                        pe.wait_ge(s_in[(j + 2) % RING], 16 * i + 16 * (1 + (j + 2) // RING))
                        pe.wait_ge(s_xc, RING * i + (j + 2))
                        to_columns((j + 2) % RING)
                    pe.wait_ge(s_h, RING * i + (j + 2))
                    pe.wait_ge(s_hc, RING * i + (j + 1))
                    for k in range(cfg.kc):
                        last = nc.tensor.transpose(psH[:, k // 3, (k % 3) * 128:(k % 3 + 1) * 128],
                                                   hid[:, k * 128:(k + 1) * 128], ident[:])
                    last.then_inc(s_ht, 1)
                    here = nc.tensor.snap(owner[j % 2], min_val=0, max_val=NE - 1)
                    if j < ahead + 1:
                        nc.tensor.reg_load(owner[1 - j % 2], eid[0:1, bass.ds(RING * i + (j + 1), 1)])
                        pe.wait_ge(s_xc, RING * i + (j + 2))
                        first_products(1 - j % 2, nc.tensor.snap(owner[1 - j % 2], min_val=0, max_val=NE - 1))
                    pe.wait_ge(s_hc, RING * i + (j + 2))
                    pe.wait_ge(s_y, RING * i + (j + 1))
                    for k in range(cfg.kc):
                        last = nc.tensor.matmul(psY[:, 0:E], hidT[:, k * 128:(k + 1) * 128],
                                                w2[:, bass.ds(here, 1), k, :].rearrange("f o e -> f (o e)"),
                                                start=(k == 0), stop=(cfg.gated and k == cfg.kc - 1))
                    if not cfg.gated:
                        last = nc.tensor.matmul(psY[:, 0:E], ones[0:1, 0:128],
                                                b2[:, bass.ds(here, 1), :].rearrange("f o e -> f (o e)"),
                                                start=False, stop=True)
                    last.then_inc(s_c, 1)

            with pe.Fori(0, turns) as i:
                turn(i, RING, RING)
            turn(turns, rest, rest - 2)

        @block.scalar
        def _(act):
            act.wait_ge(s_ln, 1)
            nc.scalar.activation(rstd[:], rstd[:], ACT.Sqrt).then_inc(s_sd, 1)
            if cfg.gated:
                act.wait_ge(s_ln, 2)
                nc.scalar.activation(msq[:], msq[:], ACT.Sqrt).then_inc(s_sd, 1)
            for t in range(NT):
                act.wait_ge(s_rt, t + 1)
                if t >= RING:
                    act.wait_ge(s_lg, t - RING + 1)
                nc.scalar.activation(xnT[:, t % RING, :, :].rearrange("d k p -> d (k p)"),
                                     psG[t % 2][0:96, t // 2 % 2, 0:2 * P], ACT.Copy).then_inc(s_rc, 1)
            act.wait_ge(s_ls, 1)
            nc.scalar.activation(lg[:], lg[:], ACT.Exp).then_inc(s_ex, 1)

            def columns(buf):
                nc.scalar.activation(xgT[0:96, buf, :, :].rearrange("d k p -> d (k p)"), psX[0:96, 0:2 * SLOT],
                                     ACT.Copy).then_inc(s_xc, 1)

            if not cfg.gated:
                act.wait_ge(s_z, 2)
            for j in range(2):
                act.wait_ge(s_xt, j + 1)
                columns(j)

            def turn(i, count, ahead):
                for j in range(count):
                    act.wait_ge(s_gu, RING * i + (j + 1))
                    if cfg.gated:
                        act.wait_ge(s_h, RING * i + (j + 1))
                        nc.scalar.activation(act_g[:], psG[j % 2][:, 0, 0:384], ACT.Silu).then_inc(s_sg, 1)
                    else:
                        act.wait_ge(s_ht, RING * i + (j + 1))
                        nc.scalar.activation(hid[:].rearrange("p (a f) -> p a f", a=2), psG[j % 2][:, :, 0:384],
                                             ACT.Gelu).then_inc(s_h, 1)
                    if j < ahead:
                        act.wait_ge(s_xt, RING * i + (j + 3))
                        columns(j % 2)

            with act.Fori(0, turns) as i:
                turn(i, RING, RING)
            turn(turns, rest, rest - 2)

        @block.vector
        def _(dve):
            v = nc.vector
            link = Chain(dve, s_v)
            for t in range(NT):
                v.bn_stats(st[:, t, :], h[:, t, :]).then_inc(s_v, 1)
            link.n += NT
            dve.wait_ge(s_v, link.n)
            for t in range(NT):
                v.bn_aggr(mv[:, t, :], st[:, t, :]).then_inc(s_v, 1)
            link.n += NT
            dve.wait_ge(s_v, link.n)
            v.tensor_scalar(rstd[:], mv[:, :, 1], EPS, None, ALU.add).then_inc(s_ln, 1)
            dve.wait_ge(s_sd, 1)
            link(v.reciprocal(rstd[:], rstd[:]))
            if cfg.gated:
                link(v.tensor_tensor(msq[:], rstd[:], rstd[:], ALU.mult))
                link(v.tensor_tensor(msq[:], msq[:], mv[:, :, 1], ALU.mult))
                v.tensor_scalar(msq[:], msq[:], 1e-6, None, ALU.add).then_inc(s_ln, 1)
            if cfg.gated:
                dve.wait_ge(s_sd, 2)
                link(v.reciprocal(msq[:], msq[:]))
                dve.wait_ge(s_r, 32)
            for t in range(NT + 1):
                if t < NT:
                    v.tensor_scalar(n[:, t, :], h[:, t, :], mv[:, t, 0:1], rstd[:, t:t + 1], ALU.subtract,
                                    ALU.mult).then_inc(s_n, 1)
                if cfg.gated and t:
                    dve.wait_ge(s_n, t)
                    v.scalar_tensor_tensor(xn[:, t - 1, :], n[:, t - 1, :], msq[:, t - 1:t], row[:], ALU.mult,
                                           ALU.mult).then_inc(s_xn, 1)
            dve.wait_ge(s_lg, NT)
            dve.wait_ge(s_r, 32)
            lps = psX[0:P, 256:256 + NT * NE].rearrange("p (t e) -> p t e", e=NE)
            if cfg.gated:
                link(v.tensor_copy(lg[:], lps))
            else:
                link(v.tensor_tensor(lg[:], lps, row[:].unsqueeze(1).broadcast_to([P, NT, NE]), ALU.add))
            link(v.tensor_reduce(lm[:], lg[:], AX.X, ALU.max))
            v.tensor_tensor(lg[:], lg[:], lm[:].unsqueeze(2).broadcast_to([P, NT, NE]), ALU.subtract).then_inc(s_ls, 1)
            dve.wait_ge(s_ex, 1)
            link(v.tensor_reduce(lm[:], lg[:], AX.X, ALU.add))
            link(v.reciprocal(lm[:], lm[:]))
            link(v.tensor_tensor(pr[:], lg[:], lm[:].unsqueeze(2).broadcast_to([P, NT, NE]), ALU.mult))
            dve.wait_ge(s_z, 2)
            for k in range(top):
                link(v.tensor_reduce(pe_[:, k, :], pr[:], AX.X, ALU.max))
                link(v.tensor_tensor(tmp[:], pr[:], pe_[:, k, :].unsqueeze(2).broadcast_to([P, NT, NE]), ALU.is_equal))
                link(v.scalar_tensor_tensor(tmp[:].rearrange("p t e -> p (t e)"), tmp[:].rearrange("p t e -> p (t e)"),
                                            -float(NE), iotx[:].rearrange("p t e -> p (t e)"), ALU.mult, ALU.add))
                link(v.tensor_reduce(idx[:], tmp[:], AX.X, ALU.min))
                link(v.tensor_scalar(idx[:], idx[:], float(NE), None, ALU.add))
                link(v.tensor_tensor(oh[:, k, :, :], iotx[:], idx[:].unsqueeze(2).broadcast_to([P, NT, NE]),
                                     ALU.is_equal))
                if k + 1 < top:
                    link(v.scalar_tensor_tensor(pr[:].rearrange("p t e -> p (t e)"),
                                                oh[:, k, :, :].rearrange("p t e -> p (t e)"), -2.0,
                                                pr[:].rearrange("p t e -> p (t e)"), ALU.mult, ALU.add))
            if top == 2:
                v.tensor_tensor(msk[:], oh[:, 0], oh[:, 1], ALU.add).then_inc(s_m, 1)
            else:
                v.tensor_copy(msk[:], oh[:, 0]).then_inc(s_m, 1)
            dve.wait_ge(s_rank, 1)
            flat = "p e t -> p (e t)"
            link(v.tensor_copy(tot[:], psG[0][:, 1, 0:NT * NE].rearrange("p (t e) -> p e t", e=NE)))
            link(v.tensor_tensor_scan(inc[:].rearrange(flat), ones[:], tot[:].rearrange(flat), 0.0, ALU.mult, ALU.add))
            link(v.tensor_tensor(exc[:], inc[:], tot[:], ALU.subtract))
            link(v.tensor_tensor(cnt[:], inc[:, :, NT - 1], exc[:, :, 0], ALU.subtract))
            link(v.tensor_tensor(big[:], cnt[:].unsqueeze(2).broadcast_to([128, NE, NT]),
                                 iot128[:].unsqueeze(1).broadcast_to([128, NE, NT]), ALU.is_gt))
            link(v.tensor_reduce(nt_[:], big[:], AX.X, ALU.add))
            link(v.tensor_tensor_scan(cum[:], ones[:, 0:NE], nt_[:], 0.0, ALU.mult, ALU.add))
            link(v.tensor_tensor(ecmp[:], iots[:].unsqueeze(2).broadcast_to([1, S + 2, NE]),
                                 cum[0:1, :].unsqueeze(1).broadcast_to([1, S + 2, NE]), ALU.is_ge))
            link(v.tensor_reduce(eidf[:], ecmp[:], AX.X, ALU.add))
            link(v.tensor_scalar(eidf[:], eidf[:], float(NE - 1), None, ALU.min))
            v.tensor_copy(eid[:], eidf[:]).then_inc(s_eid, 1)
            link(v.tensor_tensor(cnt[:], cum[:], nt_[:], ALU.subtract))
            link(v.tensor_scalar(cnt[:], cnt[:], float(SLOT), None, ALU.mult))
            link(v.tensor_tensor(cnt[:], cnt[:], exc[:, :, 0], ALU.subtract))
            link(v.tensor_tensor(exc[:], exc[:], cnt[:].unsqueeze(2).broadcast_to([128, NE, NT]), ALU.add))
            link(v.tensor_tensor(pos[:], exc[0:P].rearrange("p e t -> p t e"),
                                 psG[0][0:P, 0, 0:NT * NE].rearrange("p (t e) -> p t e", e=NE), ALU.add))
            for k in range(top):
                link(v.tensor_tensor(tmp[:], pos[:], oh[:, k], ALU.mult))
                link(v.tensor_reduce(posf[:, k, :], tmp[:], AX.X, ALU.add))
            shape = [P, top * NT, S]
            link(v.tensor_copy(posi[:, 0], posf[:]))
            link(v.tensor_scalar(posi[:, 1], posi[:, 0], SLOT_BITS, None, ALU.logical_shift_right))
            link(v.tensor_scalar(posi[:, 0], posi[:, 0], SLOT - 1, None, ALU.bitwise_and))
            link(v.tensor_copy(at[:], posi[:, 1]))
            link(v.tensor_copy(lane[:], posi[:, 0]))
            v.tensor_tensor(tile0[:].rearrange("p k t s -> p (k t) s"),
                            at[:].rearrange("p k t -> p (k t)").unsqueeze(2).broadcast_to(shape),
                            iott[:].unsqueeze(1).broadcast_to(shape), ALU.is_equal).then_inc(s_num, 1)
            for k in range(top):
                v.tensor_tensor(lane1[:, k], iotl[:].unsqueeze(1).broadcast_to([P, NT, SLOT]),
                                lane[:, k, :].unsqueeze(2).broadcast_to([P, NT, SLOT]), ALU.is_equal
                                ).then_inc(s_b, 1)
            dve.wait_ge(s_num, 1)
            v.tensor_scalar(tile1[:, :, :, 0, :].rearrange("p k t s -> p (k t) s"),
                            tile0[:].rearrange("p k t s -> p (k t) s"), num_p[:], None, ALU.mult).then_inc(s_who, 1)
            dve.wait_ge(s_rank, 2)
            link(v.tensor_copy(who[:, 2, :], psY[:, 0:S]))
            link(v.scalar_tensor_tensor(who[:, 0, :], psY[:, S:2 * S], float(P), who[:, 2, :], ALU.mult, ALU.add))
            link(v.tensor_scalar(who[:, 1, :], who[:, 0, :], 0.0, None, ALU.is_equal))
            link(v.tensor_tensor(who[:, 2, :], who[:, 1, :], padrow[:], ALU.mult))
            link(v.tensor_tensor(who[:, 2, :], who[:, 2, :], who[:, 0, :], ALU.add))
            link(v.tensor_scalar(who[:, 2, :], who[:, 2, :], -1.0, None, ALU.add))
            link(v.tensor_copy(give[:], who[:, 2, :]))
            link(v.tensor_tensor(who[:, 0, :], who[:, 0, :], who[:, 1, :], ALU.add))
            if top == 2:
                link(v.tensor_scalar(who[:, 1, :], who[:, 0, :], float(NTOK), -float(NTOK), ALU.is_gt, ALU.mult))
                link(v.tensor_tensor(who[:, 0, :], who[:, 0, :], who[:, 1, :], ALU.add))
            link(v.tensor_scalar(who[:, 0, :], who[:, 0, :], -1.0, None, ALU.add))
            v.tensor_copy(take[:, 0:S], who[:, 0, :]).then_inc(s_pos, 1)
            v.sem_inc(s_h, 1)
            v.sem_inc(s_hc, 1)
            v.sem_inc(s_y, 1)

            def gated_hidden(i, j):
                dve.wait_ge(s_sg, RING * i + (j + 1))
                dve.wait_ge(s_ht, RING * i + (j + 1))
                v.tensor_tensor(hid[:], act_g[:], psG[j % 2][:, 1, 0:384], ALU.mult).then_inc(s_h, 1)

            def hidden_columns(i, j):
                dve.wait_ge(s_ht, RING * i + (j + 2))
                dve.wait_ge(s_c, RING * i + (j + 1))
                v.tensor_copy(hidT[:].rearrange("p (a f) -> p a f", a=nH), psH[:, :, 0:384]).then_inc(s_hc, 1)

            def turn(i, count, ahead):
                for j in range(count):
                    if cfg.gated and j < ahead:
                        gated_hidden(i, j + 1)
                    dve.wait_ge(s_c, RING * i + (j + 2))
                    dve.wait_ge(s_st[j], 16 * i + 16)
                    v.tensor_copy(y[:, j, :], psY[:, 0:E]).then_inc(s_y, 1)
                    if j < ahead:
                        hidden_columns(i, j + 1)

            if cfg.gated:
                link(v.tensor_tensor(h[:], h[:], n[:], ALU.add))
                gated_hidden(0, 0)
            hidden_columns(0, 0)
            with dve.Fori(0, turns) as i:
                turn(i, RING, RING)
            turn(turns, rest, rest - 1)
            for t in range(NT):
                if t % CH == 0:
                    dve.wait_ge(s_got[t // CH], 16 * top)
                for k in range(top):
                    ins = v.scalar_tensor_tensor(h[:, t, :], got[k][:, t, :], pe_[:, k, t:t + 1], h[:, t, :], ALU.mult,
                                                 ALU.add)
                    if k + 1 < top:
                        link(ins)
                ins.then_inc(s_res, 1)
            dve.wait_ge(s_res, NT)


def moe_inputs(f):
    t = np.ascontiguousarray
    gu = np.concatenate([f["L0_ffn_gate_w"], f["L0_ffn_up_w"]], axis=1)
    w1 = f["L1_ffn_W1"].reshape(NE, 2, 96, 768).transpose(2, 0, 1, 3)
    w1b = np.zeros((97,) + w1.shape[1:], w1.dtype)
    w1b[:96] = w1
    w1b[96, :, 1] = f["L1_ffn_b1"]
    return {
        "m0_wr": t(f["L0_ffn_router_w"].T.reshape(2, 96, NE).transpose(1, 0, 2)),
        "m0_row": f["L0_ffn_norm_w"],
        "m0_w1": t(gu.transpose(2, 0, 1).reshape(2, 96, NE, 768).transpose(1, 2, 0, 3)),
        "m0_w2": t(f["L0_ffn_down_w"].transpose(2, 0, 1).reshape(3, 128, NE, E).transpose(1, 2, 0, 3)),
        "m1_wr": t(f["L1_ffn_Ws"].reshape(2, 96, NE).transpose(1, 0, 2)),
        "m1_row": f["L1_ffn_bs"],
        "m1_w1": w1b,
        "m1_w2": t(f["L1_ffn_W2"].reshape(NE, 6, 128, E).transpose(2, 0, 1, 3)),
        "m1_b2": t(f["L1_ffn_b2"].reshape(1, NE, E)),
    }


NH, HD, GRID, REACH = 12, 64, 27, 14
HG = 6
AHEAD = 10
LP, HP = 752, 376
LW = 1 + 28 * GRID
NPR = HG // 2
NVG = -(-(L - 1) // GRID)
SCALE = HD ** -0.5
RV, RH, ONE = 64, 96, 127
V_SETS = [(range(a, min(a + 6, NVG - 1)), GRID) for a in range(0, NVG - 1, 6)] \
    + [(range(NVG - 1, NVG), L - 1 - GRID * (NVG - 1))]
FULL = L - 1 - GRID * (NVG - 1)
H_SETS = [(range(a, min(a + 6, FULL)), NVG) for a in range(0, FULL, 6)] \
    + [(range(a, min(a + 6, GRID)), NVG - 1) for a in range(FULL, GRID, 6)]
NV, NHS = len(V_SETS), len(H_SETS)
NSET = NV + NHS + 1


def relative_inputs(f):
    def rows(table, n, g):
        at = np.zeros(n, int) if g is None else np.clip(np.arange(n) - g, -REACH, REACH) + REACH + 1
        return table[at]

    out = {}
    for key, v, hh in (("rq", f["L1_attn_rk_v"], f["L1_attn_rk_h"]), ("rv", f["L1_attn_rv_v"], f["L1_attn_rv_h"])):
        for side, table, n, count in (("v", v, NVG, NVG), ("h", hh, GRID, GRID)):
            t = np.zeros((128, count + 1, 64), table.dtype)
            for g in range(count + 1):
                r = np.concatenate([rows(table, n, None if g == 0 else g - 1), table[0:1]])
                if key == "rq":
                    t[0:64, g, 0:n + 1] = r.T
                    t[64:128, g, 32:33 + n] = r.T
                else:
                    at = RV if side == "v" else RH
                    t[at:at + n + 1, g] = r
                    if side == "v":
                        t[0:64, g] = np.eye(64, dtype=table.dtype)
            out[key + side] = t
    oh = np.zeros((64, L), np.float32)
    j = np.arange(1, L)
    oh[(j - 1) // GRID, j] = 1
    oh[RH - 64 + (j - 1) % GRID, j] = 1
    oh[NVG, 0] = oh[RH - 64 + GRID, 0] = 1
    oh[ONE - 64] = 1
    out["oh"] = oh
    out["ohT"] = np.ascontiguousarray(oh.T.reshape(CH, P, 64).transpose(1, 0, 2))
    t = np.ascontiguousarray
    for k in "qkv":
        out["w" + k] = t(f["L1_attn_w" + k].reshape(2, 96, NH * HD).transpose(1, 0, 2))
    out["wp"] = t(f["L1_attn_wproj"].reshape(NH // 2, 128, E).transpose(1, 0, 2))
    out["bp"] = f["L1_attn_bproj"]
    return {"a1_" + k: v for k, v in out.items()}


def window_attention(nc, keep, A, h, ident):
    ctx = ExitStack()
    with ctx:
        def sb(n, shape, dt=F32):
            return ctx.enter_context(nc.sbuf_tensor(f"a1_{n}", shape, dt))

        def sem(n):
            return keep.enter_context(nc.semaphore(f"a1_{n}"))

        w = {k: sb("w" + k, [96, 2, HG * HD]) for k in "qkv"}
        wp = sb("wp", [128, NPR, E])
        rqv, rvv = sb("rqv", [128, NVG + 1, 64]), sb("rvv", [128, NVG + 1, 64])
        rqh, rvh = sb("rqh", [128, GRID + 1, 64]), sb("rvh", [128, GRID + 1, 64])
        bp = sb("bp", [P, E])
        qhi, qlo = sb("qhi", [128, HG, LP], F32R), sb("qlo", [128, HG, LP], F32R)
        khi, klo = sb("khi", [128, HG, L], F32R), sb("klo", [128, HG, L], F32R)
        work = sb("work", [128, HG, LW])
        pairs = sb("pairs", [128, NPR, LW])
        vhi, vlo = sb("vhi", [P, CH, HG, 128], F32R), sb("vlo", [P, CH, HG, HD], F32R)
        hnT = sb("hnT", [96, 2, L])
        PT = sb("PT", [P, 2, LP])
        Phi, Plo = sb("Phi", [P, 2, LP], F32R), sb("Plo", [P, 2, LP], F32R)
        nb = pairs[0:P].rearrange("p a l -> p (a l)")[:, 0:CH * E].rearrange("p (c e) -> p c e", e=E)
        rdb = qhi[:].bitcast(F32)[:, 0:NPR, :]
        dcol = PT[0:LP // 8, 0, 0:HG * 8].rearrange("p (h s) -> p h s", s=8)
        oh = pairs[64:128, NPR - 1, 0:L]
        ohT = PT[:, 1, 0:CH * 64].rearrange("p (c d) -> p c d", d=64)
        st = PT[:, 0, 0:6 * NT].rearrange("p (t s) -> p t s", s=6)
        mean = sb("mean", [P, NT])
        rstd = sb("rstd", [P, NT])
        mv_ = PT[:, 0, 6 * NT:8 * NT].rearrange("p (t s) -> p t s", s=2)
        nmx = sb("nmx", [P, 2, CH])
        mrow = sb("mrow", [CH, 2, P], F32R)
        psS = [ctx.enter_context(nc.psum_tensor(f"a1_S{i}", [128, 2, 512], F32)) for i in range(2)]
        psM = ctx.enter_context(nc.psum_tensor("a1_M", [128, 2, 512], F32))
        psO = ctx.enter_context(nc.psum_tensor("a1_O", [128, 2, 512], F32))

        s_bpw = sem("bpw")
        s_bp = sem("bp")
        s_wh, s_wp = sem("wh"), sem("wp")
        s_w, s_oh, s_oz, s_og = sem("w"), sem("oh"), sem("oz"), sem("og")
        s_v, s_ln, s_sd = sem("v"), sem("ln"), sem("sd")
        PER = {
            "tokens_normal": CH,
            "tokens_turned": 3,
            "columns_ready": 3,
            "k_product": 6,
            "khi_ready": 6,
            "klo_ready": 6,
            "q_product": 6,
            "pairs_ready": 6,
            "work_ready": 6,
            "v_product": 12,
            "vhi_ready": 12,
            "vlo_ready": 12,
            "table_product": 2 * NSET,
            "table_rows_act": 2 * NSET,
            "table_rows_dve": 2 * NSET,
            "qhi_ready": 12,
            "qlo_ready": 12,
            "row_scores": 72,
            "max_ready": 72,
            "max_turned": 12,
            "max_row": 12,
            "scores_ready": 72,
            "exp_ready": 72,
            "exp_rest": 72,
            "values_added": 72,
            "out_dve": 12,
            "out_act": 12,
            "rel_product": 2 * NSET,
            "rel_v_copied": 2 * NV,
            "rel_h_added": 2 * (NHS + 1),
            "inverse_ready": 2,
            "out_divided": 12,
            "projected": 12,
            "h_updated": 12,
        }
        sg = {n: sem(n) for n in PER}
        dens = nc.dram_tensor("a1_dens", (HG, LP), F32, kind="Internal").ap()
        rdens = nc.dram_tensor("a1_rdens", (HG, LP), F32, kind="Internal").ap()
        s_dr, s_dc, s_dw = sem("dr"), sem("dc"), sem("dw")
        s_md, s_db = [sem("md0"), sem("md1")], sem("db")

        def waiter(eng, i):
            def wait(name, k):
                eng.wait_ge(sg[name], i * PER[name] + k)
            return wait

        k_banks = (psS[0], psS[1], psM)
        q_banks = (psS[1], psS[0], psO)
        rv_banks = (psO[:, 0], psO[:, 1], psS[0][:, 0], psS[0][:, 1])
        xt_banks = (psS[0][0:96, 0], psS[0][0:96, 1], psS[1][0:96, 0])
        t_banks = (psS[0][:, 0], psS[0][:, 1], psO[:, 0], psO[:, 1])
        block = ctx.enter_context(nc.Block())

        @block.sync
        def _(sp):
            def load_weights(half):
                for k in "qkv":
                    sp.dma_start(w[k][:], A["a1_w" + k][:, :, half * HG * HD:(half + 1) * HG * HD]).then_inc(s_wh, 16)

            sp.dma_start(oh, A["a1_oh"]).then_inc(s_oh, 16)
            sp.dma_start(ohT, A["a1_ohT"]).then_inc(s_oh, 16)
            sp.dma_start(bp[:], A["a1_bp"].partition_broadcast(P)).then_inc(s_bpw, 16)
            load_weights(0)
            for t, k in ((rqv, "rqv"), (rqh, "rqh"), (rvv, "rvv"), (rvh, "rvh")):
                sp.dma_start(t[:], A["a1_" + k]).then_inc(s_w, 16)
            with sp.Fori(0, B) as i:
                wait = waiter(sp, i)
                for half in range(2):
                    def max_row(u):
                        wait("max_row", u + 1)
                        for c in range(CH):
                            sp.dma_start(qhi[ONE:ONE + 1, u % HG, c * P:(c + 1) * P].bitcast(F32),
                                         mrow[c:c + 1, u % 2, :].bitcast(F32)).then_inc(s_md[u % 2], 16)

                    u0 = half * HG
                    max_row(u0)
                    max_row(u0 + 1)
                    wait("v_product", (half + 1) * CH)
                    load_weights(1 - half)
                    sp.dma_start(wp[:], A["a1_wp"][:, half * NPR:(half + 1) * NPR]).then_inc(s_wp, 16)
                    for u in range(u0, u0 + HG):
                        if u + 2 < u0 + HG:
                            max_row(u + 2)
                        wait("out_dve", u + 1)
                        sp.dma_start(dens[u % HG:u % HG + 1, 0:HP], work[ONE:ONE + 1, u % HG, 0:HP]).then_inc(s_dr, 16)
                        wait("out_act", u + 1)
                        sp.dma_start(dens[u % HG:u % HG + 1, HP:LP], work[ONE:ONE + 1, u % HG, HP:LP]
                                     ).then_inc(s_dr, 16)
                    sp.wait_ge(s_dr, (2 * i + half + 1) * (32 * HG))
                    sp.dma_start(dcol, dens.rearrange("h (p s) -> p h s", s=8)).then_inc(s_dc, 16)
                    wait("inverse_ready", half + 1)
                    sp.dma_start(rdens.rearrange("h (p s) -> p h s", s=8), dcol).then_inc(s_dw, 16)
                    sp.wait_ge(s_dw, (2 * i + half + 1) * 16)
                    for par in range(2):
                        sp.dma_start(rdb[64 * par:64 * par + 64, :, 0:L],
                                     rdens[par::2, 0:L].partition_broadcast(64)).then_inc(s_db, 16)
            sp.wait_ge(s_wh, 48 * (2 * B + 1))

        @block.gpsimd
        def _(pool):
            pool.memset(klo[64:128].bitcast(F32), 0.0)
            pool.memset(qlo[64:128].bitcast(F32), 0.0)
            pool.memset(work[64:128], 0.0).then_inc(s_oz, 1)
            pool.wait_ge(s_oz, 1)
            pool.memset(qhi[:, :, L:LP].bitcast(F32), 0.0)
            pool.memset(qlo[0:64, :, L:LP].bitcast(F32), 0.0).then_inc(s_oz, 1)
            pool.wait_ge(s_oz, 2)
            with pool.Fori(0, B) as i:
                wait = waiter(pool, i)
                for u in range(2 * HG):
                    wait("qhi_ready", u + 1)
                    pool.tensor_tensor(qlo[0:ONE, u % HG, 0:L], work[0:ONE, u % HG, 0:L],
                                       qhi[0:ONE, u % HG, 0:L].bitcast(F32), ALU.subtract).then_inc(sg["qlo_ready"], 1)

        def group_sets():
            for m, (gs, n) in enumerate(V_SETS):
                yield m, "v", gs, n
            for m, (gs, n) in enumerate(H_SETS):
                yield NV + m, "h", gs, n

        def tokens(view, side, g, n):
            if side == "v":
                return view[:, :, 1 + GRID * g:1 + GRID * g + n]
            return view[:, :, 1 + g:1 + g + GRID * (n - 1) + 1:GRID]

        def grid_rows(view, gs, n):
            lo = 1 + GRID * gs[0]
            return view[:, :, lo:lo + n * len(gs)].rearrange("p h (g n) -> p h g n", n=n)

        def relative_rows(eng, wait, half, par, copy, done):
            for m, side, gs, n in group_sets():
                wait("table_product", half * NSET + m + 1)
                rows, at = (NVG + 1, RV) if side == "v" else (GRID + 1, RH)
                k = len(gs)
                dst = work[at:at + rows, par::2, :]
                src = t_banks[m % 4][32 * par:32 * par + rows, 0:k * NPR * n]
                if side == "v":
                    last = copy(grid_rows(dst, gs, n), src.rearrange("p (g h n) -> p h g n", h=NPR, n=n))
                else:
                    last = copy(grid_columns(dst, gs, n), src.rearrange("p (g h n) -> p h n g", h=NPR, n=n))
                last.then_inc(sg[done], 1)
            m = NSET - 1
            wait("table_product", half * NSET + m + 1)
            copy(work[RV:RV + NVG + 1, par::2, 0], t_banks[m % 4][32 * par:32 * par + NVG + 1, 0:NPR])
            copy(work[RH:RH + GRID + 1, par::2, 0], t_banks[m % 4][32 * par:32 * par + GRID + 1, NPR:2 * NPR]
                 ).then_inc(sg[done], 1)

        def grid_columns(view, gs, n):
            return view[:, :, 1:1 + GRID * n].rearrange("p h (n g) -> p h n g", g=GRID)[:, :, :, gs[0]:gs[0] + len(gs)]

        @block.tensor
        def _(pe):

            def token_columns(i):
                wait = waiter(pe, i)
                for c in range(CH):
                    wait("tokens_normal", c + 1)
                    for k in range(2):
                        last = nc.tensor.transpose(xt_banks[c // 2][:, (2 * (c % 2) + k) * P:(2 * (c % 2) + k + 1) * P],
                                                   nb[:, c, 96 * k:96 * k + 96], ident[0:P, 0:P])
                    if c % 2:
                        last.then_inc(sg["tokens_turned"], 1)
                wait("columns_ready", 3)

            def project(which, bank, pr, done):
                col = pr * 128
                for a in range(2):
                    for k in range(2):
                        last = nc.tensor.matmul(bank[:, a, 0:HALF], w[which][:, k, col:col + 128],
                                                hnT[:, k, a * HALF:(a + 1) * HALF], start=(k == 0), stop=(k == 1))
                last.then_inc(sg[done], 1)

            def keys(i, half):
                pe.wait_ge(s_wh, 96 * i + 48 * (half + 1))
                for pr in range(NPR):
                    project("k", k_banks[pr], pr, "k_product")

            def turn(i, last_batch):
                wait = waiter(pe, i)
                for half in range(2):
                    u0 = half * HG
                    wait("khi_ready", half * NPR + NPR)
                    wait("klo_ready", half * NPR + NPR)
                    for pr in range(NPR):
                        project("q", q_banks[pr], pr, "q_product")

                    def token_values(c):
                        if c >= 2:
                            wait("vlo_ready", half * CH + c - 1)
                        for k in range(2):
                            last = nc.tensor.matmul(psS[1][0:P, c % 2, 0:HG * HD], hnT[:, k, c * P:(c + 1) * P],
                                                    w["v"][:, k, :],
                                                    start=(k == 0), stop=(k == 1))
                        last.then_inc(sg["v_product"], 1)

                    wait("pairs_ready", half * NPR + 1)
                    wait("work_ready", half * NPR + 1)
                    token_values(0)
                    wait("pairs_ready", half * NPR + NPR)
                    wait("work_ready", half * NPR + 2)

                    def bank_free(m):
                        if m == 2:
                            wait("work_ready", half * NPR + NPR)
                        if m >= 4:
                            wait("table_rows_act", half * NSET + m - 3)
                            wait("table_rows_dve", half * NSET + m - 3)

                    for m, side, gs, n in group_sets():
                        bank_free(m)
                        for a, g in enumerate(gs):
                            last = nc.tensor.matmul(t_banks[m % 4][0:64, a * NPR * n:(a + 1) * NPR * n],
                                                    (rqv if side == "v" else rqh)[:, g + 1, :],
                                                    tokens(pairs, side, g, n), start=True, stop=True)
                        last.then_inc(sg["table_product"], 1)
                    m = NSET - 1
                    bank_free(m)
                    nc.tensor.matmul(t_banks[m % 4][0:64, 0:NPR], rqv[:, 0, :], pairs[:, :, 0], start=True, stop=True)
                    nc.tensor.matmul(t_banks[m % 4][0:64, NPR:2 * NPR], rqh[:, 0, :], pairs[:, :, 0], start=True,
                                     stop=True).then_inc(sg["table_product"], 1)

                    def row_scores(u, c, bank):
                        for a in range(2):
                            last = nc.tensor.matmul(bank[0:P, a, 0:376],
                                                    qhi[0:ONE, u % HG, c * P:(c + 1) * P],
                                                    khi[0:ONE, u % HG, a * 374:a * 374 + 376],
                                                    start=True, stop=True)
                        last.then_inc(sg["row_scores"], 1)

                    def max_to_row(u, out):
                        wait("max_ready", (u + 1) * CH)
                        nc.tensor.transpose(out, nmx[:, u % 2, :], ident[0:P, 0:P]).then_inc(sg["max_turned"], 1)

                    def scores(u, c):
                        wd = u * CH + c
                        if c == 0:
                            wait("qlo_ready", u + 1)
                            pe.wait_ge(s_md[u % 2], i * (96 * 6) + 96 * (u // 2 + 1))
                        if wd >= u0 * CH + 2:
                            wait("exp_ready", wd - 1)
                        at = slice(c * P, (c + 1) * P)
                        for x, (kk, qq) in enumerate(((khi, qhi), (khi, qlo), (klo, qhi))):
                            for a in range(2):
                                last = nc.tensor.matmul(psS[wd % 2][0:P, a, 0:HP], kk[:, u % HG, at],
                                                        qq[:, u % HG, a * HP:(a + 1) * HP], start=(x == 0),
                                                        stop=(x == 2))
                        last.then_inc(sg["scores_ready"], 1)

                    def values(u, c):
                        wd = u * CH + c
                        wait("exp_rest", wd + 1)
                        if c == 0 and u > u0:
                            wait("out_dve", u)
                            wait("out_act", u)
                        for a in range(2):
                            at = slice(a * HP, (a + 1) * HP)
                            nc.tensor.matmul(psO[:, a, 0:HP], vhi[:, c, u % HG, :], Phi[:, wd % 2, at],
                                             start=(c == 0), stop=False)
                            nc.tensor.matmul(psO[0:HD, a, 0:HP], vlo[:, c, u % HG, :], Phi[:, wd % 2, at],
                                             start=False, stop=False)
                            last = nc.tensor.matmul(psO[:, a, 0:HP], vhi[:, c, u % HG, :], Plo[:, wd % 2, at],
                                                    start=False, stop=(c == CH - 1))
                        last.then_inc(sg["values_added"], 1)

                    token_values(1)
                    values_after = {3: 2, 5: 3, 7: 4, 8: 5}
                    for x in range(AHEAD):
                        if x % CH == 0:
                            wait("qhi_ready", u0 + x // CH + 1)
                        if x >= 2:
                            wait("max_ready", u0 * CH + x - 1)
                        row_scores(u0 + x // CH, x % CH, (psS[0], psM)[x % 2])
                        if x in values_after:
                            token_values(values_after[x])
                        if x == CH:
                            max_to_row(u0, psO[0:CH, 0, 0:P])
                    wait("max_ready", u0 * CH + AHEAD - (1 - AHEAD % 2))
                    scores(u0, 0)
                    wait("vlo_ready", (half + 1) * CH)
                    for wd in range(u0 * CH, (u0 + HG) * CH):
                        u, c = divmod(wd, CH)
                        if wd + 1 < (u0 + HG) * CH:
                            scores(*divmod(wd + 1, CH))
                        mu, mc = divmod(wd + AHEAD, CH)
                        if mu < u0 + HG:
                            if mc == 0:
                                wait("qhi_ready", mu + 1)
                                wait("max_row", mu)
                            wait("max_ready", mu * CH + mc)
                            row_scores(mu, mc, psM)
                        if wd > u0 * CH:
                            values(*divmod(wd - 1, CH))
                        if mc == CH - 1 and mu < u0 + HG:
                            max_to_row(mu, psM[0:CH, 0, 384:384 + P])
                    values(u0 + HG - 1, CH - 1)
                    wait("exp_ready", (half + 1) * 36)
                    if half == 0:
                        keys(i, 1)
                    elif not last_batch:
                        token_columns(i + 1)
                        keys(i + 1, 0)
                    ahead = half == 0 or not last_batch
                    wait("out_dve", u0 + HG)
                    wait("out_act", u0 + HG)

                    def out_bank(m):
                        return rv_banks[m % 4]

                    def bank_done(m):
                        if ahead and m == 2:
                            wait("khi_ready", half * NPR + NPR + 1)
                            wait("klo_ready", half * NPR + NPR + 1)
                        if m >= 4:
                            k = m - 4
                            if k < NV:
                                wait("rel_v_copied", half * NV + k + 1)
                            else:
                                wait("rel_h_added", half * (NHS + 1) + k - NV + 1)

                    for m, side, gs, n in group_sets():
                        bank_done(m)
                        for a, g in enumerate(gs):
                            for par in range(2):
                                last = nc.tensor.matmul(
                                    out_bank(m)[64 * par:64 * par + 64, a * NPR * n:(a + 1) * NPR * n],
                                    (rvv if side == "v" else rvh)[:, g + 1, :],
                                    tokens(work[:, par::2, :], side, g, n), start=True, stop=True)
                        last.then_inc(sg["rel_product"], 1)
                    m = NSET - 1
                    bank_done(m)
                    for par in range(2):
                        for x, table in enumerate((rvv, rvh)):
                            last = nc.tensor.matmul(out_bank(m)[64 * par:64 * par + 64, 0:NPR], table[:, 0, :],
                                                    work[:, par::2, 0], start=(x == 0), stop=(x == 1))
                    last.then_inc(sg["rel_product"], 1)
                    pe.wait_ge(s_wp, 32 * i + 16 * (half + 1))
                    if ahead:
                        wait("khi_ready", half * NPR + 2 * NPR)
                        wait("klo_ready", half * NPR + 2 * NPR)
                    for c in range(CH):
                        wait("out_divided", half * CH + c + 1)
                        if c >= 2:
                            wait("h_updated", half * CH + c - 1)
                        for pr in range(NPR):
                            last = nc.tensor.matmul(psM[0:P, c % 2, 0:E], pairs[:, pr, c * P:(c + 1) * P],
                                                    wp[:, pr, :], start=(pr == 0), stop=(pr == NPR - 1))
                        last.then_inc(sg["projected"], 1)

            token_columns(0)
            keys(0, 0)
            pe.wait_ge(s_w, 16 * 4)
            pe.wait_ge(s_oz, 2)
            pe.wait_ge(s_og, 1)
            with pe.Fori(0, B - 1) as i:
                turn(i, False)
            turn(B - 1, True)

        @block.scalar
        def _(act):
            act.wait_ge(s_oh, 32)
            for hh in range(HG):
                nc.scalar.activation(khi[64:128, hh, :], oh, ACT.Copy)
                last = nc.scalar.activation(vhi[:, :, hh, 64:128], ohT, ACT.Copy)
            last.then_inc(s_og, 1)
            act.wait_ge(s_ln, 1)
            nc.scalar.activation(rstd[:], rstd[:], ACT.Sqrt).then_inc(s_sd, 1)

            def token_columns(i):
                wait = waiter(act, i)
                for g in range(3):
                    wait("tokens_turned", g + 1)
                    nc.scalar.activation(
                        hnT[:, :, 2 * g * P:2 * (g + 1) * P].rearrange("d k (c p) -> d c k p", p=P),
                        xt_banks[g][:, 0:4 * P].rearrange("d (c k p) -> d c k p", c=2, k=2), ACT.Copy
                        ).then_inc(sg["columns_ready"], 1)

            def keys(i, half):
                wait = waiter(act, i)
                for pr in range(NPR):
                    wait("k_product", half * NPR + pr + 1)
                    for par in range(2):
                        last = nc.scalar.activation(
                            khi[0:64, 2 * pr + par, :].rearrange("p (a l) -> p a l", a=2),
                            k_banks[pr][64 * par:64 * par + 64, :, 0:HALF], ACT.Copy)
                    last.then_inc(sg["khi_ready"], 1)

            def turn(i, last_batch):
                wait = waiter(act, i)
                for half in range(2):
                    u0 = half * HG
                    for pr in range(NPR):
                        wait("q_product", half * NPR + pr + 1)
                        nc.scalar.activation(pairs[:, pr, 0:L].rearrange("p (a l) -> p a l", a=2),
                                             q_banks[pr][:, :, 0:HALF], ACT.Copy).then_inc(sg["pairs_ready"], 1)
                    relative_rows(act, wait, half, 0, lambda o, x: nc.scalar.activation(o, x, ACT.Copy),
                                  "table_rows_act")
                    wait("table_rows_act", (half + 1) * NSET)
                    wait("table_rows_dve", (half + 1) * NSET)
                    wait("work_ready", half * NPR + NPR)
                    for x in range(HG + 2):
                        if x < HG:
                            nc.scalar.activation(qhi[0:ONE, x, 0:L], work[0:ONE, x, 0:L], ACT.Copy
                                                 ).then_inc(sg["qhi_ready"], 1)
                        if x >= 2:
                            c = x - 2
                            wait("v_product", half * CH + c + 1)
                            nc.scalar.activation(vhi[:, c, :, 0:64],
                                                 psS[1][0:P, c % 2, 0:HG * HD].rearrange("p (h d) -> p h d", d=HD),
                                                 ACT.Copy).then_inc(sg["vhi_ready"], 1)

                    def output(u):
                        wait("values_added", (u + 1) * CH)
                        nc.scalar.activation(work[:, u % HG, HP:LP], psO[:, 1, 0:HP], ACT.Copy
                                             ).then_inc(sg["out_act"], 1)

                    for u in range(u0, u0 + HG):
                        for c in range(CH):
                            wd = u * CH + c
                            wait("scores_ready", wd + 1)
                            if wd >= u0 * CH + 2:
                                wait("values_added", wd - 1)
                            for to in (Phi, PT):
                                last = nc.scalar.activation(to[:, wd % 2, :].rearrange("p (a l) -> p a l", a=2),
                                                            psS[wd % 2][0:P, :, 0:HP], ACT.Exp, scale=SCALE)
                            last.then_inc(sg["exp_ready"], 1)
                            if c == 0 and u > u0:
                                output(u - 1)
                    output(u0 + HG - 1)
                    if half == 0:
                        keys(i, 1)
                    elif not last_batch:
                        token_columns(i + 1)
                        keys(i + 1, 0)
                    for m, (gs, n) in enumerate(V_SETS):
                        wait("rel_product", half * NSET + m + 1)
                        k = len(gs)
                        nc.scalar.activation(
                            grid_rows(pairs, gs, n),
                            rv_banks[m % 4][:, 0:k * NPR * n].rearrange("p (g h n) -> p h g n", h=NPR, n=n),
                            ACT.Copy).then_inc(sg["rel_v_copied"], 1)

            token_columns(0)
            keys(0, 0)
            with act.Fori(0, B - 1) as i:
                turn(i, False)
            turn(B - 1, True)

        @block.vector
        def _(dve):
            v = nc.vector
            link = Chain(dve, s_v)
            for t in range(NT):
                v.bn_stats(st[:, t, :], h[:, t, :]).then_inc(s_v, 1)
            link.n += NT
            dve.wait_ge(s_v, link.n)
            for t in range(NT):
                v.bn_aggr(mv_[:, t, :], st[:, t, :]).then_inc(s_v, 1)
            link.n += NT
            dve.wait_ge(s_v, link.n)
            link(v.tensor_copy(mean[:], mv_[:, :, 0]))
            v.tensor_scalar(rstd[:], mv_[:, :, 1], EPS, None, ALU.add).then_inc(s_ln, 1)
            dve.wait_ge(s_sd, 1)
            link(v.reciprocal(rstd[:], rstd[:]))
            dve.wait_ge(s_bpw, 16)

            def normalise(i):
                for c in range(CH):
                    t = i * CH + c
                    v.tensor_scalar(nb[:, c, :], h[:, bass.ds(t, 1), :].rearrange("p o e -> p (o e)"),
                                    mean[:, bass.ds(t, 1)], rstd[:, bass.ds(t, 1)], ALU.subtract,
                                    ALU.mult).then_inc(sg["tokens_normal"], 1)
                waiter(dve, i)("tokens_normal", CH)
                hb = h[:, bass.ds(i * CH, CH), :]
                v.tensor_tensor(hb, hb, bp[:].unsqueeze(1).broadcast_to([P, CH, E]), ALU.add).then_inc(s_bp, 1)

            def keys(i, half):
                wait = waiter(dve, i)
                for pr in range(NPR):
                    wait("khi_ready", half * NPR + pr + 1)
                    for par in range(2):
                        last = v.tensor_tensor(
                            klo[0:64, 2 * pr + par, :].rearrange("p (a l) -> p a l", a=2),
                            k_banks[pr][64 * par:64 * par + 64, :, 0:HALF],
                            khi[0:64, 2 * pr + par, :].bitcast(F32).rearrange("p (a l) -> p a l", a=2),
                            ALU.subtract)
                    last.then_inc(sg["klo_ready"], 1)

            def turn(i, last_batch):
                wait = waiter(dve, i)
                for half in range(2):
                    u0 = half * HG
                    for pr in range(NPR):
                        wait("pairs_ready", half * NPR + pr + 1)
                        for par in range(2):
                            last = v.tensor_copy(work[0:64, 2 * pr + par, 0:L], pairs[64 * par:64 * par + 64, pr, 0:L])
                        last.then_inc(sg["work_ready"], 1)
                    relative_rows(dve, wait, half, 1, lambda o, x: v.tensor_copy(o, x), "table_rows_dve")

                    def maxima(u, c, bank):
                        wait("row_scores", u * CH + c + 1)
                        v.tensor_reduce(nmx[:, u % 2, c:c + 1], bank[0:P, :, 0:376], AX.XY, ALU.max,
                                        negate=True).then_inc(sg["max_ready"], 1)

                    def to_row(u, src):
                        wait("max_turned", u + 1)
                        v.tensor_copy(mrow[:, u % 2, :], src).then_inc(sg["max_row"], 1)

                    def values_rest(c):
                        wait("vhi_ready", half * CH + c + 1)
                        v.tensor_tensor(vlo[:, c, :, :],
                                        psS[1][0:P, c % 2, 0:HG * HD].rearrange("p (h d) -> p h d", d=HD),
                                        vhi[:, c, :, 0:64].bitcast(F32), ALU.subtract).then_inc(sg["vlo_ready"], 1)

                    for x in range(AHEAD):
                        if x == AHEAD - 1:
                            for c in range((AHEAD - 1) // 2, CH):
                                values_rest(c)
                        maxima(u0 + x // CH, x % CH, (psS[0], psM)[x % 2])
                        if x == CH:
                            to_row(u0, psO[0:CH, 0, 0:P])
                        if x % 2 and x < AHEAD - 2:
                            values_rest(x // 2)

                    def output(u):
                        wait("values_added", (u + 1) * CH)
                        v.tensor_copy(work[:, u % HG, 0:HP], psO[:, 0, 0:HP]).then_inc(sg["out_dve"], 1)

                    for u in range(u0, u0 + HG):
                        if half == 1 and not last_batch and u == u0 + HG - 2:
                            normalise(i + 1)
                        for c in range(CH):
                            wd = u * CH + c
                            mu, mc = divmod(wd + AHEAD, CH)
                            if mu < u0 + HG:
                                if mc == 0:
                                    dve.wait_ge(s_md[mu % 2], i * (96 * 6) + 96 * (mu // 2))
                                maxima(mu, mc, psM)
                            wait("exp_ready", wd + 1)
                            v.tensor_tensor(Plo[:, wd % 2, :], PT[:, wd % 2, :], Phi[:, wd % 2, :].bitcast(F32),
                                            ALU.subtract).then_inc(sg["exp_rest"], 1)
                            if c == 0 and u > u0:
                                output(u - 1)
                            if mc == CH - 1 and mu < u0 + HG:
                                to_row(mu, psM[0:CH, 0, 384:384 + P])
                    output(u0 + HG - 1)
                    if half == 0:
                        keys(i, 1)
                    elif not last_batch:
                        keys(i + 1, 0)
                    dve.wait_ge(s_dc, (2 * i + half + 1) * 16)
                    v.reciprocal(dcol, dcol).then_inc(sg["inverse_ready"], 1)
                    wait("rel_v_copied", (half + 1) * NV)
                    for m, (gs, n) in enumerate(H_SETS):
                        mm = NV + m
                        wait("rel_product", half * NSET + mm + 1)
                        k = len(gs)
                        dst = grid_columns(pairs, gs, n)
                        v.tensor_tensor(dst, dst, rv_banks[mm % 4][:, 0:k * NPR * n].rearrange(
                            "p (g h n) -> p h n g", h=NPR, n=n), ALU.add).then_inc(sg["rel_h_added"], 1)
                    mm = NSET - 1
                    wait("rel_product", half * NSET + mm + 1)
                    v.tensor_copy(pairs[:, :, 0], rv_banks[mm % 4][:, 0:NPR]).then_inc(sg["rel_h_added"], 1)
                    wait("rel_h_added", (half + 1) * (NHS + 1))
                    dve.wait_ge(s_db, (2 * i + half + 1) * 32)
                    dve.wait_ge(s_bp, i + 1)

                    def divide(c):
                        at = slice(c * P, (c + 1) * P)
                        v.tensor_tensor(pairs[:, :, at], pairs[:, :, at], rdb[:, :, at], ALU.mult
                                        ).then_inc(sg["out_divided"], 1)

                    divide(0)
                    divide(1)
                    for c in range(CH):
                        if c + 2 < CH:
                            divide(c + 2)
                        wait("projected", half * CH + c + 1)
                        if half == 1:
                            wait("h_updated", c + 1)
                        hc = h[:, bass.ds(i * CH + c, 1), :].rearrange("p o e -> p (o e)")
                        v.tensor_tensor(hc, hc, psM[0:P, c % 2, 0:E], ALU.add).then_inc(sg["h_updated"], 1)
                    wait("h_updated", (half + 1) * CH)

            normalise(0)
            keys(0, 0)
            dve.wait_ge(s_og, 1)
            dve.wait_ge(s_oz, 2)
            with dve.Fori(0, B - 1) as i:
                turn(i, False)
            turn(B - 1, True)


def host_inputs(i):
    sel, xy, merge, one9 = moment_constants()
    t = np.ascontiguousarray
    f = {k: np.asarray(v) for k, v in i.items()}
    return {
        "x": f["x"],
        "wt": conv_weights([f[f"L0_tok_w_t{k}"] for k in KS], [f[f"L0_tok_b_t{k}"] for k in KS]),
        "wc": conv_weights([f[f"L0_tok_w_c{k}"] for k in KS], [f[f"L0_tok_b_c{k}"] for k in KS]),
        "Wq0T": t(f["L0_attn_Wq"].T), "Wk0T": t(f["L0_attn_Wk"].T), "Wv0T": t(f["L0_attn_Wv"].T),
        "Wo0T": t(f["L0_attn_Wo"].T),
        "sel": sel, "selxy": xy, "merge": merge, "one9": one9,
        **moe_inputs(f),
        **relative_inputs(f),
    }


def build(nc, A, out):
    ctx = ExitStack()
    with ctx:
        h = ctx.enter_context(nc.sbuf_tensor("h", [P, NT, E], F32))
        ident = ctx.enter_context(nc.sbuf_tensor("ident", [128, 128], F32))
        for run in (lambda keep: token_mixer_and_attention(nc, keep, A, h, ident),
                    lambda keep: moe(nc, keep, A, h, ident, MOE0, None),
                    lambda keep: window_attention(nc, keep, A, h, ident)):
            stage = Stage(nc)
            run(stage)
            stage.close()
        moe(nc, ctx, A, h, ident, MOE1, out)


def kernel(**inputs):
    import concourse.bacc as bacc
    from concourse.bass_utils import run_bass_kernel_spmd

    nc = bacc.Bacc("TRN2", target_bir_lowering=False, num_devices=1)
    arrays, A = {}, {}
    for name, a in host_inputs(inputs).items():
        a = np.ascontiguousarray(a)
        arrays[f"in_{name}"] = a
        A[name] = nc.dram_tensor(f"in_{name}", a.shape, mybir.dt.from_np(a.dtype), kind="ExternalInput").ap()
    out = nc.dram_tensor("out_0", (B, L, E), F32, kind="ExternalOutput").ap()
    build(nc, A, out)
    r = run_bass_kernel_spmd(nc, [arrays], core_ids=[0])
    return r.results[0]["out_0"]
```
